# Optimizing a Trainium2 kernel written in Bass

```python
import numpy as np
import jax
import jax.numpy as jnp

def _softmax(x, axis=-1):
    return jax.nn.softmax(x, axis=axis)

def _gelu(x):
    return jax.nn.gelu(x, approximate=True)

def _silu(x):
    return jax.nn.silu(x)

def _sigmoid(x):
    return jax.nn.sigmoid(x)

def _layernorm(x, axis=-1, eps=1e-05):
    m = jnp.mean(x, axis=axis, keepdims=True)
    v = jnp.var(x, axis=axis, keepdims=True)
    return (x - m) / jnp.sqrt(v + eps)

def _scatter_add(tgt, idx, src, axis=0):
    return tgt.at[idx].add(src)

def _segment_sum(src, seg, n):
    return jax.ops.segment_sum(src, seg, n)
kernel_name = 'mk_xattn_ffn_d1_seqx_r2_07dc6f'

def setup_inputs(seed: int=0):
    np.random.seed(seed)
    _w = jnp.asarray

    def _rec_inputs():
        import jax
        import jax.numpy as jnp
        _rk = jax.random.key(seed)
        x = -0.0005207 + 1.001 * jax.random.normal(jax.random.fold_in(_rk, 1), (4, 2048, 512), jnp.float32)
        _lenS = 2048 - jax.random.randint(jax.random.fold_in(_rk, 7), (4,), 0, max(1, 2048 // 4) + 1, jnp.int32)
        _lenS2 = 154 - jax.random.randint(jax.random.fold_in(_rk, 8), (4,), 0, max(1, 154 // 4) + 1, jnp.int32)
        _ctx_1024P = jax.random.normal(jax.random.fold_in(_rk, 11), (4, 16, 512), jnp.float32)
        _ctx_1024c = jax.random.dirichlet(jax.random.fold_in(_rk, 511), 0.3 * jnp.ones((16,), jnp.float32), (4, 154))
        _ctx_1024t = jnp.einsum('bsk,bkd->bsd', _ctx_1024c, _ctx_1024P)
        _ctx_1024t = _ctx_1024t * jax.lax.rsqrt(jnp.mean(jnp.square(_ctx_1024t)) + 1e-12) * 0.953939
        ctx_1024 = -0.000514642 + 1.00011 * (_ctx_1024t + 0.3 * jax.random.normal(jax.random.fold_in(_rk, 611), (4, 154, 512), jnp.float32))
        _validS = jnp.arange(2048)[None, :] < _lenS[:, None]
        _validS2 = jnp.arange(154)[None, :] < _lenS2[:, None]
        _causal = jnp.tril(jnp.ones((2048, 2048), dtype=bool))
        mask_SxS2_ik0 = jnp.where(jnp.broadcast_to(_validS2[0:1, :], (2048, 154)), 0, 1).astype(jnp.int32)
        return (x, ctx_1024, mask_SxS2_ik0)
    x, ctx_1024, mask_SxS2_ik0 = _rec_inputs()

    def _L0_xattn_setup():
        import jax, jax.numpy as jnp
        import numpy as np
        import math
        B, S, D, H = (1, 1024, 512, 16)
        DK = D // H
        key = jax.random.key(seed)
        ks = jax.random.split(key, 8)
        scale = 1.0 / math.sqrt(D)
        queries = jax.random.normal(ks[0], (B, S, D), dtype=jnp.float32)
        keys_ = jax.random.normal(ks[1], (B, S, D), dtype=jnp.float32)
        values = jax.random.normal(ks[2], (B, S, D), dtype=jnp.float32)
        mask = jnp.tril(jnp.ones((S, S), dtype=jnp.int32))
        Wq = jax.random.normal(ks[3], (H, D, DK), dtype=jnp.float32) * scale
        Wk = jax.random.normal(ks[4], (H, D, DK), dtype=jnp.float32) * scale
        Wv = jax.random.normal(ks[5], (H, D, DK), dtype=jnp.float32) * scale
        Wo = jax.random.normal(ks[6], (D, D), dtype=jnp.float32) * scale
        return {'queries': queries, 'keys': keys_, 'values': values, 'mask': mask, 'Wq': Wq, 'Wk': Wk, 'Wv': Wv, 'Wo': Wo}
    _L0_xattn_all = _L0_xattn_setup()
    _L0_xattn_in = {k: v for k, v in _L0_xattn_all.items() if k in ('Wq', 'Wk', 'Wv', 'Wo')}
    del _L0_xattn_all

    def _L0_ffn_setup():
        import jax, jax.numpy as jnp
        import numpy as np
        B, S, D, H = (8, 512, 512, 2048)
        E, R = (3, 8)
        SCALING = 1.0 / R

        def _mole(x, W, b, A, Bm, Rw):
            gates = jax.nn.softmax(jnp.einsum('bsd,de->bse', x, Rw), axis=-1)
            base = jnp.einsum('bsd,dh->bsh', x, W) + b
            z = jnp.einsum('bsd,edr->ebsr', x, A)
            zg = z * jnp.transpose(gates, (2, 0, 1))[..., None]
            lora = jnp.einsum('ebsr,erh->bsh', zg, Bm)
            return base + SCALING * lora
        key = jax.random.key(seed)
        ks = jax.random.split(key, 12)
        s = lambda k, shape, scale: jax.random.normal(k, shape, dtype=jnp.float32) * scale
        return {'x': s(ks[0], (B, S, D), 1.0), 'W1': s(ks[1], (D, H), D ** (-0.5)), 'b1': jnp.zeros((H,), jnp.float32), 'A1': s(ks[2], (E, D, R), D ** (-0.5)), 'B1': s(ks[3], (E, R, H), 0.0) + s(ks[4], (E, R, H), R ** (-0.5)), 'R1': s(ks[5], (D, E), D ** (-0.5)), 'W2': s(ks[6], (H, D), H ** (-0.5)), 'b2': jnp.zeros((D,), jnp.float32), 'A2': s(ks[7], (E, H, R), H ** (-0.5)), 'B2': s(ks[8], (E, R, D), R ** (-0.5)), 'R2': s(ks[9], (H, E), H ** (-0.5))}
    _L0_ffn_all = _L0_ffn_setup()
    _L0_ffn_in = {k: v for k, v in _L0_ffn_all.items() if k in ('W1', 'b1', 'A1', 'B1', 'R1', 'W2', 'b2', 'A2', 'B2', 'R2')}
    del _L0_ffn_all
    return {'x': x, 'ctx_1024': ctx_1024, 'mask_SxS2_ik0': mask_SxS2_ik0, 'L0_xattn_Wq': _L0_xattn_in['Wq'], 'L0_xattn_Wk': _L0_xattn_in['Wk'], 'L0_xattn_Wv': _L0_xattn_in['Wv'], 'L0_xattn_Wo': _L0_xattn_in['Wo'], 'L0_ffn_W1': _L0_ffn_in['W1'], 'L0_ffn_b1': _L0_ffn_in['b1'], 'L0_ffn_A1': _L0_ffn_in['A1'], 'L0_ffn_B1': _L0_ffn_in['B1'], 'L0_ffn_R1': _L0_ffn_in['R1'], 'L0_ffn_W2': _L0_ffn_in['W2'], 'L0_ffn_b2': _L0_ffn_in['b2'], 'L0_ffn_A2': _L0_ffn_in['A2'], 'L0_ffn_B2': _L0_ffn_in['B2'], 'L0_ffn_R2': _L0_ffn_in['R2']}

def reference(x, ctx_1024, mask_SxS2_ik0, L0_xattn_Wq, L0_xattn_Wk, L0_xattn_Wv, L0_xattn_Wo, L0_ffn_W1, L0_ffn_b1, L0_ffn_A1, L0_ffn_B1, L0_ffn_R1, L0_ffn_W2, L0_ffn_b2, L0_ffn_A2, L0_ffn_B2, L0_ffn_R2):
    import jax
    import jax.numpy as jnp

    def _L0_xattn_ref(queries, keys, values, mask, Wq, Wk, Wv, Wo):
        import jax, jax.numpy as jnp
        import numpy as np
        import math
        B, S, D, H = (1, 1024, 512, 16)
        DK = D // H
        q = jnp.einsum('bsd,hdk->bhsk', queries, Wq)
        k = jnp.einsum('bsd,hdk->bhsk', keys, Wk)
        v = jnp.einsum('bsd,hdk->bhsk', values, Wv)
        attn = jnp.einsum('bhsk,bhtk->bhst', q, k) / jnp.sqrt(jnp.asarray(DK, q.dtype))
        attn = jnp.where(mask == 0, -jnp.inf, attn)
        p = jax.nn.softmax(attn, axis=-1)
        o = jnp.einsum('bhst,bhtk->bhsk', p, v)
        o = o.transpose(0, 2, 1, 3).reshape(queries.shape[0], queries.shape[1], -1)
        out = jnp.einsum('bsd,ed->bse', o, Wo)
        return out

    def _L0_ffn_ref(x, W1, b1, A1, B1, R1, W2, b2, A2, B2, R2):
        import jax, jax.numpy as jnp
        import numpy as np
        B, S, D, H = (8, 512, 512, 2048)
        E, R = (3, 8)
        SCALING = 1.0 / R

        def _mole(x, W, b, A, Bm, Rw):
            gates = jax.nn.softmax(jnp.einsum('bsd,de->bse', x, Rw), axis=-1)
            base = jnp.einsum('bsd,dh->bsh', x, W) + b
            z = jnp.einsum('bsd,edr->ebsr', x, A)
            zg = z * jnp.transpose(gates, (2, 0, 1))[..., None]
            lora = jnp.einsum('ebsr,erh->bsh', zg, Bm)
            return base + SCALING * lora
        h = _mole(x, W1, b1, A1, B1, R1)
        h = jax.nn.relu(h)
        return _mole(h, W2, b2, A2, B2, R2)
    x = x + _L0_xattn_ref(_layernorm(x, axis=-1), ctx_1024, ctx_1024, mask_SxS2_ik0, L0_xattn_Wq, L0_xattn_Wk, L0_xattn_Wv, L0_xattn_Wo)
    x = x + _L0_ffn_ref(_layernorm(x, axis=-1), L0_ffn_W1, L0_ffn_b1, L0_ffn_A1, L0_ffn_B1, L0_ffn_R1, L0_ffn_W2, L0_ffn_b2, L0_ffn_A2, L0_ffn_B2, L0_ffn_R2)
    return x

_drawn_inputs = setup_inputs


def setup_inputs(seed=0):
    import zlib

    import numpy as np

    out = dict(_drawn_inputs(seed))
    spreads = {'L0_ffn_b1': (0.0, 0.1), 'L0_ffn_b2': (0.0, 0.1)}
    factors = {'L0_ffn_R2': 3.304}
    for name, (base, spread) in spreads.items():
        noise = np.random.default_rng([zlib.crc32(name.encode()), seed]).standard_normal(out[name].shape)
        drawn = base * np.exp(spread * noise) if base else spread * noise
        out[name] = jnp.asarray(drawn.astype(out[name].dtype))
    for name, factor in factors.items():
        out[name] = (out[name] * factor).astype(out[name].dtype)
    return out
```

```python
from contextlib import ExitStack

import concourse.bass as bass
from concourse import mybir

F32 = mybir.dt.float32
F32R = mybir.dt.float32r
I32 = mybir.dt.int32
ALU = mybir.AluOpType
ACT = mybir.ActivationFunctionType
AX = mybir.AxisListType

P = 128
B, S, D = 4, 2048, 512
KEYS, H = 154, 16
DK = D // H
F = 2048
E, R = 3, 8
EPS = 1e-5
C = D // P
G = C
HG = P // DK
LEFT = KEYS - P
TILE = 512
SUB = TILE // P
TILES = B * S // TILE
TILES_B = S // TILE
UNITS = G * SUB
PAIR = 2 * KEYS
ER = E * R
FC = F // P
MASKED = -3.0e38
Q = 32
AR = ER + E + 1
ARW = 2 * Q + 2
STACK = 3 * Q
LORA_LOADS = 2 * (E + 1) + 3 * 2 + 2 * 2
HI, LO = 0, 1
PARTS = ((HI, HI), (HI, LO), (LO, HI))


def raw(ap):
    return ap.bitcast(F32)


def held(engine, value):
    return value if isinstance(value, int) else engine.to_reg(value)


class Banks:

    def __init__(self, nc, stack):
        self.bank = [stack.enter_context(nc.psum_tensor(f"bank{i}", [P, 512], F32)) for i in range(8)]

    def __getitem__(self, i):
        return self.bank[i]


def prepare(nc, sem, banks, ident, sum_parts, wq, wo, ar, b2s, ctx, Wq, Wk, Wv, Wo, lora, k_parts, v_parts, b1_parts):
    A1, B1, R1, b1, A2, B2, R2, b2 = lora
    with ExitStack() as stack:
        def sb(name, shape, dt):
            return stack.enter_context(nc.sbuf_tensor(name, shape, dt))

        ctx_main = sb("ctx_main", [P, B, D], F32)
        ctx_left = sb("ctx_left", [B * LEFT, D], F32)
        wq_raw = sb("wq_raw", [P, C, D], F32)
        wk_raw = sb("wk_raw", [P, C, D], F32)
        wv_raw = sb("wv_raw", [P, C, D], F32)
        wo_raw = sb("wo_raw", [P, C, D], F32)
        wk = sb("wk", [P, 2, C, D], F32R)
        wv = sb("wv", [P, 2, C, D], F32R)
        ctxT = sb("ctxT", [P, 2, C, B, KEYS], F32R)
        ctxT_left = sb("ctxT_left", [P, 2, C, B * LEFT], F32R)
        k_out = sb("k_out", [P, 2, G, B, KEYS], F32R)
        v_out = sb("v_out", [P, B, 2, D], F32R)
        vl_out = sb("vl_out", [B * LEFT, 2, D], F32R)
        ar_raw = sb("ar_raw", [P, C + FC, AR], F32)
        b_raw = sb("b_raw", [STACK, F + D], F32)
        b1s = sb("b1s_out", [STACK, F], F32R)

        ident_zero, ident_ready = sem("ident_zero"), sem("ident_ready")
        lora_zero = sem("lora_zero")
        lora_loaded = sem("lora_loaded")
        lora_hi, lora_lo = sem("lora_hi"), sem("lora_lo")
        ctx_loaded = sem("ctx_loaded")
        wk_loaded, wv_loaded = sem("wk_loaded"), sem("wv_loaded")
        wq_loaded, wo_loaded = sem("wq_loaded"), sem("wo_loaded")
        bank_full = sem("prep_bank_full")
        bank_hi = sem("prep_bank_hi")
        bank_lo = sem("prep_bank_lo")
        weight_hi = sem("prep_weight_hi")
        weight_lo = sem("prep_weight_lo")
        left_copied = sem("left_copied")
        parts_stored = sem("parts_stored")

        K0 = 2 * C + 1
        V0 = K0 + G * B // 2
        USES = V0 + B + 1

        def result(u):
            bank = banks[u % 8]
            if u < C:
                return (bank[:, :].rearrange("p (b k) -> p b k", b=B),
                        [ctxT[:, i, u, :, 0:P] for i in (HI, LO)])
            if u == C:
                return (bank[:, 0:C * B * LEFT],
                        [ctxT_left[:, i, :, :].rearrange("p c k -> p (c k)") for i in (HI, LO)])
            if u < K0:
                return bank[:, :], [wo[:, i, u - C - 1, :] for i in (HI, LO)]
            if u < V0:
                g, b = (u - K0) // 2, 2 * ((u - K0) % 2)
                return (bank[:, 0:PAIR],
                        [k_out[:, i, g, b:b + 2, :].rearrange("p b k -> p (b k)") for i in (HI, LO)])
            if u < V0 + B:
                return bank[:, :], [v_out[:, u - V0, i, :] for i in (HI, LO)]
            return bank[0:B * LEFT, :], [vl_out[:, i, :] for i in (HI, LO)]

        weights = [(wk_raw, wk, wk_loaded), (wv_raw, wv, wv_loaded), (wq_raw, wq, wq_loaded)]
        WEIGHT_BEFORE = {C + 1: (0, 1), K0: (2,)}

        with nc.Block() as block:
            @block.sync
            def _(sp):
                sp.dma_start(ctx_main[:, :, :], ctx[:, 0:P, :].rearrange("b k d -> k b d")).then_inc(ctx_loaded, 16)
                for b in range(B):
                    sp.dma_start(ctx_left[b * LEFT:(b + 1) * LEFT, :], ctx[b, P:KEYS, :]).then_inc(ctx_loaded, 16)
                for w, t, s in ((Wk, wk_raw, wk_loaded), (Wq, wq_raw, wq_loaded)):
                    for c in range(C):
                        sp.dma_start(t[:, c, :].rearrange("p (h k) -> p h k", h=H),
                                     w[:, c * P:(c + 1) * P, :].rearrange("h p k -> p h k")).then_inc(s, 16)
                sp.wait_ge(lora_zero, 2)
                for c0, n, A, Rt in ((0, C, A1, R1), (C, FC, A2, R2)):
                    for e in range(E):
                        sp.dma_start(ar_raw[:, c0:c0 + n, e * R:(e + 1) * R],
                                     A[e, :, :].rearrange("(c p) r -> p c r", p=P)).then_inc(lora_loaded, 16)
                    sp.dma_start(ar_raw[:, c0:c0 + n, ER:ER + E],
                                 Rt.rearrange("(c p) e -> p c e", p=P)).then_inc(lora_loaded, 16)
                for q in range(3):
                    for cols, Bt in ((slice(0, F), B1), (slice(F, F + D), B2)):
                        sp.dma_start(b_raw[q * Q:q * Q + ER, cols],
                                     Bt.rearrange("e r h -> (e r) h")).then_inc(lora_loaded, 16)
                for q in range(2):
                    for cols, bt in ((slice(0, F), b1), (slice(F, F + D), b2)):
                        sp.dma_start(b_raw[q * Q + ER:q * Q + ER + 1, cols],
                                     bt.rearrange("(a h) -> a h", a=1)).then_inc(lora_loaded, 16)
                sp.wait_ge(bank_lo, V0)
                for i in (HI, LO):
                    for b in range(B):
                        sp.dma_start(k_parts[i, b, :, :, :], raw(k_out[:, i, :, b, :])).then_inc(parts_stored, 16)
                sp.wait_ge(bank_lo, USES)
                for i in (HI, LO):
                    sp.dma_start(v_parts[i, :, 0:P, :].rearrange("b k d -> k b d"),
                                 raw(v_out[:, :, i, :])).then_inc(parts_stored, 16)
                    for b in range(B):
                        sp.dma_start(v_parts[i, b, P:KEYS, :],
                                     raw(vl_out[b * LEFT:(b + 1) * LEFT, i, :])).then_inc(parts_stored, 16)
                sp.wait_ge(lora_lo, 2)
                sp.dma_start(b1_parts, raw(b1s[:, :])).then_inc(parts_stored, 16)
                sp.wait_ge(parts_stored, 16 * (2 * B + 2 + 2 * B + 1))

            @block.tensor
            def _(pe):
                pe.wait_ge(ident_ready, 1)
                pe.wait_ge(ctx_loaded, 16 * (1 + B))

                def free(u):
                    if u >= 8:
                        pe.wait_ge(bank_lo, u - 7)

                for c in range(C):
                    for b in range(B):
                        last = pe.transpose(banks[c][:, b * P:(b + 1) * P],
                                            ctx_main[:, b, c * P:(c + 1) * P], ident[:, :])
                    last.then_inc(bank_full, 1)
                n = B * LEFT
                for c in range(C):
                    last = pe.transpose(banks[C][:, c * n:(c + 1) * n],
                                        ctx_left[:, c * P:(c + 1) * P], ident[0:n, 0:n])
                last.then_inc(bank_full, 1)
                pe.wait_ge(wo_loaded, 16)
                for c in range(C):
                    u = C + 1 + c
                    free(u)
                    for e in range(C):
                        last = pe.transpose(banks[u % 8][:, e * P:(e + 1) * P],
                                            wo_raw[:, e, c * P:(c + 1) * P], ident[:, :])
                    last.then_inc(bank_full, 1)
                pe.wait_ge(weight_lo, 1)
                pe.wait_ge(left_copied, 1)
                for g in range(G):
                    for b in range(0, B, 2):
                        u = K0 + 2 * g + b // 2
                        free(u)
                        for n, (c, (i, j)) in enumerate((c, ij) for c in range(C) for ij in PARTS):
                            last = pe.matmul(banks[u % 8][:, 0:PAIR], wk[:, i, c, g * P:(g + 1) * P],
                                             ctxT[:, j, c, b:b + 2, :].rearrange("p b k -> p (b k)"),
                                             start=(n == 0), stop=(n == 3 * C - 1))
                        last.then_inc(bank_full, 1)
                pe.wait_ge(weight_lo, 2)
                for b in range(B + 1):
                    u = V0 + b
                    free(u)
                    rows = P if b < B else B * LEFT
                    for n, (c, (i, j)) in enumerate((c, ij) for c in range(C) for ij in PARTS):
                        keys = ctxT[:, i, c, b, 0:P] if b < B else ctxT_left[:, i, c, :]
                        last = pe.matmul(banks[u % 8][0:rows, :], keys, wv[:, j, c, :],
                                         start=(n == 0), stop=(n == 3 * C - 1))
                    last.then_inc(bank_full, 1)

            @block.scalar
            def _(act):
                for c in range(C):
                    act.dma_start(wv_raw[:, c, :].rearrange("p (h k) -> p h k", h=H),
                                  Wv[:, c * P:(c + 1) * P, :].rearrange("h p k -> p h k")).then_inc(wv_loaded, 16)
                act.dma_start(wo_raw[:, :, :], Wo.rearrange("(c p) d -> p c d", p=P)).then_inc(wo_loaded, 16)
                for u in range(USES):
                    for n in WEIGHT_BEFORE.get(u, ()):
                        src, dst, loaded = weights[n]
                        act.wait_ge(loaded, 16 * C)
                        nc.scalar.activation(dst[:, HI, :, :], src[:, :, :], ACT.Copy).then_inc(weight_hi, 1)
                    psum, parts = result(u)
                    act.wait_ge(bank_full, u + 1)
                    nc.scalar.activation(parts[HI], psum, ACT.Copy).then_inc(bank_hi, 1)
                act.wait_ge(lora_loaded, 16 * LORA_LOADS)
                act.wait_ge(lora_zero, 3)
                nc.scalar.activation(ar[:, :, 0:AR], ar_raw[:, :, :], ACT.Copy).then_inc(lora_hi, 1)
                nc.scalar.activation(b1s[:, :], b_raw[:, 0:F], ACT.Copy).then_inc(lora_hi, 1)
                nc.scalar.activation(b2s[:, :], b_raw[:, F:F + D], ACT.Copy).then_inc(lora_hi, 1)

            @block.vector
            def _(dve):
                for u in range(USES):
                    for n in WEIGHT_BEFORE.get(u, ()):
                        src, dst, loaded = weights[n]
                        dve.wait_ge(weight_hi, n + 1)
                        nc.vector.tensor_tensor(dst[:, LO, :, :], src[:, :, :], raw(dst[:, HI, :, :]),
                                                ALU.subtract).then_inc(weight_lo, 1)
                    psum, parts = result(u)
                    dve.wait_ge(bank_hi, u + 1)
                    nc.vector.tensor_tensor(parts[LO], psum, raw(parts[HI]), ALU.subtract).then_inc(bank_lo, 1)
                dve.wait_ge(lora_hi, 3)
                nc.vector.tensor_tensor(ar[:, :, Q:Q + AR], ar_raw[:, :, :], raw(ar[:, :, 0:AR]),
                                        ALU.subtract).then_inc(lora_lo, 1)
                for t, cols in ((b1s, slice(0, F)), (b2s, slice(F, F + D))):
                    nc.vector.tensor_tensor(t[Q:2 * Q, :], b_raw[Q:2 * Q, cols], raw(t[Q:2 * Q, :]),
                                            ALU.subtract).then_inc(lora_lo, 1)

            @block.gpsimd
            def _(pool):
                nc.gpsimd.memset(ident[:, :], 0.0).then_inc(ident_zero, 1)
                nc.gpsimd.memset(sum_parts[:, :], 0.0).then_inc(ident_zero, 1)
                pool.wait_ge(ident_zero, 2)
                nc.gpsimd.affine_select(out=ident[:, :], in_=ident[:, :], compare_op=ALU.not_equal, fill=1.0,
                                        base=0, pattern=[[-1, P]], channel_multiplier=1).then_inc(ident_ready, 1)
                nc.gpsimd.memset(ar_raw[:, :, :], 0.0).then_inc(lora_zero, 1)
                nc.gpsimd.memset(b_raw[:, :], 0.0).then_inc(lora_zero, 1)
                nc.gpsimd.memset(raw(ar[:, :, :]), 0.0).then_inc(lora_zero, 1)
                nc.gpsimd.affine_select(out=sum_parts[:, :], in_=sum_parts[:, :], compare_op=ALU.not_equal,
                                        fill=1.0, base=0, pattern=[[-1, AR]], channel_multiplier=1).then_inc(ident_zero, 1)
                pool.wait_ge(ident_zero, 3)
                nc.gpsimd.affine_select(out=sum_parts[:, :], in_=sum_parts[:, :], compare_op=ALU.not_equal,
                                        fill=1.0, base=-Q, pattern=[[-1, AR]], channel_multiplier=1).then_inc(ident_zero, 1)
                pool.wait_ge(bank_lo, C + 1)
                for i in (HI, LO):
                    for c in range(C):
                        last = nc.gpsimd.tensor_copy(
                            ctxT[:, i, c, :, P:KEYS],
                            raw(ctxT_left[:, i, c, :]).rearrange("p (b k) -> p b k", b=B))
                last.then_inc(left_copied, 1)


STEADY = {
    0: [("PV", -1, 2)],
    2: [("Q", 0, 1)],
    3: [("Q", 0, 2)],
    4: [("PV", -1, 3)],
    5: [("Y", -1, 0)],
    6: [("Y", -1, 1)],
    7: [("Y", -1, 2)],
    8: [("Y", -1, 3), ("PV", 0, 0)],
    9: [("Q", 0, 3)],
    10: [("A", 1, 0), ("A", 1, 1)],
    11: [("A", 1, 2), ("A", 1, 3)],
    12: [("PV", 0, 1)],
    13: [("Q", 1, 0)],
}
LAG = 3
STEPS = UNITS
BEFORE = {0: [("A", 0, c) for c in range(C)] + [("Q", 0, 0)]}
AFTER = {0: [("PV", 0, 2)], LAG - 1: [("PV", 0, 3)] + [("Y", 0, s) for s in range(SUB)]}
PLANS = {
    "before": BEFORE,
    "first": {n: [x for x in l if x[1] >= 0] for n, l in STEADY.items()},
    "steady": STEADY,
    "last": {n: [x for x in l if x[1] <= 0] for n, l in STEADY.items()},
    "after": AFTER,
}


def two_bank_plan():
    turns, used = {}, []
    for kind in ("before", "first", "steady", "last", "after"):
        for n in sorted(PLANS[kind]):
            for stage in PLANS[kind][n]:
                if stage[0] != "PV":
                    turns[kind, stage] = (len(used) % 2, used[-2] if len(used) > 1 else None)
                    used.append(stage)
        if kind in ("first", "steady"):
            used = [(a, dt - 1, i) for a, dt, i in used]
            assert len(used) % 2 == 1
    return turns


def attention(nc, sem, banks, ident, wq, wo, x, mask, k_parts, v_parts, x1):
    with ExitStack() as stack:
        def sb(name, shape, dt):
            return stack.enter_context(nc.sbuf_tensor(name, shape, dt))

        keys = sb("keys", [P, 2, G, HG * KEYS], F32R)
        vals = sb("vals", [P, 2, G, HG, P], F32R)
        vals_left = sb("vals_left", [HG * LEFT, 2, G, P], F32R)
        xn = sb("xn", [P, SUB, D], F32)
        xres = sb("xres", [P, SUB, D], F32)
        xnT = sb("xnT", [P, 2, C, TILE], F32R)
        qT = sb("qT", [P, 2, 2, TILE], F32R)
        mask_in = sb("mask_in", [P, SUB, KEYS], I32)
        bias = sb("bias", [P, SUB, KEYS], F32)
        nan_row = sb("nan_row", [P, SUB], F32)
        any_row = sb("any_row", [P, 3, SUB], F32)
        scores = sb("scores", [P, 2, HG, KEYS], F32)
        probs = sb("probs", [P, 2, HG, KEYS], F32)
        normed = sb("normed", [P, 4, HG * KEYS], F32)
        pT = sb("pT", [P, 2, 2, HG, TILE], F32R)
        pT_left = sb("pT_left", [HG * LEFT, 2, 2, TILE], F32R)
        oT = sb("oT", [P, 2, G, TILE], F32R)
        top = sb("top", [P, 2, HG], F32)
        neg_top = sb("neg_top", [P, 2, HG], F32)
        total = sb("total", [P, 2, HG], F32)
        inv_total = sb("inv_total", [P, 2, HG], F32)
        stats = sb("stats", [P, SUB, 6], F32)
        moments = sb("moments", [P, SUB, 2], F32)
        var_eps = sb("var_eps", [P, SUB], F32)
        minus_half = sb("minus_half", [P, SUB], F32)
        rstd = sb("rstd", [P, SUB], F32)

        score_bank = (banks[0], banks[1])
        p_bank = (banks[2], banks[3])
        left_bank = banks[4]
        pv_bank = banks[5]
        two_banks = (banks[6], banks[7])

        ready = sem("att_ready")
        x_loaded, mask_loaded = sem("x_loaded"), sem("mask_loaded")
        xres_loaded, x1_stored = sem("xres_loaded"), sem("x1_stored")
        keys_loaded, vals_loaded = sem("keys_loaded"), sem("vals_loaded")
        bias_done = sem("bias_done")
        bias_step = sem("bias_step")
        stats_step = sem("stats_step")
        var_done = sem("var_done")
        rstd_done = sem("rstd_done")
        x_normed = sem("x_normed")
        scores_full = sem("scores_full")
        scores_read = sem("scores_read")
        neg_done = sem("neg_done")
        exp_done = sem("exp_done")
        inv_done = sem("inv_done")
        probs_normed = sem("probs_normed")
        p_full, p_hi, p_lo = sem("p_full"), sem("p_hi"), sem("p_lo")
        left_hi, left_lo = sem("left_hi"), sem("left_lo")
        full = {k: sem(f"{k}_full") for k in ("A", "Q", "Y", "PV")}
        hi = {k: sem(f"{k}_hi") for k in ("A", "Q", "PV")}
        lo = {k: sem(f"{k}_lo") for k in ("A", "Q", "PV")}
        y_added = sem("y_added")

        def count(t, i):
            return t * 4 + (i + 1)

        def units(t, n):
            return t * UNITS + (n + 1)

        turns = two_bank_plan()
        x_rows = x.rearrange("b (t s p) d -> (b t) p s d", s=SUB, p=P)
        x1_rows = x1.rearrange("(t s p) d -> t p s d", s=SUB, p=P)
        mask_rows = mask.rearrange("(t s p) k -> t p s k", s=SUB, p=P)

        def walk(kind, t, step):
            plan = PLANS[kind]
            steps = range(STEPS) if kind in ("first", "steady", "last") else range(LAG if kind == "after" else 1)
            for n in steps:
                if kind == "before":
                    late = None
                elif kind == "after":
                    late = (t, UNITS - LAG + n)
                elif n >= LAG:
                    late = (t, n - LAG)
                else:
                    late = None if kind == "first" else (t - 1, UNITS - LAG + n)
                step(n, late, [(a, t + dt, i, (a, dt, i)) for a, dt, i in plan.get(n, ())])

        def all_tiles(engine, tile):
            tile("before", 0)
            tile("first", 0)
            with engine.Fori(1, TILES - 1) as t:
                tile("steady", t)
            tile("last", TILES - 1)
            tile("after", TILES - 1)

        with nc.Block() as block:
            @block.sync
            def _(sp):
                def load_keys(b):
                    for i in (HI, LO):
                        for h in range(HG):
                            rows = slice(h * DK, (h + 1) * DK)
                            sp.dma_start(raw(keys[rows, i, :, h * KEYS:(h + 1) * KEYS]),
                                         k_parts[i, b, rows, :, :]).then_inc(keys_loaded, 16)

                def load_vals(b):
                    for i in (HI, LO):
                        for h in range(HG):
                            cols = slice(h * DK, (h + 1) * DK)
                            v = v_parts[i, b, :, :].rearrange("k (g c) -> k g c", g=G)
                            sp.dma_start(raw(vals[:, i, :, h, cols]), v[0:P, :, cols]).then_inc(vals_loaded, 16)
                            sp.dma_start(raw(vals_left[h * LEFT:(h + 1) * LEFT, i, :, cols]),
                                         v[P:KEYS, :, cols]).then_inc(vals_loaded, 16)

                def traffic(t, tb, ahead=True, new_batch=None):
                    sp.dma_start(xres[:, :, :], x_rows[t]).then_inc(xres_loaded, 16)
                    if ahead:
                        value = held(sp, count(t + 1, C - 1))
                        sp.wait_ge(ready, 3)
                        sp.wait_ge(full["A"], value)
                        sp.dma_start(xn[:, :, :], x_rows[t + 2]).then_inc(x_loaded, 16)
                    if new_batch is not None:
                        value = held(sp, units(t, UNITS - 1))
                        sp.wait_ge(ready, 3)
                        sp.wait_ge(scores_full, value)
                        load_keys(new_batch)
                    if ahead:
                        value = held(sp, t + 2)
                        sp.wait_ge(ready, 3)
                        sp.wait_ge(bias_done, value)
                        sp.dma_start(mask_in[:, :, :], mask_rows[(tb + 2) % TILES_B]).then_inc(mask_loaded, 16)
                    if new_batch is not None:
                        value = held(sp, count(t, G - 1))
                        sp.wait_ge(ready, 3)
                        sp.wait_ge(full["PV"], value)
                        load_vals(new_batch)
                    for s in range(SUB):
                        value = held(sp, count(t, s))
                        sp.wait_ge(ready, 3)
                        sp.wait_ge(y_added, value)
                        sp.dma_start(x1_rows[t, :, s, :], xres[:, s, :]).then_inc(x1_stored, 16)
                    value = held(sp, (t + 1) * 16 * SUB)
                    sp.wait_ge(ready, 3)
                    sp.wait_ge(x1_stored, value)

                sp.dma_start(xn[:, :, :], x_rows[0]).then_inc(x_loaded, 16)
                sp.dma_start(mask_in[:, :, :], mask_rows[0]).then_inc(mask_loaded, 16)
                sp.wait_ge(ready, 3)
                load_keys(0)
                load_vals(0)
                sp.wait_ge(full["A"], count(0, C - 1))
                sp.dma_start(xn[:, :, :], x_rows[1]).then_inc(x_loaded, 16)
                sp.wait_ge(bias_done, 1)
                sp.dma_start(mask_in[:, :, :], mask_rows[1]).then_inc(mask_loaded, 16)
                with sp.Fori(0, B - 1) as b:
                    for tb in range(TILES_B):
                        traffic(b * TILES_B + tb, tb, new_batch=b + 1 if tb == TILES_B - 1 else None)
                for tb in range(TILES_B):
                    traffic((B - 1) * TILES_B + tb, tb, ahead=tb < TILES_B - 2)

            @block.tensor
            def _(pe):
                def score(t, n):
                    g, s = n // SUB, n % SUB
                    if s == 0:
                        pe.wait_ge(lo["Q"], count(t, g))
                    if n == 0:
                        pe.wait_ge(keys_loaded, (t // TILES_B + 1) * (16 * 2 * HG))
                    if not (isinstance(t, int) and t == 0 and n == 0):
                        pe.wait_ge(scores_read, units(t, n - 1))
                    for m, (i, j) in enumerate(PARTS):
                        for p in range(2):
                            last = pe.matmul(score_bank[p][:, 0:PAIR], qT[:, g % 2, i, s * P:(s + 1) * P],
                                             keys[:, j, g, p * PAIR:(p + 1) * PAIR],
                                             start=(m == 0), stop=(m == 2))
                    last.then_inc(scores_full, 1)

                def transpose_probs(t, n):
                    g, s = n // SUB, n % SUB
                    early = isinstance(t, int) and t == 0
                    pe.wait_ge(probs_normed, units(t, n))
                    if not (early and n < 2):
                        pe.wait_ge(p_lo, units(t, n - 2))
                    if s == 0 and not (early and g == 0):
                        pe.wait_ge(left_lo, count(t, g - 1))
                    for h in range(HG):
                        pe.transpose(p_bank[n % 2][:, h * P:(h + 1) * P],
                                     normed[:, n % 4, h * P:(h + 1) * P], ident[:, :])
                    pe.transpose(left_bank[0:HG * LEFT, s * P:(s + 1) * P],
                                 normed[:, n % 4, HG * P:HG * KEYS], ident[:, :]).then_inc(p_full, 1)

                def stage(kind, what, t, i, rel):
                    if what == "PV":
                        pe.wait_ge(p_lo, units(t, SUB * i + SUB - 1))
                        pe.wait_ge(left_lo, count(t, i))
                        if i == 0:
                            pe.wait_ge(vals_loaded, (t // TILES_B + 1) * (16 * 4 * HG))
                        if not (isinstance(t, int) and t == 0 and i == 0):
                            pe.wait_ge(lo["PV"], count(t, i - 1))
                        m = 0
                        for h in range(HG + 1):
                            for a, b in PARTS:
                                v = vals[:, a, i, h, :] if h < HG else vals_left[:, a, i, :]
                                p = pT[:, i % 2, b, h, :] if h < HG else pT_left[:, i % 2, b, :]
                                last = pe.matmul(pv_bank[:, :], v, p, start=(m == 0), stop=(m == 3 * HG + 2))
                                m += 1
                        last.then_inc(full["PV"], 1)
                        return
                    turn, before = turns[kind, rel]
                    bank = two_banks[turn]
                    if before is not None:
                        then = t - rel[1] + before[1]
                        pe.wait_ge(y_added if before[0] == "Y" else lo[before[0]], count(then, before[2]))
                    if what == "A":
                        if i == 0:
                            pe.wait_ge(x_normed, t + 1)
                        for s in range(SUB):
                            last = pe.transpose(bank[:, s * P:(s + 1) * P], xn[:, s, i * P:(i + 1) * P], ident[:, :])
                    elif what == "Q":
                        if i == 0:
                            pe.wait_ge(lo["A"], count(t, C - 1))
                        for m, (c, (a, b)) in enumerate((c, ab) for c in range(C) for ab in PARTS):
                            last = pe.matmul(bank[:, :], wq[:, a, c, i * P:(i + 1) * P], xnT[:, b, c, :],
                                             start=(m == 0), stop=(m == 3 * C - 1))
                    else:
                        if i == 0:
                            pe.wait_ge(lo["PV"], count(t, G - 1))
                        for m, (c, (a, b)) in enumerate((c, ab) for c in range(C) for ab in PARTS):
                            last = pe.matmul(bank[:, :], oT[:, a, c, i * P:(i + 1) * P], wo[:, b, c, :],
                                             start=(m == 0), stop=(m == 3 * C - 1))
                    last.then_inc(full[what], 1)

                def tile(kind, t):
                    def step(n, late, stages):
                        if kind in ("first", "steady", "last"):
                            score(t, n)
                        if late is not None:
                            transpose_probs(*late)
                        for s in stages:
                            stage(kind, *s)
                    walk(kind, t, step)

                all_tiles(pe, tile)

            @block.scalar
            def _(act):
                def split(psum, part, wait, value, done):
                    act.wait_ge(wait, value)
                    nc.scalar.activation(part, psum, ACT.Copy).then_inc(done, 1)

                def exps(t, n):
                    act.wait_ge(neg_done, units(t, n))
                    if not (isinstance(t, int) and t == 0 and n < 2):
                        act.wait_ge(probs_normed, units(t, n - 2))
                    for h in range(HG):
                        last = nc.scalar.activation(probs[:, n % 2, h, :], scores[:, n % 2, h, :], ACT.Exp,
                                                    bias=neg_top[:, n % 2, h:h + 1],
                                                    accum_out=total[:, n % 2, h:h + 1])
                    last.then_inc(exp_done, 1)

                def probs_hi(t, n):
                    g, s = n // SUB, n % SUB
                    if s == 0 and not (isinstance(t, int) and t == 0 and g < 2):
                        act.wait_ge(full["PV"], count(t, g - 2))
                    split(p_bank[n % 2][:, :].rearrange("p (h k) -> p h k", h=HG),
                          pT[:, g % 2, HI, :, s * P:(s + 1) * P], p_full, units(t, n), p_hi)
                    if s == SUB - 1:
                        split(left_bank[0:HG * LEFT, :], pT_left[:, g % 2, HI, :], p_full, units(t, n), left_hi)

                def tile(kind, t):
                    def step(n, late, stages):
                        if late is not None:
                            probs_hi(*late)
                        if kind in ("first", "steady", "last"):
                            exps(t, n)
                        for what, tt, i, rel in stages:
                            if what == "PV":
                                split(pv_bank[:, :], oT[:, HI, i, :], full[what], count(tt, i), hi[what])
                            elif what == "A":
                                split(two_banks[turns[kind, rel][0]][:, :], xnT[:, HI, i, :],
                                      full[what], count(tt, i), hi[what])
                            elif what == "Q":
                                split(two_banks[turns[kind, rel][0]][:, :], qT[:, i % 2, HI, :],
                                      full[what], count(tt, i), hi[what])
                    walk(kind, t, step)

                all_tiles(act, tile)

            @block.vector
            def _(dve):
                zeros = nc.vector.memset(raw(keys[:, :, :, :]), 0.0)
                zeros.then_inc(ready, 1)
                nc.vector.memset(minus_half[:, :], -0.5).then_inc(ready, 1)

                def split(psum, parts, wait, value, done):
                    dve.wait_ge(wait, value)
                    nc.vector.tensor_tensor(parts[LO], psum, raw(parts[HI]), ALU.subtract).then_inc(done, 1)

                def mask_bias(t):
                    dve.wait_ge(mask_loaded, (t + 1) * 16)
                    nc.vector.tensor_scalar(bias[:, :, :], mask_in[:, :, :], 0, MASKED,
                                            ALU.is_equal, ALU.mult).then_inc(bias_done, 1)
                    dve.wait_ge(bias_done, t + 1)
                    nc.vector.tensor_reduce(any_row[:, 0, :], bias[:, :, :], AX.X, ALU.max).then_inc(bias_step, 1)
                    dve.wait_ge(bias_step, t * 4 + 1)
                    nc.vector.tensor_scalar(any_row[:, 1, :], any_row[:, 0, :], 0.0, None,
                                            ALU.is_equal).then_inc(bias_step, 1)
                    dve.wait_ge(bias_step, t * 4 + 2)
                    nc.vector.reciprocal(any_row[:, 2, :], any_row[:, 1, :]).then_inc(bias_step, 1)
                    dve.wait_ge(bias_step, t * 4 + 3)
                    nc.vector.tensor_scalar(nan_row[:, :], any_row[:, 2, :], 0.0, None,
                                            ALU.mult).then_inc(bias_step, 1)

                def read_scores(t, n):
                    unit, old = held(dve, units(t, n)), held(dve, units(t, n - 2))
                    tile_bias = held(dve, t * 4 + 4) if n == 0 else None
                    dve.wait_ge(ready, 3)
                    dve.wait_ge(scores_full, unit)
                    if not (isinstance(t, int) and t == 0 and n < 2):
                        dve.wait_ge(exp_done, old)
                    if n == 0:
                        dve.wait_ge(bias_step, tile_bias)
                    for h in range(HG):
                        cols = slice((h % 2) * KEYS, (h % 2 + 1) * KEYS)
                        last = nc.vector.tensor_tensor_reduce(
                            out=scores[:, n % 2, h, :], in0=score_bank[h // 2][:, cols],
                            in1=bias[:, n % SUB, :], scale=DK ** -0.5, scalar=MASKED,
                            op0=ALU.add, op1=ALU.max, accum_out=top[:, n % 2, h:h + 1])
                    last.then_inc(scores_read, 1)
                    dve.wait_ge(scores_read, units(t, n))
                    nc.vector.tensor_scalar(neg_top[:, n % 2, :], top[:, n % 2, :], -1.0,
                                            nan_row[:, n % SUB:n % SUB + 1], ALU.mult, ALU.add).then_inc(neg_done, 1)

                def invert(t, n):
                    dve.wait_ge(exp_done, units(t, n))
                    nc.vector.reciprocal(inv_total[:, n % 2, :], total[:, n % 2, :]).then_inc(inv_done, 1)

                def probs_lo(t, n):
                    g, s = n // SUB, n % SUB
                    split(p_bank[n % 2][:, :].rearrange("p (h k) -> p h k", h=HG),
                          [pT[:, g % 2, i, :, s * P:(s + 1) * P] for i in (HI, LO)], p_hi, units(t, n), p_lo)
                    if s == SUB - 1:
                        split(left_bank[0:HG * LEFT, :], [pT_left[:, g % 2, i, :] for i in (HI, LO)],
                              left_hi, count(t, g), left_lo)

                def row_stats(t, s):
                    if s == 0:
                        dve.wait_ge(x_loaded, (t + 1) * 16)
                    nc.vector.bn_stats(stats[:, s, :], xn[:, s, :]).then_inc(stats_step, 1)
                    first_step = held(dve, t * (2 * SUB) + (2 * s + 1))
                    dve.wait_ge(ready, 3)
                    dve.wait_ge(stats_step, first_step)
                    nc.vector.bn_aggr(moments[:, s, :], stats[:, s, :]).then_inc(stats_step, 1)
                    if s == SUB - 1:
                        dve.wait_ge(stats_step, (t + 1) * (2 * SUB))
                        nc.vector.tensor_scalar(var_eps[:, :], moments[:, :, 1], EPS, None,
                                                ALU.add).then_inc(var_done, 1)

                def tile(kind, t):
                    def step(n, late, stages):
                        if kind in ("first", "steady", "last"):
                            if n == 0:
                                mask_bias(t)
                            read_scores(t, n)
                            if n > 0:
                                invert(t, n - 1)
                        elif kind == "before":
                            for s in range(SUB):
                                row_stats(0, s)
                        if late is not None:
                            probs_lo(*late)
                        if kind in ("first", "steady") and 4 <= n < 4 + SUB:
                            row_stats(t + 1, n - 4)
                        for what, tt, i, rel in stages:
                            if what == "Y":
                                if i == 0:
                                    dve.wait_ge(xres_loaded, (tt + 1) * 16)
                                dve.wait_ge(full[what], count(tt, i))
                                nc.vector.tensor_tensor(xres[:, i, :], two_banks[turns[kind, rel][0]][:, :],
                                                        xres[:, i, :], ALU.add).then_inc(y_added, 1)
                            elif what == "PV":
                                split(pv_bank[:, :], [oT[:, j, i, :] for j in (HI, LO)],
                                      hi[what], count(tt, i), lo[what])
                            elif what == "A":
                                split(two_banks[turns[kind, rel][0]][:, :], [xnT[:, j, i, :] for j in (HI, LO)],
                                      hi[what], count(tt, i), lo[what])
                            else:
                                split(two_banks[turns[kind, rel][0]][:, :], [qT[:, i % 2, j, :] for j in (HI, LO)],
                                      hi[what], count(tt, i), lo[what])
                        if kind in ("first", "steady", "last") and n == UNITS - 1:
                            invert(t, n)
                    walk(kind, t, step)

                all_tiles(dve, tile)

            @block.gpsimd
            def _(pool):
                nc.gpsimd.memset(raw(vals[:, :, :, :, :]), 0.0)
                nc.gpsimd.memset(raw(vals_left[:, :, :, :]), 0.0).then_inc(ready, 1)

                def layer_norm(t):
                    pool.wait_ge(var_done, t + 1)
                    nc.gpsimd.tensor_tensor(rstd[:, :], var_eps[:, :], minus_half[:, :], ALU.pow).then_inc(rstd_done, 1)
                    tile_rstd = held(pool, t + 1)
                    pool.wait_ge(ready, 3)
                    pool.wait_ge(rstd_done, tile_rstd)
                    for s in range(SUB):
                        last = nc.gpsimd.tensor_scalar(xn[:, s, :], xn[:, s, :], moments[:, s, 0:1],
                                                       rstd[:, s:s + 1], ALU.subtract, ALU.mult)
                    last.then_inc(x_normed, 1)

                def normalise(t, n):
                    pool.wait_ge(inv_done, units(t, n))
                    if not (isinstance(t, int) and t == 0 and n < 4):
                        pool.wait_ge(p_full, units(t, n - 4))
                    inv = inv_total[:, n % 2, :].unsqueeze(2)
                    for a, b, c in ((0, P, 0), (P, KEYS, HG * P)):
                        last = nc.gpsimd.tensor_tensor(
                            normed[:, n % 4, c:c + HG * (b - a)].rearrange("p (h k) -> p h k", h=HG),
                            probs[:, n % 2, :, a:b], inv.to_broadcast([P, HG, b - a]), ALU.mult)
                    last.then_inc(probs_normed, 1)

                def tile(kind, t):
                    if kind == "before":
                        layer_norm(0)
                    if kind not in ("first", "steady", "last"):
                        return
                    for n in range(UNITS):
                        normalise(t, n)
                        if kind != "last" and n == 7:
                            layer_norm(t + 1)

                all_tiles(pool, tile)


def ffn(nc, sem, banks, ident, sum_parts, ar, b2s, W1, W2, b1_parts, x1, out):
    with ExitStack() as stack:
        def sb(name, shape, dt):
            return stack.enter_context(nc.sbuf_tensor(name, shape, dt))

        w1 = sb("w1", [P, 2, C, F], F32R)
        w2 = sb("w2", [P, 2, FC, D], F32R)
        b1s = sb("b1s", [STACK, F], F32R)
        xin = sb("xin", [P, 2, D], F32)
        xres = sb("ffn_xres", [P, SUB, D], F32)
        xnT = sb("ffn_xnT", [P, 2, 2, C, TILE], F32R)
        hid = sb("hid", [P, 2, 2, TILE], F32R)
        z_rows = sb("z_rows", [2 * Q, TILE], F32)
        z = sb("z", [P, SUB, AR], F32)
        g_top = sb("g_top", [P, SUB], F32)
        g_exp = sb("g_exp", [P, SUB, E], F32)
        g_sum = sb("g_sum", [P, SUB], F32)
        g_inv = sb("g_inv", [P, SUB], F32)
        gate = sb("gate", [P, SUB, E], F32)
        zg = sb("zg", [P, SUB, ER], F32)
        zs = sb("zs", [P, SUB, 3, Q], F32R)
        zsT = sb("zsT", [STACK, 2, TILE], F32R)
        stats = sb("ffn_stats", [P, 2, 6], F32)
        moments = sb("ffn_moments", [P, 2, 2], F32)
        var_eps = sb("ffn_var_eps", [P, 2], F32)
        minus_half = sb("ffn_minus_half", [P, 1], F32)
        rstd = sb("ffn_rstd", [P, 2], F32)

        f1_bank = (banks[0], banks[1])
        y_bank = (banks[2], banks[3], banks[4], banks[5])
        z_bank = (banks[6], banks[7])

        ready = sem("ffn_ready")
        w_loaded = [sem(f"w_loaded{i}") for i in range(SUB)]
        w_hi, w_lo = sem("w_hi"), sem("w_lo")
        b1s_loaded = sem("b1s_loaded")
        xin_loaded = [sem(f"xin_loaded{i}") for i in range(2)]
        stats_step = sem("ffn_stats_step")
        rstd_done = sem("ffn_rstd_done")
        x_normed = sem("ffn_x_normed")
        x_full, x_hi, x_lo = sem("x_full"), sem("x_hi"), sem("x_lo")
        f1_full, h_hi, h_lo = sem("f1_full"), sem("h_hi"), sem("h_lo")
        z_full, z_copied = sem("z_full"), sem("z_copied")
        z_turned = sem("z_turned")
        gate_step = sem("gate_step")
        gate_exp = sem("gate_exp")
        zs_full, zs_copied = sem("zs_full"), sem("zs_copied")
        y_full, y_added = sem("y_full"), sem("ffn_y_added")
        xres_loaded, stored = sem("ffn_xres_loaded"), sem("stored")
        GATE_STEPS = 9

        def blocks(t, j):
            return t * FC + (j + 1)

        def subs(t, s):
            return t * SUB + (s + 1)

        def nth(kind, layer, t):
            if layer == 0:
                return 1 if kind == "before" else t * 2
            return t * 2 + (2 if kind == "last" else 3)

        def first_nth(t):
            return 1 if isinstance(t, int) and t == 0 else t * 2

        w1_rows = W1.rearrange("(c p) f -> p c f", p=P)
        x1_rows = x1.rearrange("(t s p) d -> t p s d", s=SUB, p=P)
        out_rows = out.rearrange("b (t s p) d -> (b t) p s d", s=SUB, p=P)

        STATS = {0: 0, 2: 1, 4: 2, 6: 3}
        TURN = {1: 0, 3: 1, 5: 2, 7: 3}
        Z1, TURN_Z1, TURN_ZS1 = 9, 10, 14

        def all_tiles(engine, before, tile):
            before()
            tile("first", 0, 0)
            with engine.Fori(0, (TILES - 2) // 2) as pair:
                tile("steady", pair * 2 + 1, 1)
                tile("steady", pair * 2 + 2, 0)
            tile("last", TILES - 1, 1)

        with nc.Block() as block:
            @block.sync
            def _(sp):
                def load_x(t, s):
                    if not (isinstance(t, int) and t == 0 and s < 2):
                        value = held(sp, subs(t, s - 2))
                        sp.wait_ge(ready, 3)
                        sp.wait_ge(x_full, value)
                    sp.dma_start(xin[:, s % 2, :], x1_rows[t, :, s, :]).then_inc(xin_loaded[s % 2], 16)

                def tile(kind, t, parity):
                    if kind != "first":
                        for s in range(SUB):
                            value = held(sp, subs(t - 1, s))
                            sp.wait_ge(ready, 3)
                            sp.wait_ge(y_added, value)
                            sp.dma_start(out_rows[t - 1, :, s, :], xres[:, s, :]).then_inc(stored, 16)
                        value = held(sp, t * (16 * SUB))
                        sp.wait_ge(ready, 3)
                        sp.wait_ge(stored, value)
                    sp.dma_start(xres[:, :, :], x1_rows[t]).then_inc(xres_loaded, 16)
                    if kind == "steady":
                        for s in range(SUB):
                            load_x(t + 1, s)

                NEXT_X = {3: 0, 4: 1, 6: 2, 8: 3}

                def before():
                    load_x(0, 0)
                    load_x(0, 1)
                    for j in range(FC):
                        if j == 2:
                            load_x(0, 2)
                            load_x(0, 3)
                        if j in NEXT_X:
                            load_x(1, NEXT_X[j])
                        if j >= 2:
                            sp.wait_ge(w_lo, 2 * (j - 2) + 1)
                        sp.dma_start(xres[:, j % 2, :].rearrange("p (c f) -> p c f", c=C),
                                     w1_rows[:, :, j * P:(j + 1) * P]).then_inc(w_loaded[j % 2], 16)
                        if j >= 2:
                            sp.wait_ge(w_lo, 2 * (j - 2) + 2)
                        sp.dma_start(xres[:, 2 + j % 2, :], W2[j * P:(j + 1) * P, :]).then_inc(w_loaded[2 + j % 2], 16)
                        if j == 0:
                            sp.dma_start(raw(b1s[:, :]), b1_parts).then_inc(b1s_loaded, 16)
                    sp.wait_ge(w_lo, 2 * FC)

                all_tiles(sp, before, tile)
                for s in range(SUB):
                    sp.wait_ge(y_added, subs(TILES - 1, s))
                    sp.dma_start(out_rows[TILES - 1, :, s, :], xres[:, s, :]).then_inc(stored, 16)
                sp.wait_ge(stored, TILES * 16 * SUB)

            @block.tensor
            def _(pe):
                def turn_x(t, s):
                    early = isinstance(t, int) and t == 0
                    pe.wait_ge(x_normed, subs(t, s))
                    if s > 0:
                        pe.wait_ge(x_lo, subs(t, s - 1))
                    elif not early:
                        pe.wait_ge(zs_copied, first_nth(t - 1))
                    for c in range(C):
                        last = pe.transpose(z_bank[0][:, c * P:(c + 1) * P],
                                            xin[:, s % 2, c * P:(c + 1) * P], ident[:, :])
                    last.then_inc(x_full, 1)

                def z1(t, parity):
                    pe.wait_ge(x_lo, subs(t, SUB - 1))
                    for n, (c, i) in enumerate((c, i) for c in range(C) for i in (HI, LO)):
                        last = pe.matmul(z_bank[0][0:ARW, :], ar[:, c, :], xnT[:, parity, i, c, :],
                                         start=(n == 0), stop=(n == 2 * C - 1))
                    last.then_inc(z_full, 1)

                def turn_z(layer, n):
                    pe.wait_ge(z_copied, n)
                    for s in range(SUB):
                        last = pe.matmul(z_bank[layer][:, s * AR:(s + 1) * AR], z_rows[:, s * P:(s + 1) * P],
                                         sum_parts[:, :], start=True, stop=True)
                    last.then_inc(z_turned, 1)

                def turn_zs(layer, n):
                    pe.wait_ge(gate_step, n * GATE_STEPS)
                    for s in range(SUB):
                        last = pe.transpose(z_bank[layer][0:STACK, s * P:(s + 1) * P],
                                            raw(zs[:, s, :, :]).rearrange("p a b -> p (a b)"), ident[:, :])
                    last.then_inc(zs_full, 1)

                def f1(t, j, parity, part=slice(0, 3 * C + 1)):
                    if part.start == 0:
                        if isinstance(t, int) and t == 0:
                            pe.wait_ge(w_lo, 2 * j + 1)
                        if not (isinstance(t, int) and t == 0 and j < 2):
                            pe.wait_ge(h_lo, blocks(t, j - 2))
                    terms = [(c, a, b) for c in range(C) for a, b in PARTS] + [None]
                    for n in range(part.start, part.stop):
                        if terms[n] is None:
                            if j == 0:
                                pe.wait_ge(zs_copied, first_nth(t))
                                pe.wait_ge(b1s_loaded, 16)
                            last = pe.matmul(f1_bank[j % 2][:, :], b1s[:, j * P:(j + 1) * P], zsT[:, 0, :],
                                             start=False, stop=True)
                            last.then_inc(f1_full, 1)
                        else:
                            c, a, b = terms[n]
                            pe.matmul(f1_bank[j % 2][:, :], w1[:, a, c, j * P:(j + 1) * P],
                                      xnT[:, parity, b, c, :], start=(n == 0), stop=False)

                def f2(t, j):
                    early = isinstance(t, int) and t == 0
                    pe.wait_ge(h_lo, blocks(t, j))
                    if early:
                        pe.wait_ge(w_lo, 2 * j + 2)
                    for s in range(SUB):
                        if j == 0 and not early:
                            pe.wait_ge(y_added, subs(t - 1, s))
                        for a, b in PARTS:
                            pe.matmul(y_bank[s][:, :], hid[:, j % 2, a, s * P:(s + 1) * P], w2[:, b, j, :],
                                      start=(j == 0 and (a, b) == PARTS[0]), stop=False)
                    for i in (HI, LO):
                        last = pe.matmul(z_bank[1][0:ARW, :], ar[:, C + j, :], hid[:, j % 2, i, :],
                                         start=(j == 0 and i == HI), stop=(j == FC - 1 and i == LO))
                    if j == FC - 1:
                        last.then_inc(z_full, 1)

                def lora2(n):
                    pe.wait_ge(zs_copied, n)
                    for s in range(SUB):
                        pe.matmul(y_bank[s][:, :], zsT[:, 1, s * P:(s + 1) * P], b2s[:, :],
                                  start=False, stop=True).then_inc(y_full, 1)

                def before():
                    for s in range(SUB):
                        turn_x(0, s)
                    z1(0, 0)
                    turn_z(0, 1)
                    turn_zs(0, 1)
                    f1(0, 0, 0)
                    f1(0, 1, 0)

                def tile(kind, t, parity):
                    more = kind != "last"
                    for j in range(FC):
                        f2(t, j)
                        if j + 2 < FC:
                            f1(t, j + 2, parity)
                        if more:
                            if j in TURN:
                                turn_x(t + 1, TURN[j])
                            elif j == Z1:
                                z1(t + 1, 1 - parity)
                            elif j == TURN_Z1:
                                turn_z(0, nth(kind, 0, t + 1))
                            elif j == TURN_ZS1:
                                turn_zs(0, nth(kind, 0, t + 1))
                    n = nth(kind, 1, t)
                    if more:
                        f1(t + 1, 0, 1 - parity, slice(0, 4))
                    turn_z(1, n)
                    if more:
                        f1(t + 1, 0, 1 - parity, slice(4, 3 * C + 1))
                        f1(t + 1, 1, 1 - parity, slice(0, 9))
                    turn_zs(1, n)
                    if more:
                        f1(t + 1, 1, 1 - parity, slice(9, 3 * C + 1))
                    lora2(n)

                all_tiles(pe, before, tile)

            @block.scalar
            def _(act):
                def split_w(j):
                    act.wait_ge(w_loaded[j % 2], 16 * (j // 2 + 1))
                    nc.scalar.activation(w1[:, HI, :, j * P:(j + 1) * P],
                                         xres[:, j % 2, :].rearrange("p (c f) -> p c f", c=C),
                                         ACT.Copy).then_inc(w_hi, 1)
                    act.wait_ge(w_loaded[2 + j % 2], 16 * (j // 2 + 1))
                    nc.scalar.activation(w2[:, HI, j, :], xres[:, 2 + j % 2, :], ACT.Copy).then_inc(w_hi, 1)

                def x_part(t, s, parity):
                    act.wait_ge(x_full, subs(t, s))
                    nc.scalar.activation(xnT[:, parity, HI, :, s * P:(s + 1) * P],
                                         z_bank[0][:, :].rearrange("p (c k) -> p c k", c=C), ACT.Copy).then_inc(x_hi, 1)

                def copy_z(layer, n):
                    act.wait_ge(z_full, n)
                    nc.scalar.activation(z_rows[:, :], z_bank[layer][0:2 * Q, :], ACT.Copy).then_inc(z_copied, 1)

                def exps(n):
                    act.wait_ge(gate_step, n * GATE_STEPS - (GATE_STEPS - 3))
                    nc.scalar.activation(g_exp[:, :, :], g_exp[:, :, :], ACT.Exp).then_inc(gate_exp, 1)

                def copy_zs(layer, n):
                    act.wait_ge(zs_full, n)
                    nc.scalar.activation(zsT[:, layer, :], z_bank[layer][0:STACK, :], ACT.Copy).then_inc(zs_copied, 1)

                def relu(t, j):
                    act.wait_ge(f1_full, blocks(t, j))
                    nc.scalar.activation(hid[:, j % 2, HI, :], f1_bank[j % 2][:, :], ACT.Relu).then_inc(h_hi, 1)

                def before():
                    split_w(0)
                    for s in range(SUB):
                        x_part(0, s, 0)
                    copy_z(0, 1)
                    exps(1)
                    split_w(1)
                    copy_zs(0, 1)
                    relu(0, 0)
                    relu(0, 1)

                def tile(kind, t, parity):
                    more = kind != "last"
                    for j in range(FC):
                        if kind == "first" and j + 2 < FC:
                            split_w(j + 2)
                        if j + 2 < FC:
                            relu(t, j + 2)
                        if more:
                            if j in TURN:
                                x_part(t + 1, TURN[j], 1 - parity)
                            elif j == Z1:
                                copy_z(0, nth(kind, 0, t + 1))
                            elif j == TURN_Z1:
                                exps(nth(kind, 0, t + 1))
                            elif j == TURN_ZS1:
                                copy_zs(0, nth(kind, 0, t + 1))
                    n = nth(kind, 1, t)
                    copy_z(1, n)
                    exps(n)
                    if more:
                        relu(t + 1, 0)
                    copy_zs(1, n)
                    if more:
                        relu(t + 1, 1)

                all_tiles(act, before, tile)

            @block.vector
            def _(dve):
                nc.vector.memset(minus_half[:, :], -0.5).then_inc(ready, 1)
                nc.vector.memset(raw(zs[:, :, :, :]), 0.0).then_inc(ready, 1)
                dve.wait_ge(ready, 2)
                nc.vector.memset(raw(zs[:, :, 0:2, ER:ER + 1]), 1.0).then_inc(ready, 1)

                def split_w(j):
                    dve.wait_ge(w_hi, 2 * j + 1)
                    nc.vector.tensor_tensor(w1[:, LO, :, j * P:(j + 1) * P],
                                            xres[:, j % 2, :].rearrange("p (c f) -> p c f", c=C),
                                            raw(w1[:, HI, :, j * P:(j + 1) * P]), ALU.subtract).then_inc(w_lo, 1)
                    dve.wait_ge(w_hi, 2 * j + 2)
                    nc.vector.tensor_tensor(w2[:, LO, j, :], xres[:, 2 + j % 2, :], raw(w2[:, HI, j, :]),
                                            ALU.subtract).then_inc(w_lo, 1)

                def row_stats(t, s):
                    v = t * (3 * SUB) + 3 * s
                    dve.wait_ge(xin_loaded[s % 2], t * (8 * SUB) + 16 * (s // 2 + 1))
                    nc.vector.bn_stats(stats[:, s % 2, :], xin[:, s % 2, :]).then_inc(stats_step, 1)
                    first_step = held(dve, v + 1)
                    dve.wait_ge(ready, 3)
                    dve.wait_ge(stats_step, first_step)
                    nc.vector.bn_aggr(moments[:, s % 2, :], stats[:, s % 2, :]).then_inc(stats_step, 1)
                    dve.wait_ge(stats_step, v + 2)
                    nc.vector.tensor_scalar(var_eps[:, s % 2:s % 2 + 1], moments[:, s % 2, 1:2], EPS, None,
                                            ALU.add).then_inc(stats_step, 1)

                def x_part(t, s, parity):
                    dve.wait_ge(x_hi, subs(t, s))
                    nc.vector.tensor_tensor(xnT[:, parity, LO, :, s * P:(s + 1) * P],
                                            z_bank[0][:, :].rearrange("p (c k) -> p c k", c=C),
                                            raw(xnT[:, parity, HI, :, s * P:(s + 1) * P]),
                                            ALU.subtract).then_inc(x_lo, 1)

                def relu(t, j):
                    dve.wait_ge(h_hi, blocks(t, j))
                    nc.vector.scalar_tensor_tensor(out=hid[:, j % 2, LO, :], in0=f1_bank[j % 2][:, :], scalar=0.0,
                                                   in1=raw(hid[:, j % 2, HI, :]), op0=ALU.max,
                                                   op1=ALU.subtract).then_inc(h_lo, 1)

                def route(layer, n):
                    done = n * GATE_STEPS - GATE_STEPS

                    def after(k):
                        dve.wait_ge(gate_step, done + k)

                    logits = z[:, :, ER:ER + E]
                    dve.wait_ge(z_turned, n)
                    nc.vector.tensor_copy(z[:, :, :].rearrange("p s c -> p (s c)"),
                                          z_bank[layer][:, 0:SUB * AR]).then_inc(gate_step, 1)
                    after(1)
                    nc.vector.tensor_reduce(g_top[:, :], logits, AX.X, ALU.max).then_inc(gate_step, 1)
                    after(2)
                    nc.vector.tensor_tensor(g_exp[:, :, :], logits, g_top[:, :].unsqueeze(2).to_broadcast([P, SUB, E]),
                                            ALU.subtract).then_inc(gate_step, 1)
                    dve.wait_ge(gate_exp, n)
                    nc.vector.tensor_reduce(g_sum[:, :], g_exp[:, :, :], AX.X, ALU.add).then_inc(gate_step, 1)
                    after(4)
                    nc.vector.reciprocal(g_inv[:, :], g_sum[:, :]).then_inc(gate_step, 1)
                    after(5)
                    nc.vector.scalar_tensor_tensor(out=gate[:, :, :], in0=g_exp[:, :, :], scalar=1.0 / R,
                                                   in1=g_inv[:, :].unsqueeze(2).to_broadcast([P, SUB, E]),
                                                   op0=ALU.mult, op1=ALU.mult).then_inc(gate_step, 1)
                    after(6)
                    nc.vector.tensor_tensor(zg[:, :, :].rearrange("p s (e r) -> p s e r", e=E),
                                            z[:, :, 0:ER].rearrange("p s (e r) -> p s e r", e=E),
                                            gate[:, :, :].unsqueeze(3).to_broadcast([P, SUB, E, R]),
                                            ALU.mult).then_inc(gate_step, 1)
                    after(7)
                    nc.vector.tensor_copy(zs[:, :, 0:2, 0:ER],
                                          zg[:, :, :].unsqueeze(2).to_broadcast([P, SUB, 2, ER])).then_inc(gate_step, 1)
                    after(8)
                    nc.vector.tensor_tensor(zs[:, :, 2, 0:ER], zg[:, :, :], raw(zs[:, :, 0, 0:ER]),
                                            ALU.subtract).then_inc(gate_step, 1)

                def before():
                    row_stats(0, 0)
                    row_stats(0, 1)
                    split_w(0)
                    for s in range(SUB):
                        x_part(0, s, 0)
                        if s + 2 < SUB:
                            row_stats(0, s + 2)
                    route(0, 1)
                    split_w(1)
                    relu(0, 0)
                    relu(0, 1)

                def tile(kind, t, parity):
                    more = kind != "last"
                    for j in range(FC):
                        if kind == "first" and j + 2 < FC:
                            split_w(j + 2)
                        if more and j in STATS:
                            row_stats(t + 1, STATS[j])
                        if j + 2 < FC:
                            relu(t, j + 2)
                        if more:
                            if j in TURN:
                                x_part(t + 1, TURN[j], 1 - parity)
                            elif j == TURN_Z1:
                                route(0, nth(kind, 0, t + 1))
                    n = nth(kind, 1, t)
                    route(1, n)
                    if more:
                        relu(t + 1, 0)
                        relu(t + 1, 1)
                    dve.wait_ge(xres_loaded, (t + 1) * 16)
                    for s in range(SUB):
                        dve.wait_ge(y_full, subs(t, s))
                        nc.vector.tensor_tensor(xres[:, s, :], y_bank[s][:, :], xres[:, s, :],
                                                ALU.add).then_inc(y_added, 1)

                all_tiles(dve, before, tile)

            @block.gpsimd
            def _(pool):
                def layer_norm(t, s):
                    pool.wait_ge(stats_step, t * (3 * SUB) + (3 * s + 3))
                    nc.gpsimd.tensor_tensor(rstd[:, s % 2:s % 2 + 1], var_eps[:, s % 2:s % 2 + 1],
                                            minus_half[:, :], ALU.pow).then_inc(rstd_done, 1)
                    own_rstd = held(pool, subs(t, s))
                    pool.wait_ge(ready, 3)
                    pool.wait_ge(rstd_done, own_rstd)
                    nc.gpsimd.tensor_scalar(xin[:, s % 2, :], xin[:, s % 2, :], moments[:, s % 2, 0:1],
                                            rstd[:, s % 2:s % 2 + 1], ALU.subtract, ALU.mult).then_inc(x_normed, 1)

                for s in range(SUB):
                    layer_norm(0, s)
                with pool.Fori(1, TILES) as t:
                    for s in range(SUB):
                        layer_norm(t, s)


def build(nc, x, ctx, mask, Wq, Wk, Wv, Wo, W1, b1, A1, B1, R1, W2, b2, A2, B2, R2, out):
    k_parts = nc.dram_tensor("k_parts", (2, B, P, G, KEYS), F32, kind="Internal").ap()
    v_parts = nc.dram_tensor("v_parts", (2, B, KEYS, D), F32, kind="Internal").ap()
    b1_parts = nc.dram_tensor("b1_parts", (STACK, F), F32, kind="Internal").ap()
    x1 = nc.dram_tensor("x1", (B * S, D), F32, kind="Internal").ap()
    with ExitStack() as stack:
        def sem(name):
            return stack.enter_context(nc.semaphore(name))

        banks = Banks(nc, stack)
        ident = stack.enter_context(nc.sbuf_tensor("ident", [P, P], F32))
        sum_parts = stack.enter_context(nc.sbuf_tensor("sum_parts", [2 * Q, AR], F32))
        ar = stack.enter_context(nc.sbuf_tensor("ar", [P, C + FC, ARW], F32R))
        b2s = stack.enter_context(nc.sbuf_tensor("b2s", [STACK, D], F32R))
        with ExitStack() as first_two:
            wq = first_two.enter_context(nc.sbuf_tensor("wq", [P, 2, C, D], F32R))
            wo = first_two.enter_context(nc.sbuf_tensor("wo", [P, 2, C, D], F32R))
            prepare(nc, sem, banks, ident, sum_parts, wq, wo, ar, b2s, ctx, Wq, Wk, Wv, Wo,
                    (A1, B1, R1, b1, A2, B2, R2, b2), k_parts, v_parts, b1_parts)
            attention(nc, sem, banks, ident, wq, wo, x, mask, k_parts, v_parts, x1)
        ffn(nc, sem, banks, ident, sum_parts, ar, b2s, W1, W2, b1_parts, x1, out)


_INS = ["x", "ctx_1024", "mask_SxS2_ik0", "L0_xattn_Wq", "L0_xattn_Wk", "L0_xattn_Wv", "L0_xattn_Wo",
        "L0_ffn_W1", "L0_ffn_b1", "L0_ffn_A1", "L0_ffn_B1", "L0_ffn_R1",
        "L0_ffn_W2", "L0_ffn_b2", "L0_ffn_A2", "L0_ffn_B2", "L0_ffn_R2"]


def kernel(**inputs):
    import numpy as _np
    import concourse.bacc as _bacc
    from concourse import mybir as _mybir
    from concourse.bass_utils import run_bass_kernel_spmd as _run

    nc = _bacc.Bacc("TRN2", target_bir_lowering=False, num_devices=1)
    arrays, args = {}, []
    for name in _INS:
        a = _np.ascontiguousarray(inputs[name])
        arrays[f"in_{name}_dram"] = a
        args.append(nc.dram_tensor(f"in_{name}_dram", a.shape, _mybir.dt.from_np(a.dtype), kind="ExternalInput").ap())
    args.append(nc.dram_tensor("out_0_dram", (B, S, D), F32, kind="ExternalOutput").ap())
    build(nc, *args)
    r = _run(nc, [arrays], core_ids=[0])
    return r.results[0]["out_0_dram"]
```

```python
from contextlib import ExitStack

import concourse.bass as bass
from concourse import mybir

F32 = mybir.dt.float32
F32R = mybir.dt.float32r
I32 = mybir.dt.int32
ALU = mybir.AluOpType
ACT = mybir.ActivationFunctionType
AX = mybir.AxisListType

P = 128
B, S, D = 4, 2048, 512
KEYS, H = 154, 16
DK = D // H
F = 2048
E, R = 3, 8
EPS = 1e-5
C = D // P
G = C
HG = P // DK
HALF = P // 2
LEFT = KEYS - P
TILE = 512
SUB = TILE // P
TILES = B * S // TILE
TILES_B = S // TILE
UNITS = G * SUB
PAIR = 2 * KEYS
ER = E * R
FC = F // P
MASKED = -3.0e38
Q = 32
AR = ER + E + 1
ARW = 2 * Q + 2
STACK = 3 * Q
LORA_LOADS = 2 * (E + 1) + 3 * 2 + 2 * 2
HI, LO = 0, 1
PARTS = ((HI, HI), (HI, LO), (LO, HI))


def raw(ap):
    return ap.bitcast(F32)


def held(engine, value):
    return value if isinstance(value, int) else engine.to_reg(value)


class Banks:

    def __init__(self, nc, stack):
        self.bank = [stack.enter_context(nc.psum_tensor(f"bank{i}", [P, 512], F32)) for i in range(8)]

    def __getitem__(self, i):
        return self.bank[i]


def prepare(nc, sem, banks, ident, sum_parts, wq, wo, ar, b2s, ctx, Wq, Wk, Wv, Wo, lora, k_parts, v_parts, b1_parts):
    A1, B1, R1, b1, A2, B2, R2, b2 = lora
    with ExitStack() as stack:
        def sb(name, shape, dt):
            return stack.enter_context(nc.sbuf_tensor(name, shape, dt))

        ctx_main = sb("ctx_main", [P, B, D], F32)
        ctx_left = sb("ctx_left", [B * LEFT, D], F32)
        wq_raw = sb("wq_raw", [P, C, D], F32)
        wk_raw = sb("wk_raw", [P, C, D], F32)
        wv_raw = sb("wv_raw", [P, C, D], F32)
        wo_raw = sb("wo_raw", [P, C, D], F32)
        wk = sb("wk", [P, 2, C, D], F32R)
        wv = sb("wv", [P, 2, C, D], F32R)
        ctxT = sb("ctxT", [P, 2, C, B, KEYS], F32R)
        ctxT_left = sb("ctxT_left", [P, 2, C, B * LEFT], F32R)
        k_out = sb("k_out", [P, 2, G, B, KEYS], F32R)
        v_out = sb("v_out", [P, B, 2, D], F32R)
        vl_out = sb("vl_out", [B * LEFT, 2, D], F32R)
        ar_raw = sb("ar_raw", [P, C + FC, AR], F32)
        b_raw = sb("b_raw", [STACK, F + D], F32)
        b1s = sb("b1s_out", [STACK, F], F32R)

        ident_zero, ident_ready = sem("ident_zero"), sem("ident_ready")
        lora_zero = sem("lora_zero")
        lora_loaded = sem("lora_loaded")
        lora_hi, lora_lo = sem("lora_hi"), sem("lora_lo")
        ctx_loaded = sem("ctx_loaded")
        wk_loaded, wv_loaded = sem("wk_loaded"), sem("wv_loaded")
        wq_loaded, wo_loaded = sem("wq_loaded"), sem("wo_loaded")
        bank_full = sem("prep_bank_full")
        bank_hi = sem("prep_bank_hi")
        bank_lo = sem("prep_bank_lo")
        weight_hi = sem("prep_weight_hi")
        weight_lo = sem("prep_weight_lo")
        left_copied = sem("left_copied")
        parts_stored = sem("parts_stored")

        K0 = 2 * C + 1
        V0 = K0 + G * B // 2
        USES = V0 + B + 1

        def result(u):
            bank = banks[u % 8]
            if u < C:
                return (bank[:, :].rearrange("p (b k) -> p b k", b=B),
                        [ctxT[:, i, u, :, 0:P] for i in (HI, LO)])
            if u == C:
                return (bank[:, 0:C * B * LEFT],
                        [ctxT_left[:, i, :, :].rearrange("p c k -> p (c k)") for i in (HI, LO)])
            if u < K0:
                return bank[:, :], [wo[:, i, u - C - 1, :] for i in (HI, LO)]
            if u < V0:
                g, b = (u - K0) // 2, 2 * ((u - K0) % 2)
                return (bank[:, 0:PAIR],
                        [k_out[:, i, g, b:b + 2, :].rearrange("p b k -> p (b k)") for i in (HI, LO)])
            if u < V0 + B:
                return bank[:, :], [v_out[:, u - V0, i, :] for i in (HI, LO)]
            return bank[0:B * LEFT, :], [vl_out[:, i, :] for i in (HI, LO)]

        weights = [(wk_raw, wk, wk_loaded), (wv_raw, wv, wv_loaded), (wq_raw, wq, wq_loaded)]
        WEIGHT_BEFORE = {C + 1: (0, 1), K0: (2,)}

        with nc.Block() as block:
            @block.sync
            def _(sp):
                sp.dma_start(ctx_main[:, :, :], ctx[:, 0:P, :].rearrange("b k d -> k b d")).then_inc(ctx_loaded, 16)
                for b in range(B):
                    sp.dma_start(ctx_left[b * LEFT:(b + 1) * LEFT, :], ctx[b, P:KEYS, :]).then_inc(ctx_loaded, 16)
                for w, t, s in ((Wk, wk_raw, wk_loaded), (Wq, wq_raw, wq_loaded)):
                    for c in range(C):
                        sp.dma_start(t[:, c, :].rearrange("p (h k) -> p h k", h=H),
                                     w[:, c * P:(c + 1) * P, :].rearrange("h p k -> p h k")).then_inc(s, 16)
                sp.wait_ge(lora_zero, 2)
                for c0, n, A, Rt in ((0, C, A1, R1), (C, FC, A2, R2)):
                    for e in range(E):
                        sp.dma_start(ar_raw[:, c0:c0 + n, e * R:(e + 1) * R],
                                     A[e, :, :].rearrange("(c p) r -> p c r", p=P)).then_inc(lora_loaded, 16)
                    sp.dma_start(ar_raw[:, c0:c0 + n, ER:ER + E],
                                 Rt.rearrange("(c p) e -> p c e", p=P)).then_inc(lora_loaded, 16)
                for q in range(3):
                    for cols, Bt in ((slice(0, F), B1), (slice(F, F + D), B2)):
                        sp.dma_start(b_raw[q * Q:q * Q + ER, cols],
                                     Bt.rearrange("e r h -> (e r) h")).then_inc(lora_loaded, 16)
                for q in range(2):
                    for cols, bt in ((slice(0, F), b1), (slice(F, F + D), b2)):
                        sp.dma_start(b_raw[q * Q + ER:q * Q + ER + 1, cols],
                                     bt.rearrange("(a h) -> a h", a=1)).then_inc(lora_loaded, 16)
                sp.wait_ge(bank_lo, V0)
                for i in (HI, LO):
                    for b in range(B):
                        sp.dma_start(k_parts[i, b, :, :, :], raw(k_out[:, i, :, b, :])).then_inc(parts_stored, 16)
                sp.wait_ge(bank_lo, USES)
                for i in (HI, LO):
                    sp.dma_start(v_parts[i, :, 0:P, :].rearrange("b k d -> k b d"),
                                 raw(v_out[:, :, i, :])).then_inc(parts_stored, 16)
                    for b in range(B):
                        sp.dma_start(v_parts[i, b, P:KEYS, :],
                                     raw(vl_out[b * LEFT:(b + 1) * LEFT, i, :])).then_inc(parts_stored, 16)
                sp.wait_ge(lora_lo, 2)
                sp.dma_start(b1_parts, raw(b1s[:, :])).then_inc(parts_stored, 16)
                sp.wait_ge(parts_stored, 16 * (2 * B + 2 + 2 * B + 1))

            @block.tensor
            def _(pe):
                pe.wait_ge(ident_ready, 1)
                pe.wait_ge(ctx_loaded, 16 * (1 + B))

                def free(u):
                    if u >= 8:
                        pe.wait_ge(bank_lo, u - 7)

                for c in range(C):
                    for b in range(B):
                        last = pe.transpose(banks[c][:, b * P:(b + 1) * P],
                                            ctx_main[:, b, c * P:(c + 1) * P], ident[:, :])
                    last.then_inc(bank_full, 1)
                n = B * LEFT
                for c in range(C):
                    last = pe.transpose(banks[C][:, c * n:(c + 1) * n],
                                        ctx_left[:, c * P:(c + 1) * P], ident[0:n, 0:n])
                last.then_inc(bank_full, 1)
                pe.wait_ge(wo_loaded, 16)
                for c in range(C):
                    u = C + 1 + c
                    free(u)
                    for e in range(C):
                        last = pe.transpose(banks[u % 8][:, e * P:(e + 1) * P],
                                            wo_raw[:, e, c * P:(c + 1) * P], ident[:, :])
                    last.then_inc(bank_full, 1)
                pe.wait_ge(weight_lo, 1)
                pe.wait_ge(left_copied, 1)
                for g in range(G):
                    for b in range(0, B, 2):
                        u = K0 + 2 * g + b // 2
                        free(u)
                        for n, (c, (i, j)) in enumerate((c, ij) for c in range(C) for ij in PARTS):
                            last = pe.matmul(banks[u % 8][:, 0:PAIR], wk[:, i, c, g * P:(g + 1) * P],
                                             ctxT[:, j, c, b:b + 2, :].rearrange("p b k -> p (b k)"),
                                             start=(n == 0), stop=(n == 3 * C - 1))
                        last.then_inc(bank_full, 1)
                pe.wait_ge(weight_lo, 2)
                for b in range(B + 1):
                    u = V0 + b
                    free(u)
                    rows = P if b < B else B * LEFT
                    for n, (c, (i, j)) in enumerate((c, ij) for c in range(C) for ij in PARTS):
                        keys = ctxT[:, i, c, b, 0:P] if b < B else ctxT_left[:, i, c, :]
                        last = pe.matmul(banks[u % 8][0:rows, :], keys, wv[:, j, c, :],
                                         start=(n == 0), stop=(n == 3 * C - 1))
                    last.then_inc(bank_full, 1)

            @block.scalar
            def _(act):
                for c in range(C):
                    act.dma_start(wv_raw[:, c, :].rearrange("p (h k) -> p h k", h=H),
                                  Wv[:, c * P:(c + 1) * P, :].rearrange("h p k -> p h k")).then_inc(wv_loaded, 16)
                act.dma_start(wo_raw[:, :, :], Wo.rearrange("(c p) d -> p c d", p=P)).then_inc(wo_loaded, 16)
                for u in range(USES):
                    for n in WEIGHT_BEFORE.get(u, ()):
                        src, dst, loaded = weights[n]
                        act.wait_ge(loaded, 16 * C)
                        nc.scalar.activation(dst[:, HI, :, :], src[:, :, :], ACT.Copy).then_inc(weight_hi, 1)
                    psum, parts = result(u)
                    act.wait_ge(bank_full, u + 1)
                    nc.scalar.activation(parts[HI], psum, ACT.Copy).then_inc(bank_hi, 1)
                act.wait_ge(lora_loaded, 16 * LORA_LOADS)
                act.wait_ge(lora_zero, 3)
                nc.scalar.activation(ar[:, :, 0:AR], ar_raw[:, :, :], ACT.Copy).then_inc(lora_hi, 1)
                nc.scalar.activation(b1s[:, :], b_raw[:, 0:F], ACT.Copy).then_inc(lora_hi, 1)
                nc.scalar.activation(b2s[:, :], b_raw[:, F:F + D], ACT.Copy).then_inc(lora_hi, 1)

            @block.vector
            def _(dve):
                for u in range(USES):
                    for n in WEIGHT_BEFORE.get(u, ()):
                        src, dst, loaded = weights[n]
                        dve.wait_ge(weight_hi, n + 1)
                        nc.vector.tensor_tensor(dst[:, LO, :, :], src[:, :, :], raw(dst[:, HI, :, :]),
                                                ALU.subtract).then_inc(weight_lo, 1)
                    psum, parts = result(u)
                    dve.wait_ge(bank_hi, u + 1)
                    nc.vector.tensor_tensor(parts[LO], psum, raw(parts[HI]), ALU.subtract).then_inc(bank_lo, 1)
                dve.wait_ge(lora_hi, 3)
                nc.vector.tensor_tensor(ar[:, :, Q:Q + AR], ar_raw[:, :, :], raw(ar[:, :, 0:AR]),
                                        ALU.subtract).then_inc(lora_lo, 1)
                for t, cols in ((b1s, slice(0, F)), (b2s, slice(F, F + D))):
                    nc.vector.tensor_tensor(t[Q:2 * Q, :], b_raw[Q:2 * Q, cols], raw(t[Q:2 * Q, :]),
                                            ALU.subtract).then_inc(lora_lo, 1)

            @block.gpsimd
            def _(pool):
                nc.gpsimd.memset(ident[:, :], 0.0).then_inc(ident_zero, 1)
                nc.gpsimd.memset(sum_parts[:, :], 0.0).then_inc(ident_zero, 1)
                pool.wait_ge(ident_zero, 2)
                nc.gpsimd.affine_select(out=ident[:, :], in_=ident[:, :], compare_op=ALU.not_equal, fill=1.0,
                                        base=0, pattern=[[-1, P]], channel_multiplier=1).then_inc(ident_ready, 1)
                nc.gpsimd.memset(ar_raw[:, :, :], 0.0).then_inc(lora_zero, 1)
                nc.gpsimd.memset(b_raw[:, :], 0.0).then_inc(lora_zero, 1)
                nc.gpsimd.memset(raw(ar[:, :, :]), 0.0).then_inc(lora_zero, 1)
                nc.gpsimd.affine_select(out=sum_parts[:, :], in_=sum_parts[:, :], compare_op=ALU.not_equal,
                                        fill=1.0, base=0, pattern=[[-1, AR]], channel_multiplier=1).then_inc(ident_zero, 1)
                pool.wait_ge(ident_zero, 3)
                nc.gpsimd.affine_select(out=sum_parts[:, :], in_=sum_parts[:, :], compare_op=ALU.not_equal,
                                        fill=1.0, base=-Q, pattern=[[-1, AR]], channel_multiplier=1).then_inc(ident_zero, 1)
                pool.wait_ge(bank_lo, C + 1)
                for i in (HI, LO):
                    for c in range(C):
                        last = nc.gpsimd.tensor_copy(
                            ctxT[:, i, c, :, P:KEYS],
                            raw(ctxT_left[:, i, c, :]).rearrange("p (b k) -> p b k", b=B))
                last.then_inc(left_copied, 1)


ALL = 2
STEADY = {
    0: [("PV", -1, 2, 1)],
    1: [("Q", 0, 1, ALL)],
    2: [("Q", 0, 2, 0)],
    3: [("PV", -1, 3, ALL)],
    4: [("Q", 0, 2, 1)],
    5: [("Y", -1, 0, ALL)],
    6: [("Y", -1, 1, ALL)],
    7: [("Y", -1, 2, ALL)],
    8: [("Q", 0, 3, ALL)],
    9: [("Y", -1, 3, ALL)],
    10: [("PV", 0, 0, ALL)],
    11: [("A", 1, 0, ALL), ("A", 1, 1, ALL)],
    12: [("PV", 0, 1, 0), ("A", 1, 2, ALL), ("A", 1, 3, ALL)],
    13: [("PV", 0, 1, 1)],
    14: [("Q", 1, 0, ALL)],
    15: [("PV", 0, 2, 0)],
}
LAG = 3
STEPS = UNITS
BEFORE = {0: [("A", 0, c, ALL) for c in range(C)] + [("Q", 0, 0, ALL)]}
AFTER = {0: [("PV", 0, 2, 1)], LAG - 1: [("PV", 0, 3, ALL)] + [("Y", 0, s, ALL) for s in range(SUB)]}
PLANS = {
    "before": BEFORE,
    "first": {n: [x for x in l if x[1] >= 0] for n, l in STEADY.items()},
    "steady": STEADY,
    "last": {n: [x for x in l if x[1] <= 0] for n, l in STEADY.items()},
    "after": AFTER,
}


def two_bank_plan():
    turns, used = {}, []
    for kind in ("before", "first", "steady", "last", "after"):
        for n in sorted(PLANS[kind]):
            for what, dt, i, part in PLANS[kind][n]:
                if what != "PV" and part != 1:
                    turns[kind, (what, dt, i)] = (len(used) % 2, used[-2] if len(used) > 1 else None)
                    used.append((what, dt, i))
        if kind in ("first", "steady"):
            used = [(a, dt - 1, i) for a, dt, i in used]
            assert len(used) % 2 == 1
    return turns


def attention(nc, sem, banks, ident, wq, wo, x, mask, k_parts, v_parts, x1):
    with ExitStack() as stack:
        def sb(name, shape, dt):
            return stack.enter_context(nc.sbuf_tensor(name, shape, dt))

        keys = sb("keys", [P, 2, G, 2, PAIR], F32R)
        vals = sb("vals", [P, 2, G, HG, P], F32R)
        vals_left = sb("vals_left", [HG * LEFT, 2, G, P], F32R)
        xn = sb("xn", [P, SUB, D], F32)
        xres = sb("xres", [P, SUB, D], F32)
        xnT = sb("xnT", [P, 2, C, TILE], F32R)
        qT = sb("qT", [P, 2, 2, TILE], F32R)
        mask_in = sb("mask_in", [P, SUB, KEYS], I32)
        bias = sb("bias", [P, SUB, KEYS + 1], F32)
        next_bias = sb("next_bias", [P, SUB, KEYS + 1], F32)
        any_row = sb("any_row", [P, 3, SUB], F32)
        scores = sb("scores", [P, 2, HG, KEYS], F32)
        probs = sb("probs", [P, 2, HG, KEYS], F32)
        normed = sb("normed", [P, 4, HG * KEYS], F32)
        pT = sb("pT", [P, 2, 2, HG, TILE], F32R)
        pT_left = sb("pT_left", [HG * LEFT, 2, 2, TILE], F32R)
        oT = sb("oT", [P, 2, G, TILE], F32R)
        top = sb("top", [P, 2, HG], F32)
        neg_top = sb("neg_top", [P, 2, HG], F32)
        total = sb("total", [P, 2, HG], F32)
        inv_total = sb("inv_total", [P, 2, HG], F32)
        stats = sb("stats", [P, SUB, 6], F32)
        moments = sb("moments", [P, SUB, 2], F32)
        var_eps = sb("var_eps", [P, SUB], F32)
        minus_half = sb("minus_half", [P, SUB], F32)
        rstd = sb("rstd", [P, SUB], F32)

        score_bank = (banks[0], banks[1])
        p_bank = (banks[2], banks[3])
        left_bank = banks[4]
        pv_bank = banks[5]
        two_banks = (banks[6], banks[7])

        ready = sem("att_ready")
        x_loaded, mask_loaded = sem("x_loaded"), sem("mask_loaded")
        xres_loaded, x1_stored = sem("xres_loaded"), sem("x1_stored")
        keys_loaded = [sem(f"keys_loaded{g}") for g in range(G)]
        vals_loaded = sem("vals_loaded")
        bias_done = sem("bias_done")
        bias_step = sem("bias_step")
        bias_moved = sem("bias_moved")
        stats_step = sem("stats_step")
        var_done = sem("var_done")
        rstd_done = sem("rstd_done")
        x_normed = sem("x_normed")
        scores_full = sem("scores_full")
        scores_read = sem("scores_read")
        neg_done = sem("neg_done")
        exp_done = sem("exp_done")
        inv_done = sem("inv_done")
        probs_normed = sem("probs_normed")
        p_full, p_hi, p_lo = sem("p_full"), sem("p_hi"), sem("p_lo")
        left_hi, left_lo = sem("left_hi"), sem("left_lo")
        full = {k: sem(f"{k}_full") for k in ("A", "Q", "Y", "PV")}
        hi = {k: sem(f"{k}_hi") for k in ("A", "Q", "PV")}
        lo = {k: sem(f"{k}_lo") for k in ("A", "Q", "PV")}
        y_added = sem("y_added")

        def count(t, i):
            return t * 4 + (i + 1)

        def units(t, n):
            return t * UNITS + (n + 1)

        turns = two_bank_plan()
        x_rows = x.rearrange("b (t s p) d -> (b t) p s d", s=SUB, p=P)
        x1_rows = x1.rearrange("(t s p) d -> t p s d", s=SUB, p=P)
        mask_rows = mask.rearrange("(t s p) k -> t p s k", s=SUB, p=P)

        def walk(kind, t, step, engine_is_pe=False):
            plan = PLANS[kind]
            steps = range({"before": 1, "after": LAG + 1}.get(kind, STEPS))
            for n in steps:
                found = plan.get(n, ()) if kind == "before" or engine_is_pe else plan.get(n - 1, ())
                if kind == "before" or (kind == "after" and n == LAG):
                    late = None
                elif kind == "after":
                    late = (t, UNITS - LAG + n)
                elif n >= LAG:
                    late = (t, n - LAG)
                else:
                    late = None if kind == "first" else (t - 1, UNITS - LAG + n)
                step(n, late, [(a, t + dt, i, part, (a, dt, i)) for a, dt, i, part in found
                               if part != 0 or engine_is_pe])

        def all_tiles(engine, tile):
            tile("before", 0)
            tile("first", 0)
            with engine.Fori(1, TILES - 1) as t:
                tile("steady", t)
            tile("last", TILES - 1)
            tile("after", TILES - 1)

        with nc.Block() as block:
            @block.sync
            def _(sp):
                def load_keys(b, g):
                    for r in range(HG):
                        for p in range(2):
                            h = 2 * p + r % 2
                            sp.dma_start(
                                raw(keys[r * DK:(r + 1) * DK, :, g, p, (r % 2) * KEYS:(r % 2 + 1) * KEYS]),
                                k_parts[:, b, h * DK:(h + 1) * DK, g, :].rearrange("i k n -> k i n"),
                            ).then_inc(keys_loaded[g], 16)

                def load_vals(b):
                    for i in (HI, LO):
                        for h in range(HG):
                            cols = slice(h * DK, (h + 1) * DK)
                            v = v_parts[i, b, :, :].rearrange("k (g c) -> k g c", g=G)
                            sp.dma_start(raw(vals[:, i, :, h, cols]), v[0:P, :, cols]).then_inc(vals_loaded, 16)
                            sp.dma_start(raw(vals_left[h * LEFT:(h + 1) * LEFT, i, :, cols]),
                                         v[P:KEYS, :, cols]).then_inc(vals_loaded, 16)

                def traffic(t, tb, ahead=True, new_batch=None):
                    def next_keys(groups):
                        for g in groups:
                            value = held(sp, units(t, SUB * g + SUB - 1))
                            sp.wait_ge(ready, 3)
                            sp.wait_ge(scores_full, value)
                            load_keys(new_batch, g)

                    sp.dma_start(xres[:, :, :], x_rows[t]).then_inc(xres_loaded, 16)
                    if new_batch is not None:
                        next_keys(range(G - 1))
                    if ahead:
                        value = held(sp, count(t + 1, C - 1))
                        sp.wait_ge(ready, 3)
                        sp.wait_ge(full["A"], value)
                        sp.dma_start(xn[:, :, :], x_rows[t + 2]).then_inc(x_loaded, 16)
                    if new_batch is not None:
                        next_keys([G - 1])
                    if ahead:
                        value = held(sp, t + 2)
                        sp.wait_ge(ready, 3)
                        sp.wait_ge(bias_done, value)
                        sp.dma_start(mask_in[:, :, :], mask_rows[(tb + 2) % TILES_B]).then_inc(mask_loaded, 16)
                    if new_batch is not None:
                        value = held(sp, count(t, G - 1))
                        sp.wait_ge(ready, 3)
                        sp.wait_ge(full["PV"], value)
                        load_vals(new_batch)
                    for s in range(SUB):
                        value = held(sp, count(t, s))
                        sp.wait_ge(ready, 3)
                        sp.wait_ge(y_added, value)
                        sp.dma_start(x1_rows[t, :, s, :], xres[:, s, :]).then_inc(x1_stored, 16)
                    value = held(sp, (t + 1) * 16 * SUB)
                    sp.wait_ge(ready, 3)
                    sp.wait_ge(x1_stored, value)

                sp.dma_start(xn[:, :, :], x_rows[0]).then_inc(x_loaded, 16)
                sp.dma_start(mask_in[:, :, :], mask_rows[0]).then_inc(mask_loaded, 16)
                sp.wait_ge(ready, 3)
                for g in range(G):
                    load_keys(0, g)
                load_vals(0)
                sp.wait_ge(full["A"], count(0, C - 1))
                sp.dma_start(xn[:, :, :], x_rows[1]).then_inc(x_loaded, 16)
                sp.wait_ge(bias_done, 1)
                sp.dma_start(mask_in[:, :, :], mask_rows[1]).then_inc(mask_loaded, 16)
                with sp.Fori(0, B - 1) as b:
                    for tb in range(TILES_B):
                        traffic(b * TILES_B + tb, tb, new_batch=b + 1 if tb == TILES_B - 1 else None)
                for tb in range(TILES_B):
                    traffic((B - 1) * TILES_B + tb, tb, ahead=tb < TILES_B - 2)

            @block.tensor
            def _(pe):
                def score(t, n):
                    g, s = n // SUB, n % SUB
                    if s == 0:
                        pe.wait_ge(lo["Q"], count(t, g))
                        pe.wait_ge(keys_loaded[g], (t // TILES_B + 1) * (16 * 2 * HG))
                    if not (isinstance(t, int) and t == 0 and n == 0):
                        pe.wait_ge(scores_read, units(t, n - 1))
                    for p in range(2):
                        for j in (HI, LO):
                            last = pe.matmul(score_bank[p][:, 0:PAIR], qT[:, g % 2, p, s * P:(s + 1) * P],
                                             keys[:, j, g, p, :], start=(j == HI), stop=(j == LO))
                    last.then_inc(scores_full, 1)

                def transpose_probs(t, n):
                    g, s = n // SUB, n % SUB
                    early = isinstance(t, int) and t == 0
                    pe.wait_ge(probs_normed, units(t, n))
                    if not (early and n < 2):
                        pe.wait_ge(p_lo, units(t, n - 2))
                    if s == 0 and not (early and g == 0):
                        pe.wait_ge(left_lo, count(t, g - 1))
                    for h in range(HG):
                        pe.transpose(p_bank[n % 2][:, h * P:(h + 1) * P],
                                     normed[:, n % 4, h * P:(h + 1) * P], ident[:, :])
                    pe.transpose(left_bank[0:HG * LEFT, s * P:(s + 1) * P],
                                 normed[:, n % 4, HG * P:HG * KEYS], ident[:, :]).then_inc(p_full, 1)

                def stage(kind, what, t, i, part, rel):
                    if what != "PV":
                        turn, before = turns[kind, rel]
                        bank = two_banks[turn]
                        if before is not None and part != 1:
                            then = t - rel[1] + before[1]
                            pe.wait_ge(y_added if before[0] == "Y" else lo[before[0]], count(then, before[2]))
                    if what == "A":
                        if i == 0:
                            pe.wait_ge(x_normed, t + 1)
                        for s in range(SUB):
                            last = pe.transpose(bank[:, s * P:(s + 1) * P], xn[:, s, i * P:(i + 1) * P], ident[:, :])
                        last.then_inc(full["A"], 1)
                        return
                    if what == "PV":
                        products = [(a, b, h) for h in range(HG + 1) for a, b in PARTS]
                    else:
                        products = [(a, b, c) for c in range(C) for a, b in PARTS]
                    half = len(products) // 2
                    start, stop = {0: (0, half), 1: (half, len(products)), ALL: (0, len(products))}[part]
                    if start == 0:
                        if what == "PV":
                            pe.wait_ge(p_lo, units(t, SUB * i + SUB - 1))
                            pe.wait_ge(left_lo, count(t, i))
                            if i == 0:
                                pe.wait_ge(vals_loaded, (t // TILES_B + 1) * (16 * 4 * HG))
                            if not (isinstance(t, int) and t == 0 and i == 0):
                                pe.wait_ge(lo["PV"], count(t, i - 1))
                        elif what == "Q" and i == 0:
                            pe.wait_ge(lo["A"], count(t, C - 1))
                        elif what == "Y" and i == 0:
                            pe.wait_ge(lo["PV"], count(t, G - 1))
                    for m in range(start, stop):
                        a, b, c = products[m]
                        if what == "PV":
                            v = vals[:, a, i, c, :] if c < HG else vals_left[:, a, i, :]
                            p = pT[:, i % 2, b, c, :] if c < HG else pT_left[:, i % 2, b, :]
                            out, left, right = pv_bank, v, p
                        elif what == "Q":
                            out, left, right = bank, wq[:, a, c, i * P:(i + 1) * P], xnT[:, b, c, :]
                        else:
                            out, left, right = bank, oT[:, a, c, i * P:(i + 1) * P], wo[:, b, c, :]
                        last = pe.matmul(out[:, :], left, right, start=(m == 0), stop=(m == len(products) - 1))
                    if stop == len(products):
                        last.then_inc(full[what], 1)

                def tile(kind, t):
                    def step(n, late, stages):
                        if kind in ("first", "steady", "last"):
                            score(t, n)
                        if late is not None:
                            transpose_probs(*late)
                        for s in stages:
                            stage(kind, *s)
                    walk(kind, t, step, engine_is_pe=True)

                all_tiles(pe, tile)

            @block.scalar
            def _(act):
                def split(psum, part, wait, value, done):
                    act.wait_ge(wait, value)
                    nc.scalar.activation(part, psum, ACT.Copy).then_inc(done, 1)

                def exps(t, n):
                    act.wait_ge(neg_done, units(t, n))
                    if not (isinstance(t, int) and t == 0 and n < 2):
                        act.wait_ge(probs_normed, units(t, n - 2))
                    for h in range(HG):
                        last = nc.scalar.activation(probs[:, n % 2, h, :], scores[:, n % 2, h, :], ACT.Exp,
                                                    bias=neg_top[:, n % 2, h:h + 1],
                                                    accum_out=total[:, n % 2, h:h + 1])
                    last.then_inc(exp_done, 1)

                def probs_hi(t, n):
                    g, s = n // SUB, n % SUB
                    if s == 0 and not (isinstance(t, int) and t == 0 and g < 2):
                        act.wait_ge(full["PV"], count(t, g - 2))
                    split(p_bank[n % 2][:, :].rearrange("p (h k) -> p h k", h=HG),
                          pT[:, g % 2, HI, :, s * P:(s + 1) * P], p_full, units(t, n), p_hi)
                    if s == SUB - 1:
                        split(left_bank[0:HG * LEFT, :], pT_left[:, g % 2, HI, :], p_full, units(t, n), left_hi)

                def tile(kind, t):
                    def step(n, late, stages):
                        for what, tt, i, _, rel in stages:
                            if what == "PV":
                                split(pv_bank[:, :], oT[:, HI, i, :], full[what], count(tt, i), hi[what])
                            elif what == "A":
                                split(two_banks[turns[kind, rel][0]][:, :], xnT[:, HI, i, :],
                                      full[what], count(tt, i), hi[what])
                            elif what == "Q":
                                bank = two_banks[turns[kind, rel][0]]
                                act.wait_ge(full[what], count(tt, i))
                                nc.scalar.activation(qT[0:HALF, i % 2, 0, :], bank[0:HALF, :], ACT.Copy)
                                nc.scalar.activation(qT[HALF:P, i % 2, 1, :], bank[HALF:P, :],
                                                     ACT.Copy).then_inc(hi[what], 1)
                        if late is not None:
                            probs_hi(*late)
                        if kind in ("first", "steady", "last"):
                            exps(t, n)
                    walk(kind, t, step)

                all_tiles(act, tile)

            @block.vector
            def _(dve):
                zeros = nc.vector.memset(raw(keys[:, :, :, :, :]), 0.0)
                zeros.then_inc(ready, 1)
                nc.vector.memset(minus_half[:, :], -0.5).then_inc(ready, 1)

                def split(psum, parts, wait, value, done):
                    dve.wait_ge(wait, value)
                    nc.vector.tensor_tensor(parts[LO], psum, raw(parts[HI]), ALU.subtract).then_inc(done, 1)

                NEXT_MASK = 6

                def mask_bias(t):
                    dve.wait_ge(mask_loaded, (t + 1) * 16)
                    nc.vector.tensor_scalar(next_bias[:, :, 0:KEYS], mask_in[:, :, :], 0, MASKED,
                                            ALU.is_equal, ALU.mult).then_inc(bias_done, 1)
                    dve.wait_ge(bias_done, t + 1)
                    nc.vector.tensor_reduce(any_row[:, 0, :], next_bias[:, :, 0:KEYS], AX.X, ALU.max).then_inc(bias_step, 1)
                    dve.wait_ge(bias_step, t * 4 + 1)
                    nc.vector.tensor_scalar(any_row[:, 1, :], any_row[:, 0, :], 0.0, None,
                                            ALU.is_equal).then_inc(bias_step, 1)
                    dve.wait_ge(bias_step, t * 4 + 2)
                    nc.vector.reciprocal(any_row[:, 2, :], any_row[:, 1, :]).then_inc(bias_step, 1)
                    dve.wait_ge(bias_step, t * 4 + 3)
                    nc.vector.tensor_scalar(next_bias[:, :, KEYS], any_row[:, 2, :], 0.0, None,
                                            ALU.mult).then_inc(bias_step, 1)

                def move_bias(t, s):
                    if s == 0:
                        dve.wait_ge(bias_step, t * 4 + 4)
                    if not (isinstance(t, int) and t == 0):
                        dve.wait_ge(neg_done, units(t - 1, UNITS - SUB + s))
                    nc.vector.tensor_copy(bias[:, s, :], next_bias[:, s, :]).then_inc(bias_moved, 1)

                def read_scores(t, n):
                    unit, old = held(dve, units(t, n)), held(dve, units(t, n - 2))
                    bias_there = held(dve, count(t, n)) if n < SUB else None
                    dve.wait_ge(ready, 3)
                    dve.wait_ge(scores_full, unit)
                    if not (isinstance(t, int) and t == 0 and n < 2):
                        dve.wait_ge(exp_done, old)
                    if n < SUB:
                        dve.wait_ge(bias_moved, bias_there)
                    for h in range(HG):
                        cols = slice((h % 2) * KEYS, (h % 2 + 1) * KEYS)
                        last = nc.vector.tensor_tensor_reduce(
                            out=scores[:, n % 2, h, :], in0=score_bank[h // 2][:, cols],
                            in1=bias[:, n % SUB, 0:KEYS], scale=DK ** -0.5, scalar=MASKED,
                            op0=ALU.add, op1=ALU.max, accum_out=top[:, n % 2, h:h + 1])
                    last.then_inc(scores_read, 1)
                    dve.wait_ge(scores_read, units(t, n))
                    nc.vector.tensor_scalar(neg_top[:, n % 2, :], top[:, n % 2, :], -1.0,
                                            bias[:, n % SUB, KEYS:KEYS + 1], ALU.mult, ALU.add).then_inc(neg_done, 1)

                def invert(t, n):
                    dve.wait_ge(exp_done, units(t, n))
                    nc.vector.reciprocal(inv_total[:, n % 2, :], total[:, n % 2, :]).then_inc(inv_done, 1)

                def probs_lo(t, n):
                    g, s = n // SUB, n % SUB
                    split(p_bank[n % 2][:, :].rearrange("p (h k) -> p h k", h=HG),
                          [pT[:, g % 2, i, :, s * P:(s + 1) * P] for i in (HI, LO)], p_hi, units(t, n), p_lo)
                    if s == SUB - 1:
                        split(left_bank[0:HG * LEFT, :], [pT_left[:, g % 2, i, :] for i in (HI, LO)],
                              left_hi, count(t, g), left_lo)

                def row_stats(t, s):
                    if s == 0:
                        dve.wait_ge(x_loaded, (t + 1) * 16)
                    nc.vector.bn_stats(stats[:, s, :], xn[:, s, :]).then_inc(stats_step, 1)
                    first_step = held(dve, t * (2 * SUB) + (2 * s + 1))
                    dve.wait_ge(ready, 3)
                    dve.wait_ge(stats_step, first_step)
                    nc.vector.bn_aggr(moments[:, s, :], stats[:, s, :]).then_inc(stats_step, 1)
                    if s == SUB - 1:
                        dve.wait_ge(stats_step, (t + 1) * (2 * SUB))
                        nc.vector.tensor_scalar(var_eps[:, :], moments[:, :, 1], EPS, None,
                                                ALU.add).then_inc(var_done, 1)

                def tile(kind, t):
                    def step(n, late, stages):
                        if kind in ("first", "steady", "last"):
                            read_scores(t, n)
                        elif kind == "before":
                            for s in range(SUB):
                                row_stats(0, s)
                            mask_bias(0)
                            for s in range(SUB):
                                move_bias(0, s)
                        for what, tt, i, _, rel in stages:
                            if what == "Y":
                                if i == 0:
                                    dve.wait_ge(xres_loaded, (tt + 1) * 16)
                                dve.wait_ge(full[what], count(tt, i))
                                nc.vector.tensor_tensor(xres[:, i, :], two_banks[turns[kind, rel][0]][:, :],
                                                        xres[:, i, :], ALU.add).then_inc(y_added, 1)
                            elif what == "PV":
                                split(pv_bank[:, :], [oT[:, j, i, :] for j in (HI, LO)],
                                      hi[what], count(tt, i), lo[what])
                            elif what == "A":
                                split(two_banks[turns[kind, rel][0]][:, :], [xnT[:, j, i, :] for j in (HI, LO)],
                                      hi[what], count(tt, i), lo[what])
                            else:
                                bank = two_banks[turns[kind, rel][0]]
                                dve.wait_ge(hi[what], count(tt, i))
                                nc.vector.tensor_tensor(qT[HALF:P, i % 2, 0, :], bank[0:HALF, :],
                                                        raw(qT[0:HALF, i % 2, 0, :]), ALU.subtract)
                                nc.vector.tensor_tensor(qT[0:HALF, i % 2, 1, :], bank[HALF:P, :],
                                                        raw(qT[HALF:P, i % 2, 1, :]), ALU.subtract).then_inc(lo[what], 1)
                        if kind in ("first", "steady", "last") and n > 0:
                            invert(t, n - 1)
                        if late is not None:
                            probs_lo(*late)
                        if kind in ("first", "steady") and 1 <= n < 1 + SUB:
                            row_stats(t + 1, n - 1)
                        if kind in ("first", "steady"):
                            if n == NEXT_MASK:
                                mask_bias(t + 1)
                            if n > UNITS - SUB:
                                move_bias(t + 1, n - (UNITS - SUB + 1))
                            if n == UNITS - 1:
                                move_bias(t + 1, SUB - 1)
                        if kind in ("first", "steady", "last") and n == UNITS - 1:
                            invert(t, n)
                    walk(kind, t, step)

                all_tiles(dve, tile)

            @block.gpsimd
            def _(pool):
                nc.gpsimd.memset(raw(vals[:, :, :, :, :]), 0.0)
                nc.gpsimd.memset(raw(vals_left[:, :, :, :]), 0.0).then_inc(ready, 1)

                def layer_norm(t, s):
                    if s == 0:
                        pool.wait_ge(var_done, t + 1)
                        nc.gpsimd.tensor_tensor(rstd[:, :], var_eps[:, :], minus_half[:, :],
                                                ALU.pow).then_inc(rstd_done, 1)
                        tile_rstd = held(pool, t + 1)
                        pool.wait_ge(ready, 3)
                        pool.wait_ge(rstd_done, tile_rstd)
                    last = nc.gpsimd.tensor_scalar(xn[:, s, :], xn[:, s, :], moments[:, s, 0:1],
                                                   rstd[:, s:s + 1], ALU.subtract, ALU.mult)
                    if s == SUB - 1:
                        last.then_inc(x_normed, 1)

                def normalise(t, n):
                    pool.wait_ge(inv_done, units(t, n))
                    if not (isinstance(t, int) and t == 0 and n < 4):
                        pool.wait_ge(p_full, units(t, n - 4))
                    inv = inv_total[:, n % 2, :].unsqueeze(2)
                    for a, b, c in ((0, P, 0), (P, KEYS, HG * P)):
                        last = nc.gpsimd.tensor_tensor(
                            normed[:, n % 4, c:c + HG * (b - a)].rearrange("p (h k) -> p h k", h=HG),
                            probs[:, n % 2, :, a:b], inv.to_broadcast([P, HG, b - a]), ALU.mult)
                    last.then_inc(probs_normed, 1)

                def tile(kind, t):
                    if kind == "before":
                        for s in range(SUB):
                            layer_norm(0, s)
                    if kind not in ("first", "steady", "last"):
                        return
                    for n in range(UNITS):
                        normalise(t, n)
                        if kind != "last" and 5 <= n < 5 + SUB:
                            layer_norm(t + 1, n - 5)

                all_tiles(pool, tile)


def ffn(nc, sem, banks, ident, sum_parts, ar, b2s, W1, W2, b1_parts, x1, out):
    with ExitStack() as stack:
        def sb(name, shape, dt):
            return stack.enter_context(nc.sbuf_tensor(name, shape, dt))

        w1 = sb("w1", [P, 2, C, F], F32R)
        w2 = sb("w2", [P, 2, FC, D], F32R)
        b1s = sb("b1s", [STACK, F], F32R)
        xin = sb("xin", [P, 2, D], F32)
        xres = sb("ffn_xres", [P, SUB, D], F32)
        xnT = sb("ffn_xnT", [P, 2, 2, C, TILE], F32R)
        hid = sb("hid", [P, 2, 2, TILE], F32R)
        z_rows = sb("z_rows", [2 * Q, TILE], F32)
        z = sb("z", [P, SUB, AR], F32)
        g_top = sb("g_top", [P, SUB], F32)
        g_exp = sb("g_exp", [P, SUB, E], F32)
        g_sum = sb("g_sum", [P, SUB], F32)
        g_inv = sb("g_inv", [P, SUB], F32)
        gate = sb("gate", [P, SUB, E], F32)
        zg = sb("zg", [P, SUB, ER], F32)
        zs = sb("zs", [P, SUB, 3, Q], F32R)
        zsT = sb("zsT", [STACK, 2, TILE], F32R)
        stats = sb("ffn_stats", [P, 2, 6], F32)
        moments = sb("ffn_moments", [P, 2, 2], F32)
        var_eps = sb("ffn_var_eps", [P, 2], F32)
        minus_half = sb("ffn_minus_half", [P, 1], F32)
        rstd = sb("ffn_rstd", [P, 2], F32)

        f1_bank = (banks[0], banks[1])
        y_bank = (banks[2], banks[3], banks[4], banks[5])
        z_bank = (banks[6], banks[7])

        ready = sem("ffn_ready")
        w_loaded = [sem(f"w_loaded{i}") for i in range(SUB)]
        w_hi, w_lo = sem("w_hi"), sem("w_lo")
        b1s_loaded = sem("b1s_loaded")
        xin_loaded = [sem(f"xin_loaded{i}") for i in range(2)]
        stats_step = sem("ffn_stats_step")
        rstd_done = sem("ffn_rstd_done")
        x_normed = sem("ffn_x_normed")
        x_full, x_hi, x_lo = sem("x_full"), sem("x_hi"), sem("x_lo")
        f1_full, h_hi, h_lo = sem("f1_full"), sem("h_hi"), sem("h_lo")
        z_full, z_copied = sem("z_full"), sem("z_copied")
        z_turned = sem("z_turned")
        gate_step = sem("gate_step")
        gate_exp = sem("gate_exp")
        zs_full, zs_copied = sem("zs_full"), sem("zs_copied")
        y_full, y_added = sem("y_full"), sem("ffn_y_added")
        xres_loaded, stored = sem("ffn_xres_loaded"), sem("stored")
        GATE_STEPS = 9

        def blocks(t, j):
            return t * FC + (j + 1)

        def subs(t, s):
            return t * SUB + (s + 1)

        def nth(kind, layer, t):
            if layer == 0:
                return 1 if kind == "before" else t * 2
            return t * 2 + (2 if kind == "last" else 3)

        def first_nth(t):
            return 1 if isinstance(t, int) and t == 0 else t * 2

        w1_rows = W1.rearrange("(c p) f -> p c f", p=P)
        x1_rows = x1.rearrange("(t s p) d -> t p s d", s=SUB, p=P)
        out_rows = out.rearrange("b (t s p) d -> (b t) p s d", s=SUB, p=P)

        STATS = {1: 0, 3: 1, 5: 2, 7: 3}
        TURN = {3: 0, 5: 1, 7: 2, 9: 3}
        Z1, TURN_Z1, TURN_ZS1 = 11, 12, 14

        def all_tiles(engine, before, tile):
            before()
            tile("first", 0, 0)
            with engine.Fori(0, (TILES - 2) // 2) as pair:
                tile("steady", pair * 2 + 1, 1)
                tile("steady", pair * 2 + 2, 0)
            tile("last", TILES - 1, 1)

        with nc.Block() as block:
            @block.sync
            def _(sp):
                def load_x(t, s):
                    if not (isinstance(t, int) and t == 0 and s < 2):
                        value = held(sp, subs(t, s - 2))
                        sp.wait_ge(ready, 3)
                        sp.wait_ge(x_full, value)
                    sp.dma_start(xin[:, s % 2, :], x1_rows[t, :, s, :]).then_inc(xin_loaded[s % 2], 16)

                def tile(kind, t, parity):
                    if kind == "steady":
                        load_x(t + 1, 0)
                        load_x(t + 1, 1)
                    if kind != "first":
                        for s in range(SUB):
                            value = held(sp, subs(t - 1, s))
                            sp.wait_ge(ready, 3)
                            sp.wait_ge(y_added, value)
                            sp.dma_start(out_rows[t - 1, :, s, :], xres[:, s, :]).then_inc(stored, 16)
                        value = held(sp, t * (16 * SUB))
                        sp.wait_ge(ready, 3)
                        sp.wait_ge(stored, value)
                    sp.dma_start(xres[:, :, :], x1_rows[t]).then_inc(xres_loaded, 16)
                    if kind == "steady":
                        load_x(t + 1, 2)
                        load_x(t + 1, 3)

                NEXT_X = {3: 0, 4: 1, 8: 2, 10: 3}

                def before():
                    load_x(0, 0)
                    load_x(0, 1)
                    for j in range(FC):
                        if j == 2:
                            load_x(0, 2)
                            load_x(0, 3)
                        if j in NEXT_X:
                            load_x(1, NEXT_X[j])
                        if j >= 2:
                            sp.wait_ge(w_lo, 2 * (j - 2) + 1)
                        sp.dma_start(xres[:, j % 2, :].rearrange("p (c f) -> p c f", c=C),
                                     w1_rows[:, :, j * P:(j + 1) * P]).then_inc(w_loaded[j % 2], 16)
                        if j >= 2:
                            sp.wait_ge(w_lo, 2 * (j - 2) + 2)
                        sp.dma_start(xres[:, 2 + j % 2, :], W2[j * P:(j + 1) * P, :]).then_inc(w_loaded[2 + j % 2], 16)
                        if j == 0:
                            sp.dma_start(raw(b1s[:, :]), b1_parts).then_inc(b1s_loaded, 16)
                    sp.wait_ge(w_lo, 2 * FC)

                all_tiles(sp, before, tile)
                for s in range(SUB):
                    sp.wait_ge(y_added, subs(TILES - 1, s))
                    sp.dma_start(out_rows[TILES - 1, :, s, :], xres[:, s, :]).then_inc(stored, 16)
                sp.wait_ge(stored, TILES * 16 * SUB)

            @block.tensor
            def _(pe):
                def turn_x(t, s):
                    early = isinstance(t, int) and t == 0
                    pe.wait_ge(x_normed, subs(t, s))
                    if s > 0:
                        pe.wait_ge(x_lo, subs(t, s - 1))
                    elif not early:
                        pe.wait_ge(zs_copied, first_nth(t - 1))
                    for c in range(C):
                        last = pe.transpose(z_bank[0][:, c * P:(c + 1) * P],
                                            xin[:, s % 2, c * P:(c + 1) * P], ident[:, :])
                    last.then_inc(x_full, 1)

                def z1(t, parity):
                    pe.wait_ge(x_lo, subs(t, SUB - 1))
                    for n, (c, i) in enumerate((c, i) for c in range(C) for i in (HI, LO)):
                        last = pe.matmul(z_bank[0][0:ARW, :], ar[:, c, :], xnT[:, parity, i, c, :],
                                         start=(n == 0), stop=(n == 2 * C - 1))
                    last.then_inc(z_full, 1)

                def turn_z(layer, n):
                    pe.wait_ge(z_copied, n)
                    for s in range(SUB):
                        last = pe.matmul(z_bank[layer][:, s * AR:(s + 1) * AR], z_rows[:, s * P:(s + 1) * P],
                                         sum_parts[:, :], start=True, stop=True)
                    last.then_inc(z_turned, 1)

                def turn_zs(layer, n):
                    pe.wait_ge(gate_step, n * GATE_STEPS)
                    for s in range(SUB):
                        last = pe.transpose(z_bank[layer][0:STACK, s * P:(s + 1) * P],
                                            raw(zs[:, s, :, :]).rearrange("p a b -> p (a b)"), ident[:, :])
                    last.then_inc(zs_full, 1)

                def f1(t, j, parity, part=slice(0, 3 * C + 1)):
                    if part.start == 0:
                        if isinstance(t, int) and t == 0:
                            pe.wait_ge(w_lo, 2 * j + 1)
                        if not (isinstance(t, int) and t == 0 and j < 2):
                            pe.wait_ge(h_lo, blocks(t, j - 2))
                    terms = [(c, a, b) for c in range(C) for a, b in PARTS] + [None]
                    for n in range(part.start, part.stop):
                        if terms[n] is None:
                            if j == 0:
                                pe.wait_ge(zs_copied, first_nth(t))
                                pe.wait_ge(b1s_loaded, 16)
                            last = pe.matmul(f1_bank[j % 2][:, :], b1s[:, j * P:(j + 1) * P], zsT[:, 0, :],
                                             start=False, stop=True)
                            last.then_inc(f1_full, 1)
                        else:
                            c, a, b = terms[n]
                            pe.matmul(f1_bank[j % 2][:, :], w1[:, a, c, j * P:(j + 1) * P],
                                      xnT[:, parity, b, c, :], start=(n == 0), stop=False)

                def f2(t, j):
                    early = isinstance(t, int) and t == 0
                    pe.wait_ge(h_lo, blocks(t, j))
                    if early:
                        pe.wait_ge(w_lo, 2 * j + 2)
                    for s in range(SUB):
                        if j == 0 and not early:
                            pe.wait_ge(y_added, subs(t - 1, s))
                        for a, b in PARTS:
                            pe.matmul(y_bank[s][:, :], hid[:, j % 2, a, s * P:(s + 1) * P], w2[:, b, j, :],
                                      start=(j == 0 and (a, b) == PARTS[0]), stop=False)
                    for i in (HI, LO):
                        last = pe.matmul(z_bank[1][0:ARW, :], ar[:, C + j, :], hid[:, j % 2, i, :],
                                         start=(j == 0 and i == HI), stop=(j == FC - 1 and i == LO))
                    if j == FC - 1:
                        last.then_inc(z_full, 1)

                def lora2(n):
                    pe.wait_ge(zs_copied, n)
                    for s in range(SUB):
                        pe.matmul(y_bank[s][:, :], zsT[:, 1, s * P:(s + 1) * P], b2s[:, :],
                                  start=False, stop=True).then_inc(y_full, 1)

                def before():
                    for s in range(SUB):
                        turn_x(0, s)
                    z1(0, 0)
                    turn_z(0, 1)
                    turn_zs(0, 1)
                    f1(0, 0, 0)
                    f1(0, 1, 0)

                def tile(kind, t, parity):
                    more = kind != "last"
                    for j in range(FC):
                        f2(t, j)
                        if j + 2 < FC:
                            f1(t, j + 2, parity)
                        if more:
                            if j in TURN:
                                turn_x(t + 1, TURN[j])
                            elif j == Z1:
                                z1(t + 1, 1 - parity)
                            elif j == TURN_Z1:
                                turn_z(0, nth(kind, 0, t + 1))
                            elif j == TURN_ZS1:
                                turn_zs(0, nth(kind, 0, t + 1))
                    n = nth(kind, 1, t)
                    if more:
                        f1(t + 1, 0, 1 - parity, slice(0, 4))
                    turn_z(1, n)
                    if more:
                        f1(t + 1, 0, 1 - parity, slice(4, 3 * C + 1))
                        f1(t + 1, 1, 1 - parity, slice(0, 9))
                    turn_zs(1, n)
                    if more:
                        f1(t + 1, 1, 1 - parity, slice(9, 3 * C + 1))
                    lora2(n)

                all_tiles(pe, before, tile)

            @block.scalar
            def _(act):
                def split_w(j):
                    act.wait_ge(w_loaded[j % 2], 16 * (j // 2 + 1))
                    nc.scalar.activation(w1[:, HI, :, j * P:(j + 1) * P],
                                         xres[:, j % 2, :].rearrange("p (c f) -> p c f", c=C),
                                         ACT.Copy).then_inc(w_hi, 1)
                    act.wait_ge(w_loaded[2 + j % 2], 16 * (j // 2 + 1))
                    nc.scalar.activation(w2[:, HI, j, :], xres[:, 2 + j % 2, :], ACT.Copy).then_inc(w_hi, 1)

                def x_part(t, s, parity):
                    act.wait_ge(x_full, subs(t, s))
                    nc.scalar.activation(xnT[:, parity, HI, :, s * P:(s + 1) * P],
                                         z_bank[0][:, :].rearrange("p (c k) -> p c k", c=C), ACT.Copy).then_inc(x_hi, 1)

                def copy_z(layer, n):
                    act.wait_ge(z_full, n)
                    nc.scalar.activation(z_rows[:, :], z_bank[layer][0:2 * Q, :], ACT.Copy).then_inc(z_copied, 1)

                def exps(n):
                    act.wait_ge(gate_step, n * GATE_STEPS - (GATE_STEPS - 3))
                    nc.scalar.activation(g_exp[:, :, :], g_exp[:, :, :], ACT.Exp).then_inc(gate_exp, 1)

                def copy_zs(layer, n):
                    act.wait_ge(zs_full, n)
                    nc.scalar.activation(zsT[:, layer, :], z_bank[layer][0:STACK, :], ACT.Copy).then_inc(zs_copied, 1)

                def relu(t, j):
                    act.wait_ge(f1_full, blocks(t, j))
                    nc.scalar.activation(hid[:, j % 2, HI, :], f1_bank[j % 2][:, :], ACT.Relu).then_inc(h_hi, 1)

                def before():
                    split_w(0)
                    for s in range(SUB):
                        x_part(0, s, 0)
                    copy_z(0, 1)
                    exps(1)
                    split_w(1)
                    copy_zs(0, 1)
                    relu(0, 0)
                    relu(0, 1)

                def tile(kind, t, parity):
                    more = kind != "last"
                    for j in range(FC):
                        if kind == "first" and j + 2 < FC:
                            split_w(j + 2)
                        if j + 2 < FC:
                            relu(t, j + 2)
                        if more:
                            if j in TURN:
                                x_part(t + 1, TURN[j], 1 - parity)
                            elif j == Z1:
                                copy_z(0, nth(kind, 0, t + 1))
                            elif j == TURN_Z1:
                                exps(nth(kind, 0, t + 1))
                            elif j == TURN_ZS1:
                                copy_zs(0, nth(kind, 0, t + 1))
                    n = nth(kind, 1, t)
                    copy_z(1, n)
                    exps(n)
                    if more:
                        relu(t + 1, 0)
                    copy_zs(1, n)
                    if more:
                        relu(t + 1, 1)

                all_tiles(act, before, tile)

            @block.vector
            def _(dve):
                nc.vector.memset(minus_half[:, :], -0.5).then_inc(ready, 1)
                nc.vector.memset(raw(zs[:, :, :, :]), 0.0).then_inc(ready, 1)
                dve.wait_ge(ready, 2)
                nc.vector.memset(raw(zs[:, :, 0:2, ER:ER + 1]), 1.0).then_inc(ready, 1)

                def split_w(j):
                    dve.wait_ge(w_hi, 2 * j + 1)
                    nc.vector.tensor_tensor(w1[:, LO, :, j * P:(j + 1) * P],
                                            xres[:, j % 2, :].rearrange("p (c f) -> p c f", c=C),
                                            raw(w1[:, HI, :, j * P:(j + 1) * P]), ALU.subtract).then_inc(w_lo, 1)
                    dve.wait_ge(w_hi, 2 * j + 2)
                    nc.vector.tensor_tensor(w2[:, LO, j, :], xres[:, 2 + j % 2, :], raw(w2[:, HI, j, :]),
                                            ALU.subtract).then_inc(w_lo, 1)

                def row_stats(t, s):
                    v = t * (3 * SUB) + 3 * s
                    dve.wait_ge(xin_loaded[s % 2], t * (8 * SUB) + 16 * (s // 2 + 1))
                    nc.vector.bn_stats(stats[:, s % 2, :], xin[:, s % 2, :]).then_inc(stats_step, 1)
                    first_step = held(dve, v + 1)
                    dve.wait_ge(ready, 3)
                    dve.wait_ge(stats_step, first_step)
                    nc.vector.bn_aggr(moments[:, s % 2, :], stats[:, s % 2, :]).then_inc(stats_step, 1)
                    dve.wait_ge(stats_step, v + 2)
                    nc.vector.tensor_scalar(var_eps[:, s % 2:s % 2 + 1], moments[:, s % 2, 1:2], EPS, None,
                                            ALU.add).then_inc(stats_step, 1)

                def x_part(t, s, parity):
                    dve.wait_ge(x_hi, subs(t, s))
                    nc.vector.tensor_tensor(xnT[:, parity, LO, :, s * P:(s + 1) * P],
                                            z_bank[0][:, :].rearrange("p (c k) -> p c k", c=C),
                                            raw(xnT[:, parity, HI, :, s * P:(s + 1) * P]),
                                            ALU.subtract).then_inc(x_lo, 1)

                def relu(t, j):
                    dve.wait_ge(h_hi, blocks(t, j))
                    nc.vector.scalar_tensor_tensor(out=hid[:, j % 2, LO, :], in0=f1_bank[j % 2][:, :], scalar=0.0,
                                                   in1=raw(hid[:, j % 2, HI, :]), op0=ALU.max,
                                                   op1=ALU.subtract).then_inc(h_lo, 1)

                def route(layer, n):
                    done = n * GATE_STEPS - GATE_STEPS

                    def after(k):
                        dve.wait_ge(gate_step, done + k)

                    logits = z[:, :, ER:ER + E]
                    dve.wait_ge(z_turned, n)
                    nc.vector.tensor_copy(z[:, :, :].rearrange("p s c -> p (s c)"),
                                          z_bank[layer][:, 0:SUB * AR]).then_inc(gate_step, 1)
                    after(1)
                    nc.vector.tensor_reduce(g_top[:, :], logits, AX.X, ALU.max).then_inc(gate_step, 1)
                    after(2)
                    nc.vector.tensor_tensor(g_exp[:, :, :], logits, g_top[:, :].unsqueeze(2).to_broadcast([P, SUB, E]),
                                            ALU.subtract).then_inc(gate_step, 1)
                    dve.wait_ge(gate_exp, n)
                    nc.vector.tensor_reduce(g_sum[:, :], g_exp[:, :, :], AX.X, ALU.add).then_inc(gate_step, 1)
                    after(4)
                    nc.vector.reciprocal(g_inv[:, :], g_sum[:, :]).then_inc(gate_step, 1)
                    after(5)
                    nc.vector.scalar_tensor_tensor(out=gate[:, :, :], in0=g_exp[:, :, :], scalar=1.0 / R,
                                                   in1=g_inv[:, :].unsqueeze(2).to_broadcast([P, SUB, E]),
                                                   op0=ALU.mult, op1=ALU.mult).then_inc(gate_step, 1)
                    after(6)
                    nc.vector.tensor_tensor(zg[:, :, :].rearrange("p s (e r) -> p s e r", e=E),
                                            z[:, :, 0:ER].rearrange("p s (e r) -> p s e r", e=E),
                                            gate[:, :, :].unsqueeze(3).to_broadcast([P, SUB, E, R]),
                                            ALU.mult).then_inc(gate_step, 1)
                    after(7)
                    nc.vector.tensor_copy(zs[:, :, 0:2, 0:ER],
                                          zg[:, :, :].unsqueeze(2).to_broadcast([P, SUB, 2, ER])).then_inc(gate_step, 1)
                    after(8)
                    nc.vector.tensor_tensor(zs[:, :, 2, 0:ER], zg[:, :, :], raw(zs[:, :, 0, 0:ER]),
                                            ALU.subtract).then_inc(gate_step, 1)

                def before():
                    row_stats(0, 0)
                    row_stats(0, 1)
                    split_w(0)
                    for s in range(SUB):
                        x_part(0, s, 0)
                        if s + 2 < SUB:
                            row_stats(0, s + 2)
                    route(0, 1)
                    split_w(1)
                    relu(0, 0)
                    relu(0, 1)

                def tile(kind, t, parity):
                    more = kind != "last"
                    for j in range(FC):
                        if kind == "first" and j + 2 < FC:
                            split_w(j + 2)
                        if more and j in STATS:
                            row_stats(t + 1, STATS[j])
                        if j + 2 < FC:
                            relu(t, j + 2)
                        if more:
                            if j in TURN:
                                x_part(t + 1, TURN[j], 1 - parity)
                            elif j == TURN_Z1:
                                route(0, nth(kind, 0, t + 1))
                    n = nth(kind, 1, t)
                    route(1, n)
                    if more:
                        relu(t + 1, 0)
                        relu(t + 1, 1)
                    dve.wait_ge(xres_loaded, (t + 1) * 16)
                    for s in range(SUB):
                        dve.wait_ge(y_full, subs(t, s))
                        nc.vector.tensor_tensor(xres[:, s, :], y_bank[s][:, :], xres[:, s, :],
                                                ALU.add).then_inc(y_added, 1)

                all_tiles(dve, before, tile)

            @block.gpsimd
            def _(pool):
                def layer_norm(t, s):
                    pool.wait_ge(stats_step, t * (3 * SUB) + (3 * s + 3))
                    nc.gpsimd.tensor_tensor(rstd[:, s % 2:s % 2 + 1], var_eps[:, s % 2:s % 2 + 1],
                                            minus_half[:, :], ALU.pow).then_inc(rstd_done, 1)
                    own_rstd = held(pool, subs(t, s))
                    pool.wait_ge(ready, 3)
                    pool.wait_ge(rstd_done, own_rstd)
                    nc.gpsimd.tensor_scalar(xin[:, s % 2, :], xin[:, s % 2, :], moments[:, s % 2, 0:1],
                                            rstd[:, s % 2:s % 2 + 1], ALU.subtract, ALU.mult).then_inc(x_normed, 1)

                for s in range(SUB):
                    layer_norm(0, s)
                with pool.Fori(1, TILES) as t:
                    for s in range(SUB):
                        layer_norm(t, s)


def build(nc, x, ctx, mask, Wq, Wk, Wv, Wo, W1, b1, A1, B1, R1, W2, b2, A2, B2, R2, out):
    k_parts = nc.dram_tensor("k_parts", (2, B, P, G, KEYS), F32, kind="Internal").ap()
    v_parts = nc.dram_tensor("v_parts", (2, B, KEYS, D), F32, kind="Internal").ap()
    b1_parts = nc.dram_tensor("b1_parts", (STACK, F), F32, kind="Internal").ap()
    x1 = nc.dram_tensor("x1", (B * S, D), F32, kind="Internal").ap()
    with ExitStack() as stack:
        def sem(name):
            return stack.enter_context(nc.semaphore(name))

        banks = Banks(nc, stack)
        ident = stack.enter_context(nc.sbuf_tensor("ident", [P, P], F32))
        sum_parts = stack.enter_context(nc.sbuf_tensor("sum_parts", [2 * Q, AR], F32))
        ar = stack.enter_context(nc.sbuf_tensor("ar", [P, C + FC, ARW], F32R))
        b2s = stack.enter_context(nc.sbuf_tensor("b2s", [STACK, D], F32R))
        with ExitStack() as first_two:
            wq = first_two.enter_context(nc.sbuf_tensor("wq", [P, 2, C, D], F32R))
            wo = first_two.enter_context(nc.sbuf_tensor("wo", [P, 2, C, D], F32R))
            prepare(nc, sem, banks, ident, sum_parts, wq, wo, ar, b2s, ctx, Wq, Wk, Wv, Wo,
                    (A1, B1, R1, b1, A2, B2, R2, b2), k_parts, v_parts, b1_parts)
            attention(nc, sem, banks, ident, wq, wo, x, mask, k_parts, v_parts, x1)
        ffn(nc, sem, banks, ident, sum_parts, ar, b2s, W1, W2, b1_parts, x1, out)


_INS = ["x", "ctx_1024", "mask_SxS2_ik0", "L0_xattn_Wq", "L0_xattn_Wk", "L0_xattn_Wv", "L0_xattn_Wo",
        "L0_ffn_W1", "L0_ffn_b1", "L0_ffn_A1", "L0_ffn_B1", "L0_ffn_R1",
        "L0_ffn_W2", "L0_ffn_b2", "L0_ffn_A2", "L0_ffn_B2", "L0_ffn_R2"]


def kernel(**inputs):
    import numpy as _np
    import concourse.bacc as _bacc
    from concourse import mybir as _mybir
    from concourse.bass_utils import run_bass_kernel_spmd as _run

    nc = _bacc.Bacc("TRN2", target_bir_lowering=False, num_devices=1)
    arrays, args = {}, []
    for name in _INS:
        a = _np.ascontiguousarray(inputs[name])
        arrays[f"in_{name}_dram"] = a
        args.append(nc.dram_tensor(f"in_{name}_dram", a.shape, _mybir.dt.from_np(a.dtype), kind="ExternalInput").ap())
    args.append(nc.dram_tensor("out_0_dram", (B, S, D), F32, kind="ExternalOutput").ap())
    build(nc, *args)
    r = _run(nc, [arrays], core_ids=[0])
    return r.results[0]["out_0_dram"]
```

```python
from contextlib import ExitStack

import concourse.bass as bass
from concourse import mybir

F32 = mybir.dt.float32
F32R = mybir.dt.float32r
I32 = mybir.dt.int32
ALU = mybir.AluOpType
ACT = mybir.ActivationFunctionType
AX = mybir.AxisListType

P = 128
B, S, D = 4, 2048, 512
KEYS, H = 154, 16
DK = D // H
F = 2048
E, R = 3, 8
EPS = 1e-5
C = D // P
G = C
HG = P // DK
HALF = P // 2
LEFT = KEYS - P
TILE = 512
SUB = TILE // P
TILES = B * S // TILE
TILES_B = S // TILE
UNITS = G * SUB
PAIR = 2 * KEYS
ER = E * R
FC = F // P
MASKED = -3.0e38
Q = 32
AR = ER + E + 1
ARW = 2 * Q + 2
STACK = 3 * Q
LORA_LOADS = 2 * (E + 1) + 3 * 2 + 2 * 2
HI, LO = 0, 1
PARTS = ((HI, HI), (HI, LO), (LO, HI))


def raw(ap):
    return ap.bitcast(F32)


def held(engine, value):
    return value if isinstance(value, int) else engine.to_reg(value)


class Banks:

    def __init__(self, nc, stack):
        self.bank = [stack.enter_context(nc.psum_tensor(f"bank{i}", [P, 512], F32)) for i in range(8)]

    def __getitem__(self, i):
        return self.bank[i]


def by_rows_of_four(w):
    return w.rearrange("h (p c) k -> p h (c k)", c=C)


def chunk(rows, c):
    return rows.rearrange("r (p c) -> r c p", c=C)[:, c, :]


class AttentionState:

    def __init__(self, nc, sem, stack, rows):
        def sb(name, shape, dt):
            return stack.enter_context(nc.sbuf_tensor(name, shape, dt))

        with ExitStack() as place:
            self.weights_raw = place.enter_context(nc.sbuf_tensor("weights_raw", [P, 4, C * D], F32))
        self.keys = sb("keys", [P, 2, G, 2, PAIR], F32R)
        self.vals = sb("vals", [P, 2, G, HG, P], F32R)
        self.vals_left = sb("vals_left", [HG * LEFT, 2, G, P], F32R)
        self.xn = rows
        self.mask_in = sb("mask_in", [P, SUB, KEYS], I32)
        self.stats = sb("stats", [P, SUB, 6], F32)
        self.moments = sb("moments", [P, SUB, 2], F32)
        self.var_eps = sb("var_eps", [P, SUB], F32)
        self.minus_half = sb("minus_half", [P, SUB], F32)
        self.rstd = sb("rstd", [P, SUB], F32)

        self.ready = sem("att_ready")
        self.keys_loaded = [sem(f"keys_loaded{g}") for g in range(G)]
        self.x_loaded = sem("x_loaded")
        self.mask_loaded = sem("mask_loaded")
        self.stats_step = sem("stats_step")
        self.var_done = sem("var_done")
        self.rstd_done = sem("rstd_done")
        self.x_normed = sem("x_normed")


def row_stats(nc, dve, st, t, s):
    if s == 0:
        dve.wait_ge(st.x_loaded, (t + 1) * 16)
    nc.vector.bn_stats(st.stats[:, s, :], st.xn[:, s, :]).then_inc(st.stats_step, 1)
    first_step = held(dve, t * (2 * SUB) + (2 * s + 1))
    if not isinstance(t, int):
        dve.wait_ge(st.ready, 3)
    dve.wait_ge(st.stats_step, first_step)
    nc.vector.bn_aggr(st.moments[:, s, :], st.stats[:, s, :]).then_inc(st.stats_step, 1)
    if s == SUB - 1:
        dve.wait_ge(st.stats_step, (t + 1) * (2 * SUB))
        nc.vector.tensor_scalar(st.var_eps[:, :], st.moments[:, :, 1], EPS, None,
                                ALU.add).then_inc(st.var_done, 1)


def layer_norm(nc, pool, st, t, s):
    if s == 0:
        pool.wait_ge(st.var_done, t + 1)
        nc.gpsimd.tensor_tensor(st.rstd[:, :], st.var_eps[:, :], st.minus_half[:, :],
                                ALU.pow).then_inc(st.rstd_done, 1)
        tile_rstd = held(pool, t + 1)
        if not isinstance(t, int):
            pool.wait_ge(st.ready, 3)
        pool.wait_ge(st.rstd_done, tile_rstd)
    last = nc.gpsimd.tensor_scalar(st.xn[:, s, :], st.xn[:, s, :], st.moments[:, s, 0:1],
                                   st.rstd[:, s:s + 1], ALU.subtract, ALU.mult)
    if s == SUB - 1:
        last.then_inc(st.x_normed, 1)


def head_keys(st, g):
    for r in range(HG):
        for p in range(2):
            h = 2 * p + r % 2
            yield (raw(st.keys[r * DK:(r + 1) * DK, :, g, p, (r % 2) * KEYS:(r % 2 + 1) * KEYS]),
                   slice(h * DK, (h + 1) * DK))


def prepare(nc, sem, banks, ident, sum_parts, st, wq, wo, ar, b2s, x, ctx, mask, Wq, Wk, Wv, Wo, lora,
            k_parts, v_parts, b1_parts):
    A1, B1, R1, b1, A2, B2, R2, b2 = lora
    with ExitStack() as stack:
        def sb(name, shape, dt):
            return stack.enter_context(nc.sbuf_tensor(name, shape, dt))

        ctx_left = sb("ctx_left", [B * LEFT, D], F32)
        ctx_main = st.xn
        wk_raw, wv_raw, wq_raw = (st.weights_raw[:, i, :].rearrange("p (h k) -> p h k", h=H) for i in range(3))
        wo_raw = st.weights_raw[:, 3, :].rearrange("p (c d) -> p c d", c=C)
        wk = sb("wk", [P, 2, C, D], F32R)
        wv = sb("wv", [P, 2, C, D], F32R)
        ctxT = sb("ctxT", [P, 2, C, B, KEYS], F32R)
        ctxT_left = sb("ctxT_left", [P, 2, C, B * LEFT], F32R)
        k_out = sb("k_out", [P, 2, G, B, KEYS], F32R)
        v_out = sb("v_out", [P, B, 2, D], F32R)
        vl_out = sb("vl_out", [B * LEFT, 2, D], F32R)
        ar_raw = sb("ar_raw", [P, C + FC, AR], F32)
        b_raw = sb("b_raw", [STACK, F + D], F32)
        b1s = sb("b1s_out", [STACK, F], F32R)

        ident_zero, ident_ready = sem("ident_zero"), sem("ident_ready")
        keys_zero = sem("keys_zero")
        lora_zero = sem("lora_zero")
        lora_loaded = sem("lora_loaded")
        lora_hi, lora_lo = sem("lora_hi"), sem("lora_lo")
        ctx_loaded = sem("ctx_loaded")
        wk_loaded, wv_loaded = sem("wk_loaded"), sem("wv_loaded")
        wq_loaded, wo_loaded = sem("wq_loaded"), sem("wo_loaded")
        bank_full = sem("prep_bank_full")
        bank_hi = sem("prep_bank_hi")
        bank_lo = sem("prep_bank_lo")
        weight_hi = sem("prep_weight_hi")
        weight_lo = sem("prep_weight_lo")
        parts_stored = sem("parts_stored")

        K0 = C + 1
        WO0 = K0 + G * B // 2
        V0 = WO0 + C
        USES = V0 + B + 1

        def result(u):
            bank = banks[u % 8]
            if u < C:
                return (bank[:, :].rearrange("p (b k) -> p b k", b=B),
                        [ctxT[:, i, u, :, 0:P] for i in (HI, LO)])
            if u == C:
                return (bank[:, 0:C * B * LEFT],
                        [ctxT_left[:, i, :, :].rearrange("p c k -> p (c k)") for i in (HI, LO)])
            if u < WO0:
                g, b = (u - K0) // 2, 2 * ((u - K0) % 2)
                return (bank[:, 0:PAIR],
                        [k_out[:, i, g, b:b + 2, :].rearrange("p b k -> p (b k)") for i in (HI, LO)])
            if u < V0:
                return bank[:, :], [wo[:, i, u - WO0, :] for i in (HI, LO)]
            if u == V0:
                return bank[0:B * LEFT, :], [vl_out[:, i, :] for i in (HI, LO)]
            return bank[:, :], [v_out[:, u - V0 - 1, i, :] for i in (HI, LO)]

        def left_twice(i):
            return (banks[C][:, 0:C * B * LEFT].rearrange("p (a k) -> p a k", k=LEFT),
                    ctxT[:, i, :, :, P:KEYS].rearrange("p c b k -> p (c b) k"))

        weights = [(loaded, w[:, h:h + n, :].rearrange("p h (c k) -> p c h k", c=C),
                    [t[:, i, :, h * DK:(h + n) * DK].rearrange("p c (h k) -> p c h k", h=n) for i in (HI, LO)])
                   for loaded, w, t, n in ((wk_loaded, wk_raw, wk, HG), (wv_loaded, wv_raw, wv, H),
                                           (wq_loaded, wq_raw, wq, H))
                   for h in range(0, H, n)]
        WEIGHT_BEFORE = {K0: range(G), K0 + 2: (G,), K0 + 4: (G + 1,)}
        STATS_BEFORE = K0 + 3
        LORA_BEFORE = V0

        with nc.Block() as block:
            @block.sync
            def _(sp):
                sp.dma_start(ctx_main[:, :, :], ctx[:, 0:P, :].rearrange("b k d -> k b d")).then_inc(ctx_loaded, 16)
                for b in range(B):
                    sp.dma_start(ctx_left[b * LEFT:(b + 1) * LEFT, :], ctx[b, P:KEYS, :]).then_inc(ctx_loaded, 16)
                sp.dma_start(wk_raw, by_rows_of_four(Wk)).then_inc(wk_loaded, 16)
                sp.dma_start(wv_raw, by_rows_of_four(Wv)).then_inc(wv_loaded, 16)
                sp.dma_start(wq_raw, by_rows_of_four(Wq)).then_inc(wq_loaded, 16)
                sp.dma_start(wo_raw, Wo.rearrange("(c p) d -> p c d", p=P)).then_inc(wo_loaded, 16)
                sp.wait_ge(bank_full, C)
                sp.dma_start(st.xn[:, :, :], x.rearrange("b (t s p) d -> (b t) p s d", s=SUB, p=P)[0]
                             ).then_inc(st.x_loaded, 16)
                sp.dma_start(st.mask_in[:, :, :], mask.rearrange("(t s p) k -> t p s k", s=SUB, p=P)[0]
                             ).then_inc(st.mask_loaded, 16)
                sp.wait_ge(lora_zero, 2)
                for c0, n, A, Rt in ((0, C, A1, R1), (C, FC, A2, R2)):
                    for e in range(E):
                        sp.dma_start(ar_raw[:, c0:c0 + n, e * R:(e + 1) * R],
                                     A[e, :, :].rearrange("(c p) r -> p c r", p=P)).then_inc(lora_loaded, 16)
                    sp.dma_start(ar_raw[:, c0:c0 + n, ER:ER + E],
                                 Rt.rearrange("(c p) e -> p c e", p=P)).then_inc(lora_loaded, 16)
                for q in range(3):
                    for cols, Bt in ((slice(0, F), B1), (slice(F, F + D), B2)):
                        sp.dma_start(b_raw[q * Q:q * Q + ER, cols],
                                     Bt.rearrange("e r h -> (e r) h")).then_inc(lora_loaded, 16)
                for q in range(2):
                    for cols, bt in ((slice(0, F), b1), (slice(F, F + D), b2)):
                        sp.dma_start(b_raw[q * Q + ER:q * Q + ER + 1, cols],
                                     bt.rearrange("(a h) -> a h", a=1)).then_inc(lora_loaded, 16)
                for g in range(G):
                    sp.wait_ge(bank_lo, K0 + 2 * (g + 1))
                    for i in (HI, LO):
                        sp.dma_start(k_parts[i, :, :, g, :].rearrange("b k n -> k b n"),
                                     raw(k_out[:, i, g, :, :])).then_inc(parts_stored, 16)
                    if g == 1:
                        sp.wait_ge(keys_zero, 1)
                        for place, rows in head_keys(st, 0):
                            sp.dma_start(place, raw(k_out[rows, :, 0, 0, :])).then_inc(st.keys_loaded[0], 16)
                sp.wait_ge(lora_lo, 2)
                sp.dma_start(b1_parts, raw(b1s[:, :])).then_inc(parts_stored, 16)
                sp.wait_ge(bank_lo, V0 + 1)
                for b in range(B):
                    sp.dma_start(v_parts[:, b, P:KEYS, :].rearrange("i k d -> k i d"),
                                 raw(vl_out[b * LEFT:(b + 1) * LEFT, :, :])).then_inc(parts_stored, 16)
                for b in range(B):
                    sp.wait_ge(bank_lo, V0 + b + 2)
                    sp.dma_start(v_parts[:, b, 0:P, :].rearrange("i k d -> k i d"),
                                 raw(v_out[:, b, :, :])).then_inc(parts_stored, 16)
                sp.wait_ge(parts_stored, 16 * (2 * G + 2 * B + 1))
                sp.wait_ge(st.keys_loaded[0], 16 * 2 * HG)

            @block.tensor
            def _(pe):
                pe.wait_ge(ident_ready, 1)
                pe.wait_ge(ctx_loaded, 16 * (1 + B))

                def free(u):
                    if u >= 8:
                        pe.wait_ge(bank_lo, u - 7)

                for c in range(C):
                    for b in range(B):
                        last = pe.transpose(banks[c][:, b * P:(b + 1) * P],
                                            chunk(ctx_main[:, b, :], c), ident[:, :])
                    last.then_inc(bank_full, 1)
                n = B * LEFT
                for c in range(C):
                    last = pe.transpose(banks[C][:, c * n:(c + 1) * n],
                                        chunk(ctx_left[:, :], c), ident[0:n, 0:n])
                last.then_inc(bank_full, 1)
                pe.wait_ge(bank_lo, C + 1)
                for g in range(G):
                    pe.wait_ge(weight_lo, g + 1)
                    for b in range(0, B, 2):
                        u = K0 + 2 * g + b // 2
                        free(u)
                        for n, (c, (i, j)) in enumerate((c, ij) for c in range(C) for ij in PARTS):
                            last = pe.matmul(banks[u % 8][:, 0:PAIR], wk[:, i, c, g * P:(g + 1) * P],
                                             ctxT[:, j, c, b:b + 2, :].rearrange("p b k -> p (b k)"),
                                             start=(n == 0), stop=(n == 3 * C - 1))
                        last.then_inc(bank_full, 1)
                pe.wait_ge(wo_loaded, 16)
                for c in range(C):
                    u = WO0 + c
                    free(u)
                    for e in range(C):
                        last = pe.transpose(banks[u % 8][:, e * P:(e + 1) * P],
                                            wo_raw[:, e, c * P:(c + 1) * P], ident[:, :])
                    last.then_inc(bank_full, 1)
                pe.wait_ge(weight_lo, G + 1)
                for b in (B, *range(B)):
                    u = V0 + (b + 1) % (B + 1)
                    free(u)
                    rows = P if b < B else B * LEFT
                    for n, (c, (i, j)) in enumerate((c, ij) for c in range(C) for ij in PARTS):
                        keys = ctxT[:, i, c, b, 0:P] if b < B else ctxT_left[:, i, c, :]
                        last = pe.matmul(banks[u % 8][0:rows, :], keys, wv[:, j, c, :],
                                         start=(n == 0), stop=(n == 3 * C - 1))
                    last.then_inc(bank_full, 1)

            @block.scalar
            def _(act):
                for u in range(USES):
                    for n in WEIGHT_BEFORE.get(u, ()):
                        loaded, w, parts = weights[n]
                        act.wait_ge(loaded, 16)
                        nc.scalar.activation(parts[HI], w, ACT.Copy).then_inc(weight_hi, 1)
                    if u == LORA_BEFORE:
                        act.wait_ge(lora_loaded, 16 * LORA_LOADS)
                        act.wait_ge(lora_zero, 3)
                        nc.scalar.activation(ar[:, :, 0:AR], ar_raw[:, :, :], ACT.Copy).then_inc(lora_hi, 1)
                        nc.scalar.activation(b1s[:, :], b_raw[:, 0:F], ACT.Copy).then_inc(lora_hi, 1)
                        nc.scalar.activation(b2s[:, :], b_raw[:, F:F + D], ACT.Copy).then_inc(lora_hi, 1)
                    psum, parts = result(u)
                    act.wait_ge(bank_full, u + 1)
                    if u == C:
                        left, place = left_twice(HI)
                        nc.scalar.activation(place, left, ACT.Copy)
                    nc.scalar.activation(parts[HI], psum, ACT.Copy).then_inc(bank_hi, 1)

            @block.vector
            def _(dve):
                nc.vector.memset(st.minus_half[:, :], -0.5).then_inc(st.ready, 1)
                for u in range(USES):
                    for n in WEIGHT_BEFORE.get(u, ()):
                        _, w, parts = weights[n]
                        dve.wait_ge(weight_hi, n + 1)
                        nc.vector.tensor_tensor(parts[LO], w, raw(parts[HI]), ALU.subtract).then_inc(weight_lo, 1)
                    if u == STATS_BEFORE:
                        for s in range(SUB):
                            row_stats(nc, dve, st, 0, s)
                        dve.wait_ge(weight_lo, G + 1)
                        nc.vector.memset(raw(st.keys[:, :, 0, :, :]), 0.0).then_inc(keys_zero, 1)
                    if u == LORA_BEFORE:
                        dve.wait_ge(lora_hi, 3)
                        nc.vector.tensor_tensor(ar[:, :, Q:Q + AR], ar_raw[:, :, :], raw(ar[:, :, 0:AR]),
                                                ALU.subtract).then_inc(lora_lo, 1)
                        for t, cols in ((b1s, slice(0, F)), (b2s, slice(F, F + D))):
                            nc.vector.tensor_tensor(t[Q:2 * Q, :], b_raw[Q:2 * Q, cols], raw(t[Q:2 * Q, :]),
                                                    ALU.subtract).then_inc(lora_lo, 1)
                    psum, parts = result(u)
                    dve.wait_ge(bank_hi, u + 1)
                    if u == C:
                        left, place = left_twice(LO)
                        nc.vector.tensor_tensor(place, left, raw(left_twice(HI)[1]), ALU.subtract)
                    nc.vector.tensor_tensor(parts[LO], psum, raw(parts[HI]), ALU.subtract).then_inc(bank_lo, 1)

            @block.gpsimd
            def _(pool):
                nc.gpsimd.memset(ident[:, :], 0.0).then_inc(ident_zero, 1)
                pool.wait_ge(ident_zero, 1)
                nc.gpsimd.affine_select(out=ident[:, :], in_=ident[:, :], compare_op=ALU.not_equal, fill=1.0,
                                        base=0, pattern=[[-1, P]], channel_multiplier=1).then_inc(ident_ready, 1)
                nc.gpsimd.memset(ar_raw[:, :, :], 0.0).then_inc(lora_zero, 1)
                nc.gpsimd.memset(b_raw[:, :], 0.0).then_inc(lora_zero, 1)
                nc.gpsimd.memset(raw(ar[:, :, :]), 0.0).then_inc(lora_zero, 1)
                nc.gpsimd.memset(sum_parts[:, :], 0.0).then_inc(ident_zero, 1)
                pool.wait_ge(ident_zero, 2)
                nc.gpsimd.affine_select(out=sum_parts[:, :], in_=sum_parts[:, :], compare_op=ALU.not_equal,
                                        fill=1.0, base=0, pattern=[[-1, AR]],
                                        channel_multiplier=1).then_inc(ident_zero, 1)
                pool.wait_ge(ident_zero, 3)
                nc.gpsimd.affine_select(out=sum_parts[:, :], in_=sum_parts[:, :], compare_op=ALU.not_equal,
                                        fill=1.0, base=-Q, pattern=[[-1, AR]],
                                        channel_multiplier=1).then_inc(ident_zero, 1)
                nc.gpsimd.memset(raw(st.vals_left[:, :, :, :]), 0.0)
                layer_norm(nc, pool, st, 0, 0)
                pool.wait_ge(weight_lo, len(weights))
                pool.wait_ge(bank_full, V0)
                nc.gpsimd.memset(raw(st.vals[:, :, :, :, :]), 0.0).then_inc(st.ready, 1)
                nc.gpsimd.memset(raw(st.keys[:, :, 1:G, :, :]), 0.0).then_inc(st.ready, 1)
                for s in range(1, SUB):
                    layer_norm(nc, pool, st, 0, s)


ALL = 2
STEADY = {
    0: [("PV", -1, 2, 1)],
    1: [("Q", 0, 1, 0)],
    2: [("Q", 0, 1, 1), ("Q", 0, 2, 0)],
    3: [("PV", -1, 3, ALL)],
    4: [("Q", 0, 2, 1)],
    5: [("Y", -1, 0, ALL)],
    6: [("Y", -1, 1, ALL)],
    7: [("Y", -1, 2, ALL)],
    8: [("Q", 0, 3, ALL)],
    9: [("Y", -1, 3, ALL)],
    10: [("PV", 0, 0, ALL)],
    11: [("A", 1, 0, ALL), ("A", 1, 1, ALL)],
    12: [("PV", 0, 1, 0), ("A", 1, 2, ALL), ("A", 1, 3, ALL)],
    13: [("PV", 0, 1, 1)],
    14: [("Q", 1, 0, ALL)],
    15: [("PV", 0, 2, 0)],
}
LAG = 3
STEPS = UNITS
BEFORE = {0: [("A", 0, c, ALL) for c in range(C)] + [("Q", 0, 0, ALL)]}
AFTER = {0: [("PV", 0, 2, 1)], LAG - 1: [("PV", 0, 3, ALL)] + [("Y", 0, s, ALL) for s in range(SUB)]}
PLANS = {
    "before": BEFORE,
    "first": {n: [x for x in l if x[1] >= 0] for n, l in STEADY.items()},
    "steady": STEADY,
    "last": {n: [x for x in l if x[1] <= 0] for n, l in STEADY.items()},
    "after": AFTER,
}


def two_bank_plan():
    turns, used = {}, []
    for kind in ("before", "first", "steady", "last", "after"):
        for n in sorted(PLANS[kind]):
            for what, dt, i, part in PLANS[kind][n]:
                if what != "PV" and part != 1:
                    turns[kind, (what, dt, i)] = (len(used) % 2, used[-2] if len(used) > 1 else None)
                    used.append((what, dt, i))
        if kind in ("first", "steady"):
            used = [(a, dt - 1, i) for a, dt, i in used]
            assert len(used) % 2 == 1
    return turns


def attention(nc, sem, banks, ident, st, wq, wo, x, mask, k_parts, v_parts, x1):
    with ExitStack() as stack:
        def sb(name, shape, dt):
            return stack.enter_context(nc.sbuf_tensor(name, shape, dt))

        keys, vals, vals_left, xn, mask_in = st.keys, st.vals, st.vals_left, st.xn, st.mask_in
        ready, keys_loaded, x_loaded, mask_loaded = st.ready, st.keys_loaded, st.x_loaded, st.mask_loaded
        x_normed = st.x_normed
        xres = sb("xres", [P, SUB, D], F32)
        xnT = sb("xnT", [P, 2, C, TILE], F32R)
        qT = sb("qT", [P, 2, 2, TILE], F32R)
        bias = sb("bias", [P, SUB, KEYS], F32)
        next_bias = sb("next_bias", [P, SUB, KEYS], F32)
        next_nan = sb("next_nan", [P, SUB], F32)
        any_row = sb("any_row", [P, 3, SUB], F32)
        scores = sb("scores", [P, 2, HG, KEYS], F32)
        probs = sb("probs", [P, 2, HG, KEYS], F32)
        normed = sb("normed", [P, 4, HG * KEYS], F32)
        pT = sb("pT", [P, 2, 2, HG, TILE], F32R)
        pT_left = sb("pT_left", [HG * LEFT, 2, 2, TILE], F32R)
        oT = sb("oT", [P, 2, G, TILE], F32R)
        neg_top = sb("neg_top", [P, 2, HG], F32)
        total = sb("total", [P, 2, HG], F32)
        inv_total = sb("inv_total", [P, 2, HG], F32)

        score_bank = (banks[0], banks[1])
        p_bank = (banks[2], banks[3])
        left_bank = banks[4]
        pv_bank = banks[5]
        two_banks = (banks[6], banks[7])

        xres_loaded, x1_stored = sem("xres_loaded"), sem("x1_stored")
        vals_loaded = sem("vals_loaded")
        bias_done = sem("bias_done")
        bias_step = sem("bias_step")
        bias_moved = sem("bias_moved")
        scores_full = sem("scores_full")
        scores_read = sem("scores_read")
        exp_done = sem("exp_done")
        inv_done = sem("inv_done")
        probs_normed = sem("probs_normed")
        p_full, p_hi, p_lo = sem("p_full"), sem("p_hi"), sem("p_lo")
        left_hi, left_lo = sem("left_hi"), sem("left_lo")
        full = {k: sem(f"{k}_full") for k in ("A", "Q", "Y", "PV")}
        hi = {k: sem(f"{k}_hi") for k in ("A", "Q", "PV")}
        lo = {k: sem(f"{k}_lo") for k in ("A", "Q", "PV")}
        y_added = sem("y_added")

        def count(t, i):
            return t * 4 + (i + 1)

        def units(t, n):
            return t * UNITS + (n + 1)

        turns = two_bank_plan()
        x_rows = x.rearrange("b (t s p) d -> (b t) p s d", s=SUB, p=P)
        x1_rows = x1.rearrange("(t s p) d -> t p s d", s=SUB, p=P)
        mask_rows = mask.rearrange("(t s p) k -> t p s k", s=SUB, p=P)

        def walk(kind, t, step, engine_is_pe=False):
            plan = PLANS[kind]
            steps = range({"before": 1, "after": LAG + 1}.get(kind, STEPS))
            for n in steps:
                found = plan.get(n, ()) if kind == "before" or engine_is_pe else plan.get(n - 1, ())
                if kind == "before" or (kind == "after" and n == LAG):
                    late = None
                elif kind == "after":
                    late = (t, UNITS - LAG + n)
                elif n >= LAG:
                    late = (t, n - LAG)
                else:
                    late = None if kind == "first" else (t - 1, UNITS - LAG + n)
                step(n, late, [(a, t + dt, i, part, (a, dt, i)) for a, dt, i, part in found
                               if part != 0 or engine_is_pe])

        def all_tiles(engine, tile):
            tile("before", 0)
            tile("first", 0)
            with engine.Fori(1, TILES - 1) as t:
                tile("steady", t)
            tile("last", TILES - 1)
            tile("after", TILES - 1)

        with nc.Block() as block:
            @block.sync
            def _(sp):
                def load_keys(b, g):
                    for place, rows in head_keys(st, g):
                        sp.dma_start(place, k_parts[:, b, rows, g, :].rearrange("i k n -> k i n")
                                     ).then_inc(keys_loaded[g], 16)

                def load_vals(b):
                    for i in (HI, LO):
                        for h in range(HG):
                            cols = slice(h * DK, (h + 1) * DK)
                            v = v_parts[i, b, :, :].rearrange("k (g c) -> k g c", g=G)
                            sp.dma_start(raw(vals[:, i, :, h, cols]), v[0:P, :, cols]).then_inc(vals_loaded, 16)
                            sp.dma_start(raw(vals_left[h * LEFT:(h + 1) * LEFT, i, :, cols]),
                                         v[P:KEYS, :, cols]).then_inc(vals_loaded, 16)

                def traffic(t, tb, ahead=True, new_batch=None, x1_ahead=False):
                    def next_keys(groups):
                        for g in groups:
                            value = held(sp, units(t, SUB * g + SUB - 1))
                            sp.wait_ge(ready, 3)
                            sp.wait_ge(scores_full, value)
                            load_keys(new_batch, g)

                    sp.dma_start(xres[:, :, :], x_rows[t]).then_inc(xres_loaded, 16)
                    if new_batch is not None:
                        next_keys(range(G - 1))
                    if ahead:
                        value = held(sp, count(t + 1, C - 1))
                        sp.wait_ge(ready, 3)
                        sp.wait_ge(full["A"], value)
                        sp.dma_start(xn[:, :, :], x_rows[t + 2]).then_inc(x_loaded, 16)
                    if x1_ahead:
                        sp.wait_ge(full["A"], count(t + 1, C - 1))
                        sp.dma_start(xn[:, :, :], x1_rows[0]).then_inc(x_loaded, 16)
                    if new_batch is not None:
                        next_keys([G - 1])
                    if ahead:
                        value = held(sp, t + 2)
                        sp.wait_ge(ready, 3)
                        sp.wait_ge(bias_done, value)
                        sp.dma_start(mask_in[:, :, :], mask_rows[(tb + 2) % TILES_B]).then_inc(mask_loaded, 16)
                    if new_batch is not None:
                        value = held(sp, count(t, G - 1))
                        sp.wait_ge(ready, 3)
                        sp.wait_ge(full["PV"], value)
                        load_vals(new_batch)
                    for s in range(SUB):
                        value = held(sp, count(t, s))
                        sp.wait_ge(ready, 3)
                        sp.wait_ge(y_added, value)
                        sp.dma_start(x1_rows[t, :, s, :], xres[:, s, :]).then_inc(x1_stored, 16)
                    value = held(sp, (t + 1) * 16 * SUB)
                    sp.wait_ge(ready, 3)
                    sp.wait_ge(x1_stored, value)

                sp.wait_ge(full["A"], count(0, C - 1))
                sp.dma_start(xn[:, :, :], x_rows[1]).then_inc(x_loaded, 16)
                sp.wait_ge(bias_done, 1)
                sp.dma_start(mask_in[:, :, :], mask_rows[1]).then_inc(mask_loaded, 16)
                for g in range(1, G):
                    load_keys(0, g)
                load_vals(0)
                with sp.Fori(0, B - 1) as b:
                    for tb in range(TILES_B):
                        traffic(b * TILES_B + tb, tb, new_batch=b + 1 if tb == TILES_B - 1 else None)
                for tb in range(TILES_B):
                    traffic((B - 1) * TILES_B + tb, tb, ahead=tb < TILES_B - 2, x1_ahead=tb == TILES_B - 2)

            @block.tensor
            def _(pe):
                def score(t, n):
                    g, s = n // SUB, n % SUB
                    if s == 0:
                        pe.wait_ge(lo["Q"], count(t, g))
                        pe.wait_ge(keys_loaded[g], (t // TILES_B + 1) * (16 * 2 * HG))
                    if not (isinstance(t, int) and t == 0 and n == 0):
                        pe.wait_ge(scores_read, units(t, n - 1))
                    for p in range(2):
                        for j in (HI, LO):
                            last = pe.matmul(score_bank[p][:, 0:PAIR], qT[:, g % 2, p, s * P:(s + 1) * P],
                                             keys[:, j, g, p, :], start=(j == HI), stop=(j == LO))
                    last.then_inc(scores_full, 1)

                def transpose_probs(t, n):
                    g, s = n // SUB, n % SUB
                    early = isinstance(t, int) and t == 0
                    pe.wait_ge(probs_normed, units(t, n))
                    if not (early and n < 2):
                        pe.wait_ge(p_lo, units(t, n - 2))
                    for h in range(HG):
                        pe.transpose(p_bank[n % 2][:, h * P:(h + 1) * P],
                                     normed[:, n % 4, h * P:(h + 1) * P], ident[:, :])
                    if s == 0 and not (early and g == 0):
                        pe.wait_ge(left_lo, count(t, g - 1))
                    pe.transpose(left_bank[0:HG * LEFT, s * P:(s + 1) * P],
                                 normed[:, n % 4, HG * P:HG * KEYS], ident[:, :]).then_inc(p_full, 1)

                def stage(kind, what, t, i, part, rel):
                    if what != "PV":
                        turn, before = turns[kind, rel]
                        bank = two_banks[turn]
                        if before is not None and part != 1:
                            then = t - rel[1] + before[1]
                            pe.wait_ge(y_added if before[0] == "Y" else lo[before[0]], count(then, before[2]))
                    if what == "A":
                        if i == 0:
                            pe.wait_ge(x_normed, t + 1)
                        for s in range(SUB):
                            last = pe.transpose(bank[:, s * P:(s + 1) * P], chunk(xn[:, s, :], i), ident[:, :])
                        last.then_inc(full["A"], 1)
                        return
                    if what == "PV":
                        products = [(a, b, h) for h in range(HG + 1) for a, b in PARTS]
                    else:
                        products = [(a, b, c) for c in range(C) for a, b in PARTS]
                    half = len(products) // 2
                    start, stop = {0: (0, half), 1: (half, len(products)), ALL: (0, len(products))}[part]
                    if start == 0:
                        if what == "PV":
                            pe.wait_ge(p_lo, units(t, SUB * i + SUB - 1))
                            pe.wait_ge(left_lo, count(t, i))
                            if i == 0:
                                pe.wait_ge(vals_loaded, (t // TILES_B + 1) * (16 * 4 * HG))
                            if not (isinstance(t, int) and t == 0 and i == 0):
                                pe.wait_ge(lo["PV"], count(t, i - 1))
                        elif what == "Q" and i == 0:
                            pe.wait_ge(lo["A"], count(t, C - 1))
                        elif what == "Y" and i == 0:
                            pe.wait_ge(lo["PV"], count(t, G - 1))
                    for m in range(start, stop):
                        a, b, c = products[m]
                        if what == "PV":
                            v = vals[:, a, i, c, :] if c < HG else vals_left[:, a, i, :]
                            p = pT[:, i % 2, b, c, :] if c < HG else pT_left[:, i % 2, b, :]
                            out, left, right = pv_bank, v, p
                        elif what == "Q":
                            out, left, right = bank, wq[:, a, c, i * P:(i + 1) * P], xnT[:, b, c, :]
                        else:
                            out, left, right = bank, oT[:, a, c, i * P:(i + 1) * P], wo[:, b, c, :]
                        last = pe.matmul(out[:, :], left, right, start=(m == 0), stop=(m == len(products) - 1))
                    if stop == len(products):
                        last.then_inc(full[what], 1)

                def tile(kind, t):
                    def step(n, late, stages):
                        if kind in ("first", "steady", "last"):
                            score(t, n)
                        if late is not None:
                            transpose_probs(*late)
                        for s in stages:
                            stage(kind, *s)
                    walk(kind, t, step, engine_is_pe=True)

                all_tiles(pe, tile)

            @block.scalar
            def _(act):
                def split(psum, part, wait, value, done):
                    act.wait_ge(wait, value)
                    nc.scalar.activation(part, psum, ACT.Copy).then_inc(done, 1)

                def exps(t, n):
                    act.wait_ge(scores_read, units(t, n))
                    if not (isinstance(t, int) and t == 0 and n < 2):
                        act.wait_ge(probs_normed, units(t, n - 2))
                    for h in range(HG):
                        last = nc.scalar.activation(probs[:, n % 2, h, :], scores[:, n % 2, h, :], ACT.Exp,
                                                    bias=neg_top[:, n % 2, h:h + 1], scale=-1.0,
                                                    accum_out=total[:, n % 2, h:h + 1])
                    last.then_inc(exp_done, 1)

                def probs_hi(t, n):
                    g, s = n // SUB, n % SUB
                    if s == 0 and not (isinstance(t, int) and t == 0 and g < 2):
                        act.wait_ge(full["PV"], count(t, g - 2))
                    if s == SUB - 1:
                        split(left_bank[0:HG * LEFT, :], pT_left[:, g % 2, HI, :], p_full, units(t, n), left_hi)
                    split(p_bank[n % 2][:, :].rearrange("p (h k) -> p h k", h=HG),
                          pT[:, g % 2, HI, :, s * P:(s + 1) * P], p_full, units(t, n), p_hi)

                def tile(kind, t):
                    def step(n, late, stages):
                        for what, tt, i, _, rel in stages:
                            if what == "PV":
                                split(pv_bank[:, :], oT[:, HI, i, :], full[what], count(tt, i), hi[what])
                            elif what == "A":
                                split(two_banks[turns[kind, rel][0]][:, :], xnT[:, HI, i, :],
                                      full[what], count(tt, i), hi[what])
                            elif what == "Q":
                                bank = two_banks[turns[kind, rel][0]]
                                act.wait_ge(full[what], count(tt, i))
                                nc.scalar.activation(qT[0:HALF, i % 2, 0, :], bank[0:HALF, :], ACT.Copy)
                                nc.scalar.activation(qT[HALF:P, i % 2, 1, :], bank[HALF:P, :],
                                                     ACT.Copy).then_inc(hi[what], 1)
                        if late is not None:
                            probs_hi(*late)
                        if kind in ("first", "steady", "last"):
                            exps(t, n)
                    walk(kind, t, step)

                all_tiles(act, tile)

            @block.vector
            def _(dve):
                def split(psum, parts, wait, value, done):
                    dve.wait_ge(wait, value)
                    nc.vector.tensor_tensor(parts[LO], psum, raw(parts[HI]), ALU.subtract).then_inc(done, 1)

                NEXT_MASK = 8

                def mask_bias(t):
                    dve.wait_ge(mask_loaded, (t + 1) * 16)
                    nc.vector.tensor_scalar(next_bias[:, :, :], mask_in[:, :, :], 0, MASKED,
                                            ALU.is_equal, ALU.mult).then_inc(bias_done, 1)
                    dve.wait_ge(bias_done, t + 1)
                    nc.vector.tensor_reduce(any_row[:, 0, :], next_bias[:, :, :], AX.X, ALU.max).then_inc(bias_step, 1)
                    dve.wait_ge(bias_step, t * 4 + 1)
                    nc.vector.tensor_scalar(any_row[:, 1, :], any_row[:, 0, :], 0.0, None,
                                            ALU.is_equal).then_inc(bias_step, 1)
                    dve.wait_ge(bias_step, t * 4 + 2)
                    nc.vector.reciprocal(any_row[:, 2, :], any_row[:, 1, :]).then_inc(bias_step, 1)
                    dve.wait_ge(bias_step, t * 4 + 3)
                    nc.vector.tensor_scalar(next_nan[:, :], any_row[:, 2, :], 0.0, None,
                                            ALU.mult).then_inc(bias_step, 1)

                def move_bias(t, s):
                    if s == 0:
                        dve.wait_ge(bias_step, t * 4 + 4)
                    if not (isinstance(t, int) and t == 0):
                        dve.wait_ge(scores_read, units(t - 1, UNITS - SUB + s))
                    nc.vector.tensor_scalar(bias[:, s, :], next_bias[:, s, :], next_nan[:, s:s + 1], None,
                                            ALU.add).then_inc(bias_moved, 1)

                def read_scores(t, n):
                    unit, old = held(dve, units(t, n)), held(dve, units(t, n - 2))
                    bias_there = held(dve, count(t, n)) if n < SUB else None
                    dve.wait_ge(ready, 3)
                    dve.wait_ge(scores_full, unit)
                    if not (isinstance(t, int) and t == 0 and n < 2):
                        dve.wait_ge(exp_done, old)
                    if n < SUB:
                        dve.wait_ge(bias_moved, bias_there)
                    for h in range(HG):
                        cols = slice((h % 2) * KEYS, (h % 2 + 1) * KEYS)
                        last = nc.vector.tensor_tensor_reduce(
                            out=scores[:, n % 2, h, :], in0=score_bank[h // 2][:, cols],
                            in1=bias[:, n % SUB, :], scale=-(DK ** -0.5), scalar=-MASKED,
                            op0=ALU.add, op1=ALU.min, accum_out=neg_top[:, n % 2, h:h + 1])
                    last.then_inc(scores_read, 1)

                def invert(t, n):
                    dve.wait_ge(exp_done, units(t, n))
                    nc.vector.reciprocal(inv_total[:, n % 2, :], total[:, n % 2, :]).then_inc(inv_done, 1)

                def probs_lo(t, n):
                    g, s = n // SUB, n % SUB
                    if s == SUB - 1:
                        split(left_bank[0:HG * LEFT, :], [pT_left[:, g % 2, i, :] for i in (HI, LO)],
                              left_hi, count(t, g), left_lo)
                    split(p_bank[n % 2][:, :].rearrange("p (h k) -> p h k", h=HG),
                          [pT[:, g % 2, i, :, s * P:(s + 1) * P] for i in (HI, LO)], p_hi, units(t, n), p_lo)

                def tile(kind, t):
                    def step(n, late, stages):
                        if kind in ("first", "steady", "last"):
                            read_scores(t, n)
                        elif kind == "before":
                            mask_bias(0)
                            for s in range(SUB):
                                move_bias(0, s)
                        for what, tt, i, _, rel in stages:
                            if what == "Y":
                                if i == 0:
                                    dve.wait_ge(xres_loaded, (tt + 1) * 16)
                                dve.wait_ge(full[what], count(tt, i))
                                nc.vector.tensor_tensor(xres[:, i, :], two_banks[turns[kind, rel][0]][:, :],
                                                        xres[:, i, :], ALU.add).then_inc(y_added, 1)
                            elif what == "PV":
                                split(pv_bank[:, :], [oT[:, j, i, :] for j in (HI, LO)],
                                      hi[what], count(tt, i), lo[what])
                            elif what == "A":
                                split(two_banks[turns[kind, rel][0]][:, :], [xnT[:, j, i, :] for j in (HI, LO)],
                                      hi[what], count(tt, i), lo[what])
                            else:
                                bank = two_banks[turns[kind, rel][0]]
                                dve.wait_ge(hi[what], count(tt, i))
                                nc.vector.tensor_tensor(qT[HALF:P, i % 2, 0, :], bank[0:HALF, :],
                                                        raw(qT[0:HALF, i % 2, 0, :]), ALU.subtract)
                                nc.vector.tensor_tensor(qT[0:HALF, i % 2, 1, :], bank[HALF:P, :],
                                                        raw(qT[HALF:P, i % 2, 1, :]),
                                                        ALU.subtract).then_inc(lo[what], 1)
                        if kind in ("first", "steady", "last") and n > 0:
                            invert(t, n - 1)
                        elif kind in ("steady", "last"):
                            invert(t - 1, UNITS - 1)
                            move_bias(t, SUB - 1)
                        elif kind == "after" and n == 0:
                            invert(t, UNITS - 1)
                        if late is not None:
                            probs_lo(*late)
                        if kind in ("first", "steady", "last") and n < SUB:
                            row_stats(nc, dve, st, t + 1, n)
                        if kind in ("first", "steady"):
                            if n == NEXT_MASK:
                                mask_bias(t + 1)
                            if n > UNITS - SUB:
                                move_bias(t + 1, n - (UNITS - SUB + 1))
                    walk(kind, t, step)

                all_tiles(dve, tile)

            @block.gpsimd
            def _(pool):
                NORM = (3, 5, 6, 8)

                def normalise(t, n):
                    pool.wait_ge(inv_done, units(t, n))
                    if not (isinstance(t, int) and t == 0 and n < 4):
                        pool.wait_ge(p_full, units(t, n - 4))
                    inv = inv_total[:, n % 2, :].unsqueeze(2)
                    for a, b, c in ((0, P, 0), (P, KEYS, HG * P)):
                        last = nc.gpsimd.tensor_tensor(
                            normed[:, n % 4, c:c + HG * (b - a)].rearrange("p (h k) -> p h k", h=HG),
                            probs[:, n % 2, :, a:b], inv.to_broadcast([P, HG, b - a]), ALU.mult)
                    last.then_inc(probs_normed, 1)

                def tile(kind, t):
                    if kind not in ("first", "steady", "last"):
                        return
                    for n in range(UNITS):
                        normalise(t, n)
                        if n in NORM:
                            layer_norm(nc, pool, st, t + 1, NORM.index(n))

                all_tiles(pool, tile)


def ffn(nc, sem, banks, ident, sum_parts, rows, ar, b2s, W1, W2, b1_parts, x1, out):
    with ExitStack() as stack:
        def sb(name, shape, dt):
            return stack.enter_context(nc.sbuf_tensor(name, shape, dt))

        w1 = sb("w1", [P, 2, C, F], F32R)
        w2 = sb("w2", [P, 2, FC, D], F32R)
        b1s = sb("b1s", [STACK, F], F32R)
        xin = sb("xin", [P, 2, D], F32)
        xres = rows
        xnT = sb("ffn_xnT", [P, 2, 2, C, TILE], F32R)
        hid = sb("hid", [P, 2, 2, TILE], F32R)
        z_rows = sb("z_rows", [2 * Q, TILE], F32)
        z = sb("z", [P, SUB, AR], F32)
        g_top = sb("g_top", [P, SUB], F32)
        g_exp = sb("g_exp", [P, SUB, E], F32)
        g_sum = sb("g_sum", [P, SUB], F32)
        g_inv = sb("g_inv", [P, SUB], F32)
        gate = sb("gate", [P, SUB, E], F32)
        zg = sb("zg", [P, SUB, ER], F32)
        zs = sb("zs", [P, SUB, 3, Q], F32R)
        zsT = sb("zsT", [STACK, 2, TILE], F32R)
        stats = sb("ffn_stats", [P, 2, 6], F32)
        moments = sb("ffn_moments", [P, 2, 2], F32)
        var_eps = sb("ffn_var_eps", [P, 2], F32)
        minus_half = sb("ffn_minus_half", [P, 1], F32)
        rstd = sb("ffn_rstd", [P, 2], F32)

        f1_bank = (banks[0], banks[1])
        y_bank = (banks[2], banks[3], banks[4], banks[5])
        z_bank = (banks[6], banks[7])

        ready = sem("ffn_ready")
        w_loaded = [sem(f"w_loaded{i}") for i in range(SUB)]
        w_hi, w_lo = sem("w_hi"), sem("w_lo")
        b1s_loaded = sem("b1s_loaded")
        xin_loaded = [sem(f"xin_loaded{i}") for i in range(2)]
        stats_step = sem("ffn_stats_step")
        rstd_done = sem("ffn_rstd_done")
        x_normed = sem("ffn_x_normed")
        x_full, x_hi, x_lo = sem("x_full"), sem("x_hi"), sem("x_lo")
        f1_full, h_hi, h_lo = sem("f1_full"), sem("h_hi"), sem("h_lo")
        z_full, z_copied = sem("z_full"), sem("z_copied")
        z_turned = sem("z_turned")
        gate_step = sem("gate_step")
        gate_exp = sem("gate_exp")
        zs_full, zs_copied = sem("zs_full"), sem("zs_copied")
        y_full, y_added = sem("y_full"), sem("ffn_y_added")
        xres_loaded, stored = sem("ffn_xres_loaded"), sem("stored")
        GATE_STEPS = 9

        def w1_stage(j):
            return (xin if j < 2 else xres)[:, j % 2, :]

        def x_bank(t, s):
            return z_bank[s % 2 if isinstance(t, int) and t == 0 else 0]

        def blocks(t, j):
            return t * FC + (j + 1)

        def subs(t, s):
            return t * SUB + (s + 1)

        def nth(kind, layer, t):
            if layer == 0:
                return 1 if kind == "before" else t * 2
            return t * 2 + (2 if kind == "last" else 3)

        def first_nth(t):
            return 1 if isinstance(t, int) and t == 0 else t * 2

        w1_rows = W1.rearrange("(c p) f -> p c f", p=P)
        x1_rows = x1.rearrange("(t s p) d -> t p s d", s=SUB, p=P)
        out_rows = out.rearrange("b (t s p) d -> (b t) p s d", s=SUB, p=P)

        STATS = {1: 0, 3: 1, 5: 2, 7: 3}
        TURN = {3: 0, 5: 1, 7: 2, 9: 3}
        Z1, TURN_Z1, TURN_ZS1 = 11, 12, 14

        def all_tiles(engine, before, tile):
            before()
            tile("first", 0, 0)
            with engine.Fori(0, (TILES - 2) // 2) as pair:
                tile("steady", pair * 2 + 1, 1)
                tile("steady", pair * 2 + 2, 0)
            tile("last", TILES - 1, 1)

        with nc.Block() as block:
            @block.sync
            def _(sp):
                def load_x(t, s):
                    if not (isinstance(t, int) and t == 1 and s < 2):
                        value = held(sp, subs(t, s - 2))
                        sp.wait_ge(ready, 3)
                        sp.wait_ge(x_full, value)
                    sp.dma_start(xin[:, s % 2, :], x1_rows[t, :, s, :]).then_inc(xin_loaded[s % 2], 16)

                def tile(kind, t, parity):
                    if kind == "steady":
                        load_x(t + 1, 0)
                        load_x(t + 1, 1)
                    if kind != "first":
                        for s in range(SUB):
                            value = held(sp, subs(t - 1, s))
                            sp.wait_ge(ready, 3)
                            sp.wait_ge(y_added, value)
                            sp.dma_start(out_rows[t - 1, :, s, :], xres[:, s, :]).then_inc(stored, 16)
                        value = held(sp, t * (16 * SUB))
                        sp.wait_ge(ready, 3)
                        sp.wait_ge(stored, value)
                    sp.dma_start(xres[:, :, :], x1_rows[t]).then_inc(xres_loaded, 16)
                    if kind == "steady":
                        load_x(t + 1, 2)
                        load_x(t + 1, 3)

                NEXT_X = {3: 0, 4: 1, 8: 2, 10: 3}

                def before():
                    for j in range(FC):
                        if j in NEXT_X:
                            load_x(1, NEXT_X[j])
                        if j >= 2:
                            sp.wait_ge(x_full, j % 2 + 1)
                            sp.wait_ge(w_lo, 2 * (j - 2) + 1)
                        sp.dma_start(w1_stage(j).rearrange("p (c f) -> p c f", c=C),
                                     w1_rows[:, :, j * P:(j + 1) * P]).then_inc(w_loaded[j % 2], 16)
                        if j < 2:
                            sp.wait_ge(x_full, 2 + j + 1)
                        else:
                            sp.wait_ge(w_lo, 2 * (j - 2) + 2)
                        sp.dma_start(xres[:, 2 + j % 2, :], W2[j * P:(j + 1) * P, :]).then_inc(w_loaded[2 + j % 2], 16)
                        if j == 1:
                            sp.dma_start(raw(b1s[:, :]), b1_parts).then_inc(b1s_loaded, 16)
                    sp.wait_ge(w_lo, 2 * FC)

                all_tiles(sp, before, tile)
                for s in range(SUB):
                    sp.wait_ge(y_added, subs(TILES - 1, s))
                    sp.dma_start(out_rows[TILES - 1, :, s, :], xres[:, s, :]).then_inc(stored, 16)
                sp.wait_ge(stored, TILES * 16 * SUB)

            @block.tensor
            def _(pe):
                def turn_x(t, s):
                    first = isinstance(t, int) and t == 0
                    if first:
                        if s >= 2:
                            pe.wait_ge(x_lo, subs(t, s - 2))
                    else:
                        pe.wait_ge(x_normed, subs(t - 1, s))
                        if s > 0:
                            pe.wait_ge(x_lo, subs(t, s - 1))
                        else:
                            pe.wait_ge(zs_copied, first_nth(t - 1))
                    for c in range(C):
                        last = pe.transpose(x_bank(t, s)[:, c * P:(c + 1) * P],
                                            (xres[:, s, :] if first else xin[:, s % 2, :])[:, c * P:(c + 1) * P],
                                            ident[:, :])
                    last.then_inc(x_full, 1)

                def z1(t, parity):
                    pe.wait_ge(x_lo, subs(t, SUB - 1))
                    for n, (c, i) in enumerate((c, i) for c in range(C) for i in (HI, LO)):
                        last = pe.matmul(z_bank[0][0:ARW, :], ar[:, c, :], xnT[:, parity, i, c, :],
                                         start=(n == 0), stop=(n == 2 * C - 1))
                    last.then_inc(z_full, 1)

                def turn_z(layer, n):
                    pe.wait_ge(z_copied, n)
                    for s in range(SUB):
                        last = pe.matmul(z_bank[layer][:, s * AR:(s + 1) * AR], z_rows[:, s * P:(s + 1) * P],
                                         sum_parts[:, :], start=True, stop=True)
                    last.then_inc(z_turned, 1)

                def turn_zs(layer, n):
                    pe.wait_ge(gate_step, n * GATE_STEPS)
                    for s in range(SUB):
                        last = pe.transpose(z_bank[layer][0:STACK, s * P:(s + 1) * P],
                                            raw(zs[:, s, :, :]).rearrange("p a b -> p (a b)"), ident[:, :])
                    last.then_inc(zs_full, 1)

                def f1(t, j, parity, part=slice(0, 3 * C + 1)):
                    if part.start == 0:
                        if isinstance(t, int) and t == 0:
                            pe.wait_ge(w_lo, 2 * j + 1)
                        if not (isinstance(t, int) and t == 0 and j < 2):
                            pe.wait_ge(h_lo, blocks(t, j - 2))
                    terms = [(c, a, b) for c in range(C) for a, b in PARTS] + [None]
                    for n in range(part.start, part.stop):
                        if terms[n] is None:
                            if j < 2:
                                pe.wait_ge(zs_copied, first_nth(t))
                                pe.wait_ge(b1s_loaded, 16)
                            last = pe.matmul(f1_bank[j % 2][:, :], b1s[:, j * P:(j + 1) * P], zsT[:, 0, :],
                                             start=False, stop=True)
                            last.then_inc(f1_full, 1)
                        else:
                            c, a, b = terms[n]
                            pe.matmul(f1_bank[j % 2][:, :], w1[:, a, c, j * P:(j + 1) * P],
                                      xnT[:, parity, b, c, :], start=(n == 0), stop=False)

                def f2(t, j):
                    early = isinstance(t, int) and t == 0
                    pe.wait_ge(h_lo, blocks(t, j))
                    if early:
                        pe.wait_ge(w_lo, 2 * j + 2)
                    for s in range(SUB):
                        if j == 0 and not early:
                            pe.wait_ge(y_added, subs(t - 1, s))
                        for a, b in PARTS:
                            pe.matmul(y_bank[s][:, :], hid[:, j % 2, a, s * P:(s + 1) * P], w2[:, b, j, :],
                                      start=(j == 0 and (a, b) == PARTS[0]), stop=False)
                    for i in (HI, LO):
                        last = pe.matmul(z_bank[1][0:ARW, :], ar[:, C + j, :], hid[:, j % 2, i, :],
                                         start=(j == 0 and i == HI), stop=(j == FC - 1 and i == LO))
                    if j == FC - 1:
                        last.then_inc(z_full, 1)

                def lora2(n):
                    pe.wait_ge(zs_copied, n)
                    for s in range(SUB):
                        pe.matmul(y_bank[s][:, :], zsT[:, 1, s * P:(s + 1) * P], b2s[:, :],
                                  start=False, stop=True).then_inc(y_full, 1)

                def before():
                    for s in range(SUB):
                        turn_x(0, s)
                    z1(0, 0)
                    f1(0, 0, 0, slice(0, 2 * C))
                    turn_z(0, 1)
                    f1(0, 0, 0, slice(2 * C, 3 * C))
                    f1(0, 1, 0, slice(0, 3 * C))
                    turn_zs(0, 1)
                    f1(0, 0, 0, slice(3 * C, 3 * C + 1))
                    f1(0, 1, 0, slice(3 * C, 3 * C + 1))

                def tile(kind, t, parity):
                    more = kind != "last"
                    for j in range(FC):
                        if j == 0:
                            f1(t, 2, parity, slice(0, 3 * C))
                            f2(t, 0)
                            f1(t, 2, parity, slice(3 * C, 3 * C + 1))
                        else:
                            f2(t, j)
                            if j + 2 < FC:
                                f1(t, j + 2, parity)
                        if more:
                            if j in TURN:
                                turn_x(t + 1, TURN[j])
                            elif j == Z1:
                                z1(t + 1, 1 - parity)
                            elif j == TURN_Z1:
                                turn_z(0, nth(kind, 0, t + 1))
                            elif j == TURN_ZS1:
                                turn_zs(0, nth(kind, 0, t + 1))
                    n = nth(kind, 1, t)
                    if more:
                        f1(t + 1, 0, 1 - parity, slice(0, 4))
                    turn_z(1, n)
                    if more:
                        f1(t + 1, 0, 1 - parity, slice(4, 3 * C + 1))
                        f1(t + 1, 1, 1 - parity, slice(0, 9))
                    turn_zs(1, n)
                    if more:
                        f1(t + 1, 1, 1 - parity, slice(9, 3 * C + 1))
                    lora2(n)

                all_tiles(pe, before, tile)

            @block.scalar
            def _(act):
                def split_w(j):
                    act.wait_ge(w_loaded[j % 2], 16 * (j // 2 + 1))
                    nc.scalar.activation(w1[:, HI, :, j * P:(j + 1) * P],
                                         w1_stage(j).rearrange("p (c f) -> p c f", c=C),
                                         ACT.Copy).then_inc(w_hi, 1)
                    act.wait_ge(w_loaded[2 + j % 2], 16 * (j // 2 + 1))
                    nc.scalar.activation(w2[:, HI, j, :], xres[:, 2 + j % 2, :], ACT.Copy).then_inc(w_hi, 1)

                def x_part(t, s, parity):
                    act.wait_ge(x_full, subs(t, s))
                    nc.scalar.activation(xnT[:, parity, HI, :, s * P:(s + 1) * P],
                                         x_bank(t, s)[:, :].rearrange("p (c k) -> p c k", c=C),
                                         ACT.Copy).then_inc(x_hi, 1)

                def copy_z(layer, n):
                    act.wait_ge(z_full, n)
                    nc.scalar.activation(z_rows[:, :], z_bank[layer][0:2 * Q, :], ACT.Copy).then_inc(z_copied, 1)

                def exps(n):
                    act.wait_ge(gate_step, n * GATE_STEPS - (GATE_STEPS - 3))
                    nc.scalar.activation(g_exp[:, :, :], g_exp[:, :, :], ACT.Exp).then_inc(gate_exp, 1)

                def copy_zs(layer, n):
                    act.wait_ge(zs_full, n)
                    nc.scalar.activation(zsT[:, layer, :], z_bank[layer][0:STACK, :], ACT.Copy).then_inc(zs_copied, 1)

                def relu(t, j):
                    act.wait_ge(f1_full, blocks(t, j))
                    nc.scalar.activation(hid[:, j % 2, HI, :], f1_bank[j % 2][:, :], ACT.Relu).then_inc(h_hi, 1)

                def before():
                    for s in range(SUB):
                        x_part(0, s, 0)
                    split_w(0)
                    copy_z(0, 1)
                    split_w(1)
                    exps(1)
                    copy_zs(0, 1)
                    relu(0, 0)
                    relu(0, 1)

                def tile(kind, t, parity):
                    more = kind != "last"
                    for j in range(FC):
                        if kind == "first" and j + 2 < FC:
                            split_w(j + 2)
                        if j + 2 < FC:
                            relu(t, j + 2)
                        if more:
                            if j in TURN:
                                x_part(t + 1, TURN[j], 1 - parity)
                            elif j == Z1:
                                copy_z(0, nth(kind, 0, t + 1))
                            elif j == TURN_Z1:
                                exps(nth(kind, 0, t + 1))
                            elif j == TURN_ZS1:
                                copy_zs(0, nth(kind, 0, t + 1))
                    n = nth(kind, 1, t)
                    copy_z(1, n)
                    exps(n)
                    if more:
                        relu(t + 1, 0)
                    copy_zs(1, n)
                    if more:
                        relu(t + 1, 1)

                all_tiles(act, before, tile)

            @block.vector
            def _(dve):
                nc.vector.memset(minus_half[:, :], -0.5).then_inc(ready, 1)
                nc.vector.memset(raw(zs[:, :, :, :]), 0.0).then_inc(ready, 1)
                dve.wait_ge(ready, 2)
                nc.vector.memset(raw(zs[:, :, 0:2, ER:ER + 1]), 1.0).then_inc(ready, 1)

                def split_w(j):
                    dve.wait_ge(w_hi, 2 * j + 1)
                    nc.vector.tensor_tensor(w1[:, LO, :, j * P:(j + 1) * P],
                                            w1_stage(j).rearrange("p (c f) -> p c f", c=C),
                                            raw(w1[:, HI, :, j * P:(j + 1) * P]), ALU.subtract).then_inc(w_lo, 1)
                    dve.wait_ge(w_hi, 2 * j + 2)
                    nc.vector.tensor_tensor(w2[:, LO, j, :], xres[:, 2 + j % 2, :], raw(w2[:, HI, j, :]),
                                            ALU.subtract).then_inc(w_lo, 1)

                def row_stats(t, s):
                    v = (t - 1) * (3 * SUB) + 3 * s
                    dve.wait_ge(xin_loaded[s % 2], (t - 1) * (8 * SUB) + 16 * (s // 2 + 1))
                    nc.vector.bn_stats(stats[:, s % 2, :], xin[:, s % 2, :]).then_inc(stats_step, 1)
                    first_step = held(dve, v + 1)
                    dve.wait_ge(ready, 3)
                    dve.wait_ge(stats_step, first_step)
                    nc.vector.bn_aggr(moments[:, s % 2, :], stats[:, s % 2, :]).then_inc(stats_step, 1)
                    dve.wait_ge(stats_step, v + 2)
                    nc.vector.tensor_scalar(var_eps[:, s % 2:s % 2 + 1], moments[:, s % 2, 1:2], EPS, None,
                                            ALU.add).then_inc(stats_step, 1)

                def x_part(t, s, parity):
                    dve.wait_ge(x_hi, subs(t, s))
                    nc.vector.tensor_tensor(xnT[:, parity, LO, :, s * P:(s + 1) * P],
                                            x_bank(t, s)[:, :].rearrange("p (c k) -> p c k", c=C),
                                            raw(xnT[:, parity, HI, :, s * P:(s + 1) * P]),
                                            ALU.subtract).then_inc(x_lo, 1)

                def relu(t, j):
                    dve.wait_ge(h_hi, blocks(t, j))
                    nc.vector.scalar_tensor_tensor(out=hid[:, j % 2, LO, :], in0=f1_bank[j % 2][:, :], scalar=0.0,
                                                   in1=raw(hid[:, j % 2, HI, :]), op0=ALU.max,
                                                   op1=ALU.subtract).then_inc(h_lo, 1)

                def route(layer, n):
                    done = n * GATE_STEPS - GATE_STEPS

                    def after(k):
                        dve.wait_ge(gate_step, done + k)

                    logits = z[:, :, ER:ER + E]
                    dve.wait_ge(z_turned, n)
                    nc.vector.tensor_copy(z[:, :, :].rearrange("p s c -> p (s c)"),
                                          z_bank[layer][:, 0:SUB * AR]).then_inc(gate_step, 1)
                    after(1)
                    nc.vector.tensor_reduce(g_top[:, :], logits, AX.X, ALU.max).then_inc(gate_step, 1)
                    after(2)
                    nc.vector.tensor_tensor(g_exp[:, :, :], logits, g_top[:, :].unsqueeze(2).to_broadcast([P, SUB, E]),
                                            ALU.subtract).then_inc(gate_step, 1)
                    dve.wait_ge(gate_exp, n)
                    nc.vector.tensor_reduce(g_sum[:, :], g_exp[:, :, :], AX.X, ALU.add).then_inc(gate_step, 1)
                    after(4)
                    nc.vector.reciprocal(g_inv[:, :], g_sum[:, :]).then_inc(gate_step, 1)
                    after(5)
                    nc.vector.scalar_tensor_tensor(out=gate[:, :, :], in0=g_exp[:, :, :], scalar=1.0 / R,
                                                   in1=g_inv[:, :].unsqueeze(2).to_broadcast([P, SUB, E]),
                                                   op0=ALU.mult, op1=ALU.mult).then_inc(gate_step, 1)
                    after(6)
                    nc.vector.tensor_tensor(zg[:, :, :].rearrange("p s (e r) -> p s e r", e=E),
                                            z[:, :, 0:ER].rearrange("p s (e r) -> p s e r", e=E),
                                            gate[:, :, :].unsqueeze(3).to_broadcast([P, SUB, E, R]),
                                            ALU.mult).then_inc(gate_step, 1)
                    after(7)
                    nc.vector.tensor_copy(zs[:, :, 0:2, 0:ER],
                                          zg[:, :, :].unsqueeze(2).to_broadcast([P, SUB, 2, ER])).then_inc(gate_step, 1)
                    after(8)
                    nc.vector.tensor_tensor(zs[:, :, 2, 0:ER], zg[:, :, :], raw(zs[:, :, 0, 0:ER]),
                                            ALU.subtract).then_inc(gate_step, 1)

                def before():
                    for s in range(SUB):
                        x_part(0, s, 0)
                    split_w(0)
                    split_w(1)
                    route(0, 1)
                    relu(0, 0)
                    relu(0, 1)

                def tile(kind, t, parity):
                    more = kind != "last"
                    for j in range(FC):
                        if kind == "first" and j + 2 < FC:
                            split_w(j + 2)
                        if more and j in STATS:
                            row_stats(t + 1, STATS[j])
                        if j + 2 < FC:
                            relu(t, j + 2)
                        if more:
                            if j in TURN:
                                x_part(t + 1, TURN[j], 1 - parity)
                            elif j == TURN_Z1:
                                route(0, nth(kind, 0, t + 1))
                    n = nth(kind, 1, t)
                    route(1, n)
                    if more:
                        relu(t + 1, 0)
                        relu(t + 1, 1)
                    dve.wait_ge(xres_loaded, (t + 1) * 16)
                    for s in range(SUB):
                        dve.wait_ge(y_full, subs(t, s))
                        nc.vector.tensor_tensor(xres[:, s, :], y_bank[s][:, :], xres[:, s, :],
                                                ALU.add).then_inc(y_added, 1)

                all_tiles(dve, before, tile)

            @block.gpsimd
            def _(pool):
                def layer_norm(t, s):
                    pool.wait_ge(stats_step, (t - 1) * (3 * SUB) + (3 * s + 3))
                    nc.gpsimd.tensor_tensor(rstd[:, s % 2:s % 2 + 1], var_eps[:, s % 2:s % 2 + 1],
                                            minus_half[:, :], ALU.pow).then_inc(rstd_done, 1)
                    own_rstd = held(pool, subs(t - 1, s))
                    pool.wait_ge(ready, 3)
                    pool.wait_ge(rstd_done, own_rstd)
                    nc.gpsimd.tensor_scalar(xin[:, s % 2, :], xin[:, s % 2, :], moments[:, s % 2, 0:1],
                                            rstd[:, s % 2:s % 2 + 1], ALU.subtract, ALU.mult).then_inc(x_normed, 1)

                with pool.Fori(1, TILES) as t:
                    for s in range(SUB):
                        layer_norm(t, s)


def build(nc, x, ctx, mask, Wq, Wk, Wv, Wo, W1, b1, A1, B1, R1, W2, b2, A2, B2, R2, out):
    k_parts = nc.dram_tensor("k_parts", (2, B, P, G, KEYS), F32, kind="Internal").ap()
    v_parts = nc.dram_tensor("v_parts", (2, B, KEYS, D), F32, kind="Internal").ap()
    b1_parts = nc.dram_tensor("b1_parts", (STACK, F), F32, kind="Internal").ap()
    x1 = nc.dram_tensor("x1", (B * S, D), F32, kind="Internal").ap()
    with ExitStack() as stack:
        def sem(name):
            return stack.enter_context(nc.semaphore(name))

        banks = Banks(nc, stack)
        ident = stack.enter_context(nc.sbuf_tensor("ident", [P, P], F32))
        sum_parts = stack.enter_context(nc.sbuf_tensor("sum_parts", [2 * Q, AR], F32))
        ar = stack.enter_context(nc.sbuf_tensor("ar", [P, C + FC, ARW], F32R))
        b2s = stack.enter_context(nc.sbuf_tensor("b2s", [STACK, D], F32R))
        rows = stack.enter_context(nc.sbuf_tensor("rows", [P, SUB, D], F32))
        with ExitStack() as first_two:
            st = AttentionState(nc, sem, first_two, rows)
            wq = first_two.enter_context(nc.sbuf_tensor("wq", [P, 2, C, D], F32R))
            wo = first_two.enter_context(nc.sbuf_tensor("wo", [P, 2, C, D], F32R))
            prepare(nc, sem, banks, ident, sum_parts, st, wq, wo, ar, b2s, x, ctx, mask, Wq, Wk, Wv, Wo,
                    (A1, B1, R1, b1, A2, B2, R2, b2), k_parts, v_parts, b1_parts)
            attention(nc, sem, banks, ident, st, wq, wo, x, mask, k_parts, v_parts, x1)
        ffn(nc, sem, banks, ident, sum_parts, rows, ar, b2s, W1, W2, b1_parts, x1, out)


_INS = ["x", "ctx_1024", "mask_SxS2_ik0", "L0_xattn_Wq", "L0_xattn_Wk", "L0_xattn_Wv", "L0_xattn_Wo",
        "L0_ffn_W1", "L0_ffn_b1", "L0_ffn_A1", "L0_ffn_B1", "L0_ffn_R1",
        "L0_ffn_W2", "L0_ffn_b2", "L0_ffn_A2", "L0_ffn_B2", "L0_ffn_R2"]


def kernel(**inputs):
    import numpy as _np
    import concourse.bacc as _bacc
    from concourse import mybir as _mybir
    from concourse.bass_utils import run_bass_kernel_spmd as _run

    nc = _bacc.Bacc("TRN2", target_bir_lowering=False, num_devices=1)
    arrays, args = {}, []
    for name in _INS:
        a = _np.ascontiguousarray(inputs[name])
        arrays[f"in_{name}_dram"] = a
        args.append(nc.dram_tensor(f"in_{name}_dram", a.shape, _mybir.dt.from_np(a.dtype), kind="ExternalInput").ap())
    args.append(nc.dram_tensor("out_0_dram", (B, S, D), F32, kind="ExternalOutput").ap())
    build(nc, *args)
    r = _run(nc, [arrays], core_ids=[0])
    return r.results[0]["out_0_dram"]
```
